# Optimizing a Trainium2 kernel written in Bass

```python
import numpy as np
import jax
import jax.numpy as jnp

def _softmax(x, axis=-1):
    return jax.nn.softmax(x, axis=axis)

def _gelu(x):
    return jax.nn.gelu(x, approximate=True)

def _silu(x):
    return jax.nn.silu(x)

def _sigmoid(x):
    return jax.nn.sigmoid(x)

def _layernorm(x, axis=-1, eps=1e-05):
    m = jnp.mean(x, axis=axis, keepdims=True)
    v = jnp.var(x, axis=axis, keepdims=True)
    return (x - m) / jnp.sqrt(v + eps)

def _scatter_add(tgt, idx, src, axis=0):
    return tgt.at[idx].add(src)

def _segment_sum(src, seg, n):
    return jax.ops.segment_sum(src, seg, n)
kernel_name = 'mk_recurrent_d4_jaxref_r8_50ad0c'

def setup_inputs(seed: int=0):
    np.random.seed(seed)
    _w = jnp.asarray

    def _L0_attn_setup():
        import jax, jax.numpy as jnp
        import numpy as np
        key = jax.random.key(seed)
        k1, k2, k3, k4 = jax.random.split(key, 4)
        B, S, D_in, D_state, D_out = (8, 256, 128, 128, 128)
        x = jax.random.normal(k1, (B, S, D_in), dtype=jnp.float32)
        A = jax.random.uniform(k2, (D_state,), dtype=jnp.float32) * 0.1
        B_w = jax.random.uniform(k3, (D_state, D_in), dtype=jnp.float32, minval=-0.01, maxval=0.01)
        bound = 1.0 / np.sqrt(D_state)
        kw, kb = jax.random.split(k4)
        Wo = jax.random.uniform(kw, (D_out, D_state), dtype=jnp.float32, minval=-bound, maxval=bound)
        bo = jax.random.uniform(kb, (D_out,), dtype=jnp.float32, minval=-bound, maxval=bound)
        return {'x': x, 'A': A, 'B_w': B_w, 'Wo': Wo, 'bo': bo}
    _L0_attn_in = _L0_attn_setup()

    def _L0_ffn_setup():
        import jax, jax.numpy as jnp
        import numpy as np
        B, S, D, H, E = (2, 256, 128, 512, 8)
        key = jax.random.key(seed)
        k0, k1, k2, k3 = jax.random.split(key, 4)
        x = jax.random.normal(k0, (B, S, D), dtype=jnp.float32)
        router_w = jax.random.normal(k1, (E, D), dtype=jnp.float32) * 0.02
        w1 = jax.random.normal(k2, (E, D, H), dtype=jnp.float32) * 0.02
        w2 = jax.random.normal(k3, (E, H, D), dtype=jnp.float32) * 0.02
        return {'x': x, 'router_w': router_w, 'w1': w1, 'w2': w2}
    _L0_ffn_in = _L0_ffn_setup()

    def _L1_attn_setup():
        import jax, jax.numpy as jnp
        import numpy as np
        D_MODEL = 128
        D_STATE = 32
        key = jax.random.key(seed)
        k1, k2, k3, k4 = jax.random.split(key, 4)
        x = jax.random.normal(k1, (8, 512, D_MODEL), dtype=jnp.float32)
        A = jax.random.normal(k2, (D_STATE,), dtype=jnp.float32)
        B = jax.random.normal(k3, (D_STATE, D_MODEL), dtype=jnp.float32) * 0.01
        C = jax.random.normal(k4, (D_MODEL, D_STATE), dtype=jnp.float32) * 0.01
        D = jnp.ones((D_MODEL,), dtype=jnp.float32)
        return {'x': x, 'A': A, 'B': B, 'C': C, 'D': D}
    _L1_attn_in = _L1_attn_setup()

    def _L1_ffn_setup():
        import jax, jax.numpy as jnp
        import numpy as np
        B, S, H = (8, 512, 128)
        NAV = 128
        E = 8
        F = 2 * H
        key = jax.random.key(seed)
        ks = jax.random.split(key, 12)

        def w(k, shape, fan_in):
            return jax.random.normal(k, shape, dtype=jnp.float32) / np.sqrt(fan_in)
        return {'hidden_states': jax.random.normal(ks[0], (B, S, H), dtype=jnp.float32), 'Wp1': w(ks[1], (H, NAV), H), 'bp1': jnp.zeros((NAV,), jnp.float32), 'Wp2': w(ks[2], (NAV, E), NAV), 'bp2': jnp.zeros((E,), jnp.float32), 'W1': w(ks[3], (E, H, F), H), 'b1': jnp.zeros((E, F), jnp.float32), 'W2': w(ks[4], (E, F, H), F), 'b2': jnp.zeros((E, H), jnp.float32), 'Wo': w(ks[5], (H, H), H), 'bo': jnp.zeros((H,), jnp.float32)}
    _L1_ffn_in = _L1_ffn_setup()

    def _L2_attn_setup():
        import jax, jax.numpy as jnp
        import numpy as np
        H = 16
        G = 4
        THETA = 10000.0

        def _rope(x, cos, sin):
            x0 = x[..., ::2]
            x1 = x[..., 1::2]
            r0 = x0 * cos - x1 * sin
            r1 = x0 * sin + x1 * cos
            return jnp.stack([r0, r1], axis=-1).reshape(x.shape)
        key = jax.random.key(seed)
        ks = jax.random.split(key, 5)
        B, S, D = (2, 256, 128)
        return {'x': jax.random.normal(ks[0], (B, S, D), jnp.float32), 'Wq': jax.random.normal(ks[1], (D, D), jnp.float32) * 0.02, 'Wk': jax.random.normal(ks[2], (D, D // G), jnp.float32) * 0.02, 'Wv': jax.random.normal(ks[3], (D, D // G), jnp.float32) * 0.02, 'Wo': jax.random.normal(ks[4], (D, D), jnp.float32) * 0.02}
    _L2_attn_in = _L2_attn_setup()

    def _L2_ffn_setup():
        import jax, jax.numpy as jnp
        import numpy as np
        B, S, D, O, E, K = (4, 256, 128, 128, 8, 2)
        key = jax.random.key(seed)
        ks = jax.random.split(key, 5)
        scale_in = 1.0 / np.sqrt(D)
        x = jax.random.normal(ks[0], (B, S, D), dtype=jnp.float32)
        gate_w = jax.random.uniform(ks[1], (E, D), jnp.float32, -scale_in, scale_in)
        gate_b = jax.random.uniform(ks[2], (E,), jnp.float32, -scale_in, scale_in)
        expert_w = jax.random.uniform(ks[3], (E, D, O), jnp.float32, -scale_in, scale_in)
        expert_b = jax.random.uniform(ks[4], (E, O), jnp.float32, -scale_in, scale_in)
        return {'x': x, 'gate_w': gate_w, 'gate_b': gate_b, 'expert_w': expert_w, 'expert_b': expert_b}
    _L2_ffn_in = _L2_ffn_setup()

    def _L3_attn_setup():
        import jax, jax.numpy as jnp
        import numpy as np
        from jax import lax
        B, T, D = (16, 256, 128)
        S, K, M = (32, 4, 32)
        BN_EPS = 1e-05

        def silu(x):
            return x * jax.nn.sigmoid(x)

        def bn_eval(x):
            return x / np.float32(np.sqrt(1.0 + BN_EPS))

        def conv1d(x, w, pad, dil=1, b=None):
            y = lax.conv_general_dilated(x, w, (1,), ((pad, pad),), rhs_dilation=(dil,), dimension_numbers=('NCH', 'OIH', 'NCH'))
            if b is not None:
                y = y + b[None, :, None]
            return y

        def dwconv_causal(x, w, b):
            y = lax.conv_general_dilated(jnp.swapaxes(x, 1, 2), w, (1,), ((K - 1, 0),), dimension_numbers=('NCH', 'OIH', 'NCH'), feature_group_count=w.shape[0])
            return jnp.swapaxes(y + b[None, :, None], 1, 2)

        def mamba(x, in_w, in_b, conv_w, conv_b, ssm_w, ssm_b, A, Bv, Cv, Dv, out_w, out_b):
            xz = x @ in_w + in_b
            xs, gate = jnp.split(xz, 2, axis=-1)
            u = silu(dwconv_causal(xs, conv_w, conv_b))
            xssm = u @ ssm_w + ssm_b
            h0 = jnp.zeros((x.shape[0], A.shape[0]), x.dtype)

            def step(h, xt):
                h = h @ A.T + xt * Bv
                return (h, h @ Cv)
            _, c = lax.scan(step, h0, jnp.swapaxes(xssm, 0, 1))
            y = (jnp.swapaxes(c, 0, 1)[..., None] + Dv) * u
            y = y * silu(gate)
            return y @ out_w + out_b + x

        def _reference_tuple_inner(x, m1_in_w, m1_in_b, m1_conv_w, m1_conv_b, m1_ssm_w, m1_ssm_b, m1_A, m1_B, m1_C, m1_D, m1_out_w, m1_out_b, m2_in_w, m2_in_b, m2_conv_w, m2_conv_b, m2_ssm_w, m2_ssm_b, m2_A, m2_B, m2_C, m2_D, m2_out_w, m2_out_b, c1_w, c1_b, c4_w, c5_w, mem_p, mem_s, rp_w, rp_b):
            xm = mamba(x, m1_in_w, m1_in_b, m1_conv_w, m1_conv_b, m1_ssm_w, m1_ssm_b, m1_A, m1_B, m1_C, m1_D, m1_out_w, m1_out_b)
            xm = mamba(xm, m2_in_w, m2_in_b, m2_conv_w, m2_conv_b, m2_ssm_w, m2_ssm_b, m2_A, m2_B, m2_C, m2_D, m2_out_w, m2_out_b)
            o = jnp.swapaxes(xm, 1, 2)
            residual = o
            o1 = bn_eval(jax.nn.relu(conv1d(o, c1_w, 1, 1, c1_b)))
            o4 = jax.nn.relu(conv1d(o, c4_w, 0))
            oc = jnp.concatenate([o1, o4], axis=1)
            o5 = bn_eval(jax.nn.relu(conv1d(oc, c5_w, 1)))
            out = jnp.swapaxes(o5 + residual, 1, 2)
            f = out[:, -1, :]
            dp = jnp.linalg.norm(mem_p[None] - f[:, None], axis=2)
            ds = jnp.linalg.norm(mem_s[None] - f[:, None], axis=2)
            dp = dp / (dp.max(axis=1, keepdims=True) + 1e-06)
            ds = ds / (ds.max(axis=1, keepdims=True) + 1e-06)
            anomaly = jnp.minimum(dp, ds).min(axis=1)
            recon = out @ rp_w + rp_b
            return (out, anomaly, recon)
        key = jax.random.key(seed)
        ks = iter(jax.random.split(key, 64))
        rn = lambda *s: jax.random.normal(next(ks), s, dtype=jnp.float32)
        inp = {'x': rn(B, T, D)}
        for p in ('m1', 'm2'):
            inp[p + '_in_w'] = rn(D, 2 * D) * 0.02
            inp[p + '_in_b'] = jnp.zeros((2 * D,), jnp.float32)
            inp[p + '_conv_w'] = rn(D, 1, K) * 0.1
            inp[p + '_conv_b'] = jnp.zeros((D,), jnp.float32)
            inp[p + '_ssm_w'] = rn(D, S) * 0.02
            inp[p + '_ssm_b'] = jnp.zeros((S,), jnp.float32)
            inp[p + '_A'] = -jnp.eye(S, dtype=jnp.float32)
            inp[p + '_B'] = rn(S) * 0.01
            inp[p + '_C'] = rn(S) * 0.01
            inp[p + '_D'] = jnp.ones((D,), jnp.float32)
            inp[p + '_out_w'] = rn(D, D) * 0.02
            inp[p + '_out_b'] = jnp.zeros((D,), jnp.float32)
        inp['c1_w'] = rn(64, D, 3) * 0.02
        inp['c1_b'] = jnp.zeros((64,), jnp.float32)
        inp['c4_w'] = rn(64, D, 1) * 0.02
        inp['c5_w'] = rn(128, 128, 3) * 0.02
        inp['mem_p'] = rn(M, D) * 0.01
        inp['mem_s'] = rn(M, D) * 0.01
        inp['rp_w'] = rn(D, D) * 0.02
        inp['rp_b'] = jnp.zeros((D,), jnp.float32)
        return inp
    _L3_attn_in = _L3_attn_setup()

    def _L3_ffn_setup():
        import jax, jax.numpy as jnp
        import numpy as np
        E = 8
        K = 2
        D = 128
        F = 512

        def _selected_matmul(inp, weight, scales, one_hot):
            wq = weight * scales
            all_out = jnp.einsum('mk,bkn->bmn', inp, wq)
            return jnp.einsum('bm,bmn->mn', one_hot, all_out)
        key = jax.random.key(seed)
        ks = jax.random.split(key, 8)
        inputs = jax.random.normal(ks[0], (1, 256, D), dtype=jnp.float32)
        router_w = jax.random.normal(ks[1], (D, E), dtype=jnp.float32) * 0.02
        wv = jax.random.normal(ks[2], (E, D, F), dtype=jnp.float32) * 0.02
        sv = jax.random.uniform(ks[3], (E, 1, F), dtype=jnp.float32, minval=0.5, maxval=1.5)
        w = jax.random.normal(ks[4], (E, D, F), dtype=jnp.float32) * 0.02
        s = jax.random.uniform(ks[5], (E, 1, F), dtype=jnp.float32, minval=0.5, maxval=1.5)
        w1 = jax.random.normal(ks[6], (E, F, D), dtype=jnp.float32) * 0.02
        s1 = jax.random.uniform(ks[7], (E, 1, D), dtype=jnp.float32, minval=0.5, maxval=1.5)
        return {'inputs': inputs, 'router_w': router_w, 'wv': wv, 'sv': sv, 'w': w, 's': s, 'w1': w1, 's1': s1}
    _L3_ffn_in = _L3_ffn_setup()
    _d = {'L0_attn_x': _L0_attn_in['x'], 'L0_attn_A': _L0_attn_in['A'], 'L0_attn_B_w': _L0_attn_in['B_w'], 'L0_attn_Wo': _L0_attn_in['Wo'], 'L0_attn_bo': _L0_attn_in['bo'], 'L0_ffn_router_w': _L0_ffn_in['router_w'], 'L0_ffn_w1': _L0_ffn_in['w1'], 'L0_ffn_w2': _L0_ffn_in['w2'], 'L1_attn_A': _L1_attn_in['A'], 'L1_attn_B': _L1_attn_in['B'], 'L1_attn_C': _L1_attn_in['C'], 'L1_attn_D': _L1_attn_in['D'], 'L1_ffn_Wp1': _L1_ffn_in['Wp1'], 'L1_ffn_bp1': _L1_ffn_in['bp1'], 'L1_ffn_Wp2': _L1_ffn_in['Wp2'], 'L1_ffn_bp2': _L1_ffn_in['bp2'], 'L1_ffn_W1': _L1_ffn_in['W1'], 'L1_ffn_b1': _L1_ffn_in['b1'], 'L1_ffn_W2': _L1_ffn_in['W2'], 'L1_ffn_b2': _L1_ffn_in['b2'], 'L1_ffn_Wo': _L1_ffn_in['Wo'], 'L1_ffn_bo': _L1_ffn_in['bo'], 'L2_attn_Wq': _L2_attn_in['Wq'], 'L2_attn_Wk': _L2_attn_in['Wk'], 'L2_attn_Wv': _L2_attn_in['Wv'], 'L2_attn_Wo': _L2_attn_in['Wo'], 'L2_ffn_gate_w': _L2_ffn_in['gate_w'], 'L2_ffn_gate_b': _L2_ffn_in['gate_b'], 'L2_ffn_expert_w': _L2_ffn_in['expert_w'], 'L2_ffn_expert_b': _L2_ffn_in['expert_b'], 'L3_attn_m1_in_w': _L3_attn_in['m1_in_w'], 'L3_attn_m1_in_b': _L3_attn_in['m1_in_b'], 'L3_attn_m1_conv_w': _L3_attn_in['m1_conv_w'], 'L3_attn_m1_conv_b': _L3_attn_in['m1_conv_b'], 'L3_attn_m1_ssm_w': _L3_attn_in['m1_ssm_w'], 'L3_attn_m1_ssm_b': _L3_attn_in['m1_ssm_b'], 'L3_attn_m1_A': _L3_attn_in['m1_A'], 'L3_attn_m1_B': _L3_attn_in['m1_B'], 'L3_attn_m1_C': _L3_attn_in['m1_C'], 'L3_attn_m1_D': _L3_attn_in['m1_D'], 'L3_attn_m1_out_w': _L3_attn_in['m1_out_w'], 'L3_attn_m1_out_b': _L3_attn_in['m1_out_b'], 'L3_attn_m2_in_w': _L3_attn_in['m2_in_w'], 'L3_attn_m2_in_b': _L3_attn_in['m2_in_b'], 'L3_attn_m2_conv_w': _L3_attn_in['m2_conv_w'], 'L3_attn_m2_conv_b': _L3_attn_in['m2_conv_b'], 'L3_attn_m2_ssm_w': _L3_attn_in['m2_ssm_w'], 'L3_attn_m2_ssm_b': _L3_attn_in['m2_ssm_b'], 'L3_attn_m2_A': _L3_attn_in['m2_A'], 'L3_attn_m2_B': _L3_attn_in['m2_B'], 'L3_attn_m2_C': _L3_attn_in['m2_C'], 'L3_attn_m2_D': _L3_attn_in['m2_D'], 'L3_attn_m2_out_w': _L3_attn_in['m2_out_w'], 'L3_attn_m2_out_b': _L3_attn_in['m2_out_b'], 'L3_attn_c1_w': _L3_attn_in['c1_w'], 'L3_attn_c1_b': _L3_attn_in['c1_b'], 'L3_attn_c4_w': _L3_attn_in['c4_w'], 'L3_attn_c5_w': _L3_attn_in['c5_w'], 'L3_attn_mem_p': _L3_attn_in['mem_p'], 'L3_attn_mem_s': _L3_attn_in['mem_s'], 'L3_attn_rp_w': _L3_attn_in['rp_w'], 'L3_attn_rp_b': _L3_attn_in['rp_b'], 'L3_ffn_router_w': _L3_ffn_in['router_w'], 'L3_ffn_wv': _L3_ffn_in['wv'], 'L3_ffn_sv': _L3_ffn_in['sv'], 'L3_ffn_w': _L3_ffn_in['w'], 'L3_ffn_s': _L3_ffn_in['s'], 'L3_ffn_w1': _L3_ffn_in['w1'], 'L3_ffn_s1': _L3_ffn_in['s1']}
    _x0 = _d['L0_attn_x']
    _d['L0_attn_x'] = jax.random.normal(jax.random.fold_in(jax.random.key(seed), 1), (8, 512, 128), dtype=_x0.dtype)
    del _x0
    return _d

def reference(L0_attn_x, L0_attn_A, L0_attn_B_w, L0_attn_Wo, L0_attn_bo, L0_ffn_router_w, L0_ffn_w1, L0_ffn_w2, L1_attn_A, L1_attn_B, L1_attn_C, L1_attn_D, L1_ffn_Wp1, L1_ffn_bp1, L1_ffn_Wp2, L1_ffn_bp2, L1_ffn_W1, L1_ffn_b1, L1_ffn_W2, L1_ffn_b2, L1_ffn_Wo, L1_ffn_bo, L2_attn_Wq, L2_attn_Wk, L2_attn_Wv, L2_attn_Wo, L2_ffn_gate_w, L2_ffn_gate_b, L2_ffn_expert_w, L2_ffn_expert_b, L3_attn_m1_in_w, L3_attn_m1_in_b, L3_attn_m1_conv_w, L3_attn_m1_conv_b, L3_attn_m1_ssm_w, L3_attn_m1_ssm_b, L3_attn_m1_A, L3_attn_m1_B, L3_attn_m1_C, L3_attn_m1_D, L3_attn_m1_out_w, L3_attn_m1_out_b, L3_attn_m2_in_w, L3_attn_m2_in_b, L3_attn_m2_conv_w, L3_attn_m2_conv_b, L3_attn_m2_ssm_w, L3_attn_m2_ssm_b, L3_attn_m2_A, L3_attn_m2_B, L3_attn_m2_C, L3_attn_m2_D, L3_attn_m2_out_w, L3_attn_m2_out_b, L3_attn_c1_w, L3_attn_c1_b, L3_attn_c4_w, L3_attn_c5_w, L3_attn_mem_p, L3_attn_mem_s, L3_attn_rp_w, L3_attn_rp_b, L3_ffn_router_w, L3_ffn_wv, L3_ffn_sv, L3_ffn_w, L3_ffn_s, L3_ffn_w1, L3_ffn_s1):

    def _L0_attn_ref(x, A, B_w, Wo, bo):
        import jax, jax.numpy as jnp
        import numpy as np
        Bsz = x.shape[0]
        D_state = A.shape[0]
        exp_decay = jnp.exp(-jnp.minimum(A, 10.0))
        Bx = jnp.einsum('bsi,ni->bsn', x, B_w)

        def step(state, bx_t):
            state = jnp.tanh(exp_decay * state + bx_t)
            return (state, state)
        init = jnp.zeros((Bsz, D_state), dtype=x.dtype)
        _, h = jax.lax.scan(step, init, jnp.swapaxes(Bx, 0, 1))
        h = jnp.swapaxes(h, 0, 1)
        out = jnp.einsum('bsn,on->bso', h, Wo) + bo
        return out

    def _L0_ffn_ref(x, router_w, w1, w2):
        import jax, jax.numpy as jnp
        import numpy as np
        B, S, D, H, E = (2, 256, 128, 512, 8)
        b, s, d = x.shape
        e = router_w.shape[0]
        xf = x.reshape(-1, d)
        probs = jax.nn.softmax(xf @ router_w.T, axis=-1)
        topv, topi = jax.lax.top_k(probs, 2)
        topv = topv / (topv.sum(axis=-1, keepdims=True) + 1e-09)
        cw = (jax.nn.one_hot(topi, e, dtype=xf.dtype) * topv[..., None]).sum(axis=1)
        h = jax.nn.gelu(jnp.einsum('td,edh->teh', xf, w1), approximate=False)
        y = jnp.einsum('teh,ehd->ted', h, w2)
        out = jnp.einsum('te,ted->td', cw, y)
        return out.reshape(b, s, d)

    def _L1_attn_ref(x, A, B, C, D):
        import jax, jax.numpy as jnp
        import numpy as np
        D_MODEL = 128
        D_STATE = 32
        a_bar = jnp.exp(-jnp.exp(A))
        Bx = jnp.einsum('bsd,nd->bsn', x, B)

        def step(h, bx_t):
            h = a_bar * h + bx_t
            return (h, h)
        h0 = jnp.zeros((x.shape[0], A.shape[0]), dtype=x.dtype)
        _, hs = jax.lax.scan(step, h0, jnp.swapaxes(Bx, 0, 1))
        hs = jnp.swapaxes(hs, 0, 1)
        y = jnp.einsum('bsn,dn->bsd', hs, C) + D * x
        return y

    def _L1_ffn_ref(hidden_states, Wp1, bp1, Wp2, bp2, W1, b1, W2, b2, Wo, bo):
        import jax, jax.numpy as jnp
        import numpy as np
        B, S, H = (8, 512, 128)
        NAV = 128
        E = 8
        F = 2 * H
        last = hidden_states[:, -1, :]
        logits = jax.nn.gelu(last @ Wp1 + bp1, approximate=False) @ Wp2 + bp2
        action_probs = jax.nn.softmax(logits, axis=-1)
        sel = jnp.argmax(action_probs, axis=-1)
        w1 = W1[sel]
        w2 = W2[sel]
        h = jax.nn.gelu(jnp.einsum('bsh,bhf->bsf', hidden_states, w1) + b1[sel][:, None, :], approximate=False)
        reasoned = jnp.einsum('bsf,bfh->bsh', h, w2) + b2[sel][:, None, :]
        out = reasoned @ Wo + bo
        return hidden_states + 0.3 * out

    def _L2_attn_ref(x, Wq, Wk, Wv, Wo):
        import jax, jax.numpy as jnp
        import numpy as np
        H = 16
        G = 4
        THETA = 10000.0

        def _rope(x, cos, sin):
            x0 = x[..., ::2]
            x1 = x[..., 1::2]
            r0 = x0 * cos - x1 * sin
            r1 = x0 * sin + x1 * cos
            return jnp.stack([r0, r1], axis=-1).reshape(x.shape)
        B, S, D = x.shape
        hd = D // H
        Hkv = H // G
        q = x @ Wq
        k = x @ Wk
        v = x @ Wv
        k = jnp.repeat(k.reshape(B, S, Hkv, hd), G, axis=2)
        v = jnp.repeat(v.reshape(B, S, Hkv, hd), G, axis=2)
        inv = 1.0 / THETA ** (jnp.arange(0, D, 2, dtype=jnp.float32) / D)
        ang = jnp.arange(S, dtype=jnp.float32)[:, None] * inv[None, :]
        q = _rope(q, jnp.cos(ang)[None], jnp.sin(ang)[None])
        angk = ang[:, :hd // 2]
        k = _rope(k, jnp.cos(angk)[None, :, None, :], jnp.sin(angk)[None, :, None, :])
        q = q.reshape(B, S, H, hd).transpose(0, 2, 1, 3)
        k = k.transpose(0, 2, 1, 3)
        v = v.transpose(0, 2, 1, 3)
        scores = jnp.einsum('bhqd,bhkd->bhqk', q, k) / jnp.sqrt(jnp.float32(D))
        p = jax.nn.softmax(scores, axis=-1)
        o = jnp.einsum('bhqk,bhkd->bhqd', p, v)
        o = o.transpose(0, 2, 1, 3).reshape(B, S, D)
        return o @ Wo

    def _L2_ffn_ref(x, gate_w, gate_b, expert_w, expert_b):
        import jax, jax.numpy as jnp
        import numpy as np
        B, S, D, O, E, K = (4, 256, 128, 128, 8, 2)
        logits = jnp.einsum('bsd,ed->bse', x, gate_w) + gate_b
        if K < E:
            topv, topi = jax.lax.top_k(logits, K)
            keep = jax.nn.one_hot(topi, E, dtype=jnp.float32).sum(axis=-2)
            logits = jnp.where(keep > 0, logits, -jnp.inf)
        gate_score = jax.nn.softmax(logits, axis=-1)
        expert_out = jnp.einsum('bsd,edo->bseo', x, expert_w) + expert_b
        out = jnp.einsum('bseo,bse->bso', expert_out, gate_score)
        return out

    def _L3_attn_ref(x, m1_in_w, m1_in_b, m1_conv_w, m1_conv_b, m1_ssm_w, m1_ssm_b, m1_A, m1_B, m1_C, m1_D, m1_out_w, m1_out_b, m2_in_w, m2_in_b, m2_conv_w, m2_conv_b, m2_ssm_w, m2_ssm_b, m2_A, m2_B, m2_C, m2_D, m2_out_w, m2_out_b, c1_w, c1_b, c4_w, c5_w, mem_p, mem_s, rp_w, rp_b):
        import jax, jax.numpy as jnp
        import numpy as np
        from jax import lax
        B, T, D = (16, 256, 128)
        S, K, M = (32, 4, 32)
        BN_EPS = 1e-05

        def silu(x):
            return x * jax.nn.sigmoid(x)

        def bn_eval(x):
            return x / np.float32(np.sqrt(1.0 + BN_EPS))

        def conv1d(x, w, pad, dil=1, b=None):
            y = lax.conv_general_dilated(x, w, (1,), ((pad, pad),), rhs_dilation=(dil,), dimension_numbers=('NCH', 'OIH', 'NCH'))
            if b is not None:
                y = y + b[None, :, None]
            return y

        def dwconv_causal(x, w, b):
            y = lax.conv_general_dilated(jnp.swapaxes(x, 1, 2), w, (1,), ((K - 1, 0),), dimension_numbers=('NCH', 'OIH', 'NCH'), feature_group_count=w.shape[0])
            return jnp.swapaxes(y + b[None, :, None], 1, 2)

        def mamba(x, in_w, in_b, conv_w, conv_b, ssm_w, ssm_b, A, Bv, Cv, Dv, out_w, out_b):
            xz = x @ in_w + in_b
            xs, gate = jnp.split(xz, 2, axis=-1)
            u = silu(dwconv_causal(xs, conv_w, conv_b))
            xssm = u @ ssm_w + ssm_b
            h0 = jnp.zeros((x.shape[0], A.shape[0]), x.dtype)

            def step(h, xt):
                h = h @ A.T + xt * Bv
                return (h, h @ Cv)
            _, c = lax.scan(step, h0, jnp.swapaxes(xssm, 0, 1))
            y = (jnp.swapaxes(c, 0, 1)[..., None] + Dv) * u
            y = y * silu(gate)
            return y @ out_w + out_b + x

        def _reference_tuple_inner(x, m1_in_w, m1_in_b, m1_conv_w, m1_conv_b, m1_ssm_w, m1_ssm_b, m1_A, m1_B, m1_C, m1_D, m1_out_w, m1_out_b, m2_in_w, m2_in_b, m2_conv_w, m2_conv_b, m2_ssm_w, m2_ssm_b, m2_A, m2_B, m2_C, m2_D, m2_out_w, m2_out_b, c1_w, c1_b, c4_w, c5_w, mem_p, mem_s, rp_w, rp_b):
            xm = mamba(x, m1_in_w, m1_in_b, m1_conv_w, m1_conv_b, m1_ssm_w, m1_ssm_b, m1_A, m1_B, m1_C, m1_D, m1_out_w, m1_out_b)
            xm = mamba(xm, m2_in_w, m2_in_b, m2_conv_w, m2_conv_b, m2_ssm_w, m2_ssm_b, m2_A, m2_B, m2_C, m2_D, m2_out_w, m2_out_b)
            o = jnp.swapaxes(xm, 1, 2)
            residual = o
            o1 = bn_eval(jax.nn.relu(conv1d(o, c1_w, 1, 1, c1_b)))
            o4 = jax.nn.relu(conv1d(o, c4_w, 0))
            oc = jnp.concatenate([o1, o4], axis=1)
            o5 = bn_eval(jax.nn.relu(conv1d(oc, c5_w, 1)))
            out = jnp.swapaxes(o5 + residual, 1, 2)
            f = out[:, -1, :]
            dp = jnp.linalg.norm(mem_p[None] - f[:, None], axis=2)
            ds = jnp.linalg.norm(mem_s[None] - f[:, None], axis=2)
            dp = dp / (dp.max(axis=1, keepdims=True) + 1e-06)
            ds = ds / (ds.max(axis=1, keepdims=True) + 1e-06)
            anomaly = jnp.minimum(dp, ds).min(axis=1)
            recon = out @ rp_w + rp_b
            return (out, anomaly, recon)
        return _reference_tuple_inner(x, m1_in_w, m1_in_b, m1_conv_w, m1_conv_b, m1_ssm_w, m1_ssm_b, m1_A, m1_B, m1_C, m1_D, m1_out_w, m1_out_b, m2_in_w, m2_in_b, m2_conv_w, m2_conv_b, m2_ssm_w, m2_ssm_b, m2_A, m2_B, m2_C, m2_D, m2_out_w, m2_out_b, c1_w, c1_b, c4_w, c5_w, mem_p, mem_s, rp_w, rp_b)[0]

    def _L3_ffn_ref(inputs, router_w, wv, sv, w, s, w1, s1):
        import jax, jax.numpy as jnp
        import numpy as np
        E = 8
        K = 2
        D = 128
        F = 512

        def _selected_matmul(inp, weight, scales, one_hot):
            wq = weight * scales
            all_out = jnp.einsum('mk,bkn->bmn', inp, wq)
            return jnp.einsum('bm,bmn->mn', one_hot, all_out)
        B, S, Dm = inputs.shape
        x = inputs.reshape(B * S, Dm)
        logits = jnp.dot(x.astype(jnp.float32), router_w)
        probs = jax.nn.softmax(logits, axis=-1)
        expert_gate, expert_index = jax.lax.top_k(probs, K)
        xb = jnp.repeat(x, K, axis=0)
        one_hot = jax.nn.one_hot(expert_index.reshape(-1), E, axis=0)
        v = _selected_matmul(xb, wv, sv, one_hot)
        y = jax.nn.gelu(_selected_matmul(xb, w, s, one_hot))
        out = _selected_matmul(v * y, w1, s1, one_hot)
        out = out.reshape(B, S, K, Dm)
        out = jnp.sum(expert_gate.reshape(B, S, K, 1) * out, axis=2)
        return out
    x = L0_attn_x
    xn = _layernorm(x, axis=-1)
    s = _L0_attn_ref(xn, L0_attn_A, L0_attn_B_w, L0_attn_Wo, L0_attn_bo)
    g = _silu(_L0_ffn_ref(xn, L0_ffn_router_w, L0_ffn_w1, L0_ffn_w2))
    x = x + s * g
    xn = _layernorm(x, axis=-1)
    s = _L1_attn_ref(xn, L1_attn_A, L1_attn_B, L1_attn_C, L1_attn_D)
    g = _silu(_L1_ffn_ref(xn, L1_ffn_Wp1, L1_ffn_bp1, L1_ffn_Wp2, L1_ffn_bp2, L1_ffn_W1, L1_ffn_b1, L1_ffn_W2, L1_ffn_b2, L1_ffn_Wo, L1_ffn_bo))
    x = x + s * g
    xn = _layernorm(x, axis=-1)
    s = _L2_attn_ref(xn, L2_attn_Wq, L2_attn_Wk, L2_attn_Wv, L2_attn_Wo)
    g = _silu(_L2_ffn_ref(xn, L2_ffn_gate_w, L2_ffn_gate_b, L2_ffn_expert_w, L2_ffn_expert_b))
    x = x + s * g
    xn = _layernorm(x, axis=-1)
    s = _L3_attn_ref(xn, L3_attn_m1_in_w, L3_attn_m1_in_b, L3_attn_m1_conv_w, L3_attn_m1_conv_b, L3_attn_m1_ssm_w, L3_attn_m1_ssm_b, L3_attn_m1_A, L3_attn_m1_B, L3_attn_m1_C, L3_attn_m1_D, L3_attn_m1_out_w, L3_attn_m1_out_b, L3_attn_m2_in_w, L3_attn_m2_in_b, L3_attn_m2_conv_w, L3_attn_m2_conv_b, L3_attn_m2_ssm_w, L3_attn_m2_ssm_b, L3_attn_m2_A, L3_attn_m2_B, L3_attn_m2_C, L3_attn_m2_D, L3_attn_m2_out_w, L3_attn_m2_out_b, L3_attn_c1_w, L3_attn_c1_b, L3_attn_c4_w, L3_attn_c5_w, L3_attn_mem_p, L3_attn_mem_s, L3_attn_rp_w, L3_attn_rp_b)
    g = _silu(_L3_ffn_ref(xn, L3_ffn_router_w, L3_ffn_wv, L3_ffn_sv, L3_ffn_w, L3_ffn_s, L3_ffn_w1, L3_ffn_s1))
    x = x + s * g
    return x

_drawn_inputs = setup_inputs


def setup_inputs(seed=0):
    import zlib

    import numpy as np

    out = dict(_drawn_inputs(seed))
    spreads = {'L1_attn_D': (1.0, 0.2),
     'L1_ffn_bp1': (0.0, 0.1),
     'L1_ffn_bp2': (0.0, 0.1),
     'L1_ffn_b1': (0.0, 0.1),
     'L1_ffn_b2': (0.0, 0.1),
     'L1_ffn_bo': (0.0, 0.1),
     'L3_attn_m1_in_b': (0.0, 0.1),
     'L3_attn_m1_conv_b': (0.0, 0.1),
     'L3_attn_m1_ssm_b': (0.0, 0.1),
     'L3_attn_m1_D': (1.0, 0.2),
     'L3_attn_m1_out_b': (0.0, 0.1),
     'L3_attn_m2_in_b': (0.0, 0.1),
     'L3_attn_m2_conv_b': (0.0, 0.1),
     'L3_attn_m2_ssm_b': (0.0, 0.1),
     'L3_attn_m2_D': (1.0, 0.2),
     'L3_attn_m2_out_b': (0.0, 0.1),
     'L3_attn_c1_b': (0.0, 0.1),
     'L3_attn_rp_b': (0.0, 0.1)}
    factors = {}
    for name, (base, spread) in spreads.items():
        noise = np.random.default_rng([zlib.crc32(name.encode()), seed]).standard_normal(out[name].shape)
        drawn = base * np.exp(spread * noise) if base else spread * noise
        out[name] = jnp.asarray(drawn.astype(out[name].dtype))
    for name, factor in factors.items():
        out[name] = (out[name] * factor).astype(out[name].dtype)
    return out
```

```python
from contextlib import ExitStack

import numpy as np
import concourse.bass as bass
from concourse import mybir

ALU = mybir.AluOpType
ACT = mybir.ActivationFunctionType
AX_X = mybir.AxisListType.X
F32 = mybir.dt.float32
F32R = mybir.dt.float32r
U32 = mybir.dt.uint32

P = 128
NB, T, D = 8, 512, 128
NQ = T // P
NE = 8
HC = 4
HEADS, HD, NG = 16, 8, 4
LN_EPS = 1e-5
SM_SCALE = float(1.0 / np.sqrt(np.float32(D)))
BN_SCALE = float(1.0 / np.float32(np.sqrt(1.0 + 1e-5)))
CREDIT = 2000
STEPS = T // NB

C_L0A, C_L0BO, C_L1A, C_L1D, C_BP1, C_L1BO, C_C1B = range(7)
C_INX, C_ING, C_CVB, C_CVW, C_SSB, C_BV, C_DV, C_OB, C_CV = 0, 1, 2, 3, 7, 8, 9, 10, 11
C_M = (8, 20)
NCV = 32


class Progress:

    def __init__(self, nc, ctx, known):
        self.eng = {"PE": nc.tensor, "DVE": nc.vector, "ACT": nc.scalar, "POOL": nc.gpsimd, "SP": nc.sync}
        self.nc, self.ctx, self.known = nc, ctx, known
        self.sem, self.count = {}, {}
        for e in ("PE", "DVE", "ACT", "POOL"):
            self.sem[e] = ctx.enter_context(nc.semaphore(f"progress_{e}"))
            self.count[e] = CREDIT
            self.eng[e].sem_inc(self.sem[e], CREDIT)
        self.names, self.loops = {}, {}
        self.loop, self.seen = None, {}

    def dma(self, name, credit=0):
        self.sem[name] = self.ctx.enter_context(self.nc.semaphore(f"dma_{name}"))
        self.count[name] = credit
        if credit:
            self.nc.sync.sem_inc(self.sem[name], credit)

    def enter(self, name, i, n):
        self.loop, self.i, self.n, self.seen = name, i, n, {}
        self.base = dict(self.count)

    def leave(self):
        for e in self.count:
            per = self.count[e] - self.base[e]
            self.loops[(self.loop, e)] = (self.base[e], per, self.n)
            self.count[e] = self.base[e] + per * self.n
        self.loop, self.seen = None, {}

    def done(self, chan, instr, name=None, by=1):
        instr.then_inc(self.sem[chan], by)
        self.count[chan] += by
        if name:
            assert (self.loop, name) not in self.names, name
            self.names[(self.loop, name)] = (chan, self.count[chan] - (self.base[chan] if self.loop else 0))

    def wait(self, engine, *names, lag=0, of=None, alone=False):
        if not self.known:
            return
        names_of, loops = self.known
        loop = of if of is not None else self.loop
        if loop == "start":
            loop = None
        need = {}
        for name in names:
            chan, k = names_of[(loop, name)]
            need[chan] = max(need.get(chan, 0), k)
        for chan, k in need.items():
            key = (engine, chan, loop, lag)
            if self.seen.get(key, -1) >= k:
                continue
            self.seen[key] = k
            value = k
            if loop:
                base, per, n = loops[(loop, chan)]
                if loop == self.loop:
                    value = self.i * per + (base + k - lag * per)
                else:
                    value = base + (n - 1) * per + k
            self.eng[engine].wait_ge(self.sem[chan], value)
            if alone:
                self.eng[engine].sem_inc(self.sem["aside"], 1)


def build(nc, known, a, out):
    V, A, PE, G, S = nc.vector, nc.scalar, nc.tensor, nc.gpsimd, nc.sync
    ctx = ExitStack()
    pr = Progress(nc, ctx, known)
    done, wait = pr.done, pr.wait
    pr.dma("aside")

    def sb(name, shape, dt=F32, c=ctx):
        return c.enter_context(nc.sbuf_tensor(name, shape, dt))

    bank = [ctx.enter_context(nc.psum_tensor(f"bank{i}", [P, T], F32)) for i in range(8)]

    def tt(o, x, y, op):
        return V.tensor_tensor(o, x, y, op)

    def ts(o, x, s1, s2, op0, op1=None):
        return V.tensor_scalar(o, x, s1, s2, op0, op1) if op1 is not None else V.tensor_scalar(o, x, s1, s2, op0)

    def stt(o, x, s, y, op0, op1):
        return V.scalar_tensor_tensor(out=o, in0=x, scalar=s, in1=y, op0=op0, op1=op1)

    def mm(o, l, r, start=True, stop=True):
        return PE.matmul(o, l, r, start=start, stop=stop)

    def load(dst, src, name):
        done(name, S.dma_start(dst, src), by=16)

    X = sb("X", [P, NB * NQ, D])
    WA = sb("WA", [P, NE, T])
    WB = sb("WB", [P, NE, T])
    WC = sb("WC", [P, NE, T])
    cv = sb("cv", [P, NCV])
    ident = sb("ident", [P, P])
    iota = sb("iota", [P, NQ, NE])
    expo = sb("expo", [P, NQ])
    cw = sb("cw", [P, NB * NQ, NE])
    xf = sb("xf", [P, T])
    st = sb("st", [P, NQ, 6])
    mv = sb("mv", [P, NQ, 2])
    rstd = sb("rstd", [P, 2, NQ])
    xn = sb("xn", [P, NQ, D])
    lg = sb("lg", [P, NQ, NE])
    mx = sb("mx", [P, NQ, 8])
    ix = sb("ix", [P, NQ, 8], U32)
    ixf = sb("ixf", [P, NQ, 2])
    sel = sb("sel", [P, NQ, NE])
    sel2 = sb("sel2", [P, NQ, NE])
    ee = sb("ee", [P, NQ, NE])
    zz = sb("zz", [P, 4, NQ])

    def col(c, n=P):
        return cv[0:n, c:c + 1]

    pr.dma("in")
    load(X[:], a["x"].rearrange("b (q p) d -> p (b q) d", p=P), "in")
    load(cv[:], a["cv"], "in")
    load(ident[:], a["ident"], "in")
    load(iota[:], a["iota"].rearrange("p (q e) -> p q e", q=NQ), "in")

    def layer_norm(b, first):
        V.sem_inc(pr.sem["aside"], 1)
        for q in range(NQ):
            last = V.bn_stats(st[:, q, :], X[:, bass.ds(b * NQ + q, 1), :].rearrange("p a d -> p (a d)"))
        done("DVE", last, f"{first}.stats")
        wait("DVE", f"{first}.stats")
        wait("DVE", f"{first}.rstd", lag=1, alone=True)
        for q in range(NQ):
            last = V.bn_aggr(mv[:, q, :], st[:, q, :])
        done("DVE", last, f"{first}.aggr")
        wait("POOL", f"{first}.aggr", alone=True)
        done("POOL", G.tensor_scalar(rstd[:, 0, :], mv[:, :, 1], LN_EPS, None, ALU.add), f"{first}.var")
        wait("POOL", f"{first}.var", alone=True)
        done("POOL", G.tensor_tensor(rstd[:, 1, :], rstd[:, 0, :], expo[:], ALU.pow), f"{first}.rstd")
        wait("DVE", f"{first}.rstd")
        for q in range(NQ):
            last = ts(xn[:, q, :], X[:, bass.ds(b * NQ + q, 1), :].rearrange("p a d -> p (a d)"),
                      mv[:, q, 0:1], rstd[:, 1, q:q + 1], ALU.subtract, ALU.mult)
        done("DVE", last, f"{first}.xn")
        wait("PE", f"{first}.xn")
        for q in range(NQ):
            last = PE.transpose(bank[0][:, q * P:(q + 1) * P], xn[:, q, :], ident[:])
        done("PE", last, f"{first}.xnT")
        wait("ACT", f"{first}.xnT")
        done("ACT", A.copy(xf[:], bank[0][:]), f"{first}.xf")

    def top_two(n, kind, bias=None, dst=None):
        wait("DVE", f"{n}.logits")
        src = bank[1][:, 0:NQ * NE].rearrange("p (q e) -> p q e", q=NQ)
        if bias is None:
            done("DVE", V.tensor_copy(lg[:], src), f"{n}.lg")
        else:
            done("DVE", tt(lg[:], src, bias, ALU.add), f"{n}.lg")
        wait("DVE", f"{n}.lg", alone=True)
        for q in range(NQ):
            last = V.max(mx[:, q, :], lg[:, q, :])
        done("DVE", last, f"{n}.mx")
        wait("DVE", f"{n}.mx", alone=True)
        for q in range(NQ):
            last = V.max_index(ix[:, q, :], mx[:, q, :], lg[:, q, :])
        done("DVE", last, f"{n}.ix")
        done("DVE", tt(ee[:], lg[:], mx[:, :, 0:1].to_broadcast([P, NQ, NE]), ALU.subtract), f"{n}.shift")
        wait("DVE", f"{n}.ix")
        done("DVE", V.tensor_copy(ixf[:], ix[:, :, 0:2]), f"{n}.ixf")
        wait("DVE", f"{n}.ixf")
        tt(sel[:], iota[:], ixf[:, :, 0:1].to_broadcast([P, NQ, NE]), ALU.is_equal)
        done("DVE", tt(sel2[:], iota[:], ixf[:, :, 1:2].to_broadcast([P, NQ, NE]), ALU.is_equal), f"{n}.sel2")
        wait("DVE", f"{n}.sel2")
        done("DVE", tt(sel[:], sel[:], sel2[:], ALU.add), f"{n}.sel")
        wait("ACT", f"{n}.shift")
        done("ACT", A.activation(ee[:], ee[:], ACT.Exp), f"{n}.exp")
        wait("DVE", f"{n}.exp", f"{n}.sel")
        if kind != "masked":
            done("DVE", V.tensor_reduce(zz[:, 0, :], ee[:], AX_X, ALU.add), f"{n}.z0")
            wait("DVE", f"{n}.z0")
            done("DVE", V.reciprocal(zz[:, 1, :], zz[:, 0, :]), f"{n}.z1")
            wait("DVE", f"{n}.z1")
            done("DVE", tt(ee[:], ee[:], zz[:, 1, :].unsqueeze(2).to_broadcast([P, NQ, NE]), ALU.mult), f"{n}.p")
            wait("DVE", f"{n}.p")
        if kind == "probs":
            done("DVE", tt(dst, ee[:], sel[:], ALU.mult), f"{n}.w")
            return
        done("DVE", tt(ee[:], ee[:], sel[:], ALU.mult), f"{n}.ps")
        wait("DVE", f"{n}.ps")
        done("DVE", V.tensor_reduce(zz[:, 2, :], ee[:], AX_X, ALU.add), f"{n}.s0")
        wait("DVE", f"{n}.s0")
        if kind == "renormed":
            done("DVE", ts(zz[:, 2, :], zz[:, 2, :], 1e-9, None, ALU.add), f"{n}.s1")
            wait("DVE", f"{n}.s1")
        done("DVE", V.reciprocal(zz[:, 3, :], zz[:, 2, :]), f"{n}.s2")
        wait("DVE", f"{n}.s2")
        done("DVE", tt(dst, ee[:], zz[:, 3, :].unsqueeze(2).to_broadcast([P, NQ, NE]), ALU.mult), f"{n}.w")

    ph0 = ExitStack()
    GT = sb("GT", [P, NB * NQ, D], c=ph0)
    H = sb("H", [P, NB, T], c=ph0)
    s0 = sb("s0", [P, 2, T], c=ph0)
    BX = sb("BX", [P, NB, T], c=ph0)
    l0bw = sb("l0bw", [P, D], c=ph0)
    l0rw = sb("l0rw", [P, NE], c=ph0)
    decay = sb("decay", [P, 2], c=ph0)
    HG = sb("HG", [P, 2, HC, T], c=ph0)
    acc = sb("acc", [P, NQ, D], c=ph0)
    cwb = sb("cwb", [P, NQ, NE], c=ph0)
    bxs = sb("bxs", [P, STEPS, NB], c=ph0)
    hs0 = sb("hs0", [P, STEPS + 1, NB], c=ph0)
    ub = sb("ub", [P, NB], c=ph0)

    load(l0bw[:], a["l0_bw"], "in")
    l0wo = sb("l0wo", [P, D], c=ph0)
    load(l0wo[:], a["l0_wo"], "in")
    load(l0rw[:], a["l0_rw"], "in")
    pr.dma("w0")
    load(WA[:], a["l0_w1"], "w0")
    load(WB[:], a["l0_w2"], "w0")
    pr.names[(None, "in")] = ("in", pr.count["in"])
    pr.names[(None, "w0")] = ("w0", pr.count["w0"])
    for e in ("PE", "DVE", "ACT", "POOL"):
        wait(e, "in")
    done("POOL", G.memset(expo[:], -0.5), "expo")
    wait("POOL", "expo")
    done("DVE", ts(decay[:, 0:1], col(C_L0A), 10.0, None, ALU.min), "amin")
    done("DVE", V.memset(hs0[:, STEPS, :], 0.0), "h_init")
    wait("ACT", "amin")
    done("ACT", A.activation(decay[:, 1:2], decay[:, 0:1], ACT.Exp, scale=-1.0), "decay")
    wait("DVE", "decay")

    with nc.Fori(0, NB) as b:
        pr.enter("prep", b, NB)
        wait("DVE", "n.xnT", lag=1)
        wait("ACT", "bx", "bx.copied", "xn.kept", lag=1)
        layer_norm(b, "n")
        wait("PE", "n.xf")
        wait("PE", "r.lg", lag=1)
        for q in range(NQ):
            last = mm(bank[1][:, q * NE:(q + 1) * NE], xf[:, q * P:(q + 1) * P], l0rw[:])
        done("PE", last, "r.logits")
        wait("PE", "bx.copied", lag=1)
        done("PE", mm(bank[2][:], l0bw[:], xf[:]), "bx")
        wait("POOL", "n.xf")
        done("POOL", G.tensor_copy(WC[:, bass.ds(b, 1), :].rearrange("p a n -> p (a n)"), xf[:]), "xn.kept")
        wait("ACT", "bx")
        done("ACT", A.copy(BX[:, bass.ds(b, 1), :].rearrange("p a n -> p (a n)"), bank[2][:]), "bx.copied")
        top_two("r", "renormed", dst=cw[:, bass.ds(b * NQ, NQ), :])
        pr.leave()

    wait("PE", "w0", of="start")
    wait("PE", "xn.kept", "bx.copied", "r.lg", of="prep")
    with nc.Fori(0, NB) as b:
        pr.enter("moe0", b, NB)
        wait("POOL", "bx.copied", of="prep")
        wait("POOL", f"u{STEPS - 1}", lag=1)
        done("POOL", G.tensor_copy(bxs[:], BX[:, :, bass.ds(b * STEPS, STEPS)].rearrange("p n t -> p t n")), "bxs")
        wait("DVE", "r.w", of="prep")
        wait("DVE", f"acc{NE - 1}.{NQ - 1}", lag=1)
        done("DVE", V.tensor_copy(cwb[:], cw[:, bass.ds(b * NQ, NQ), :]), "cwb")
        wait("DVE", "cwb")
        wait("ACT", "h.kept", lag=1)
        wait("ACT", f"h{STEPS - 1}", lag=1)
        done("ACT", A.copy(hs0[:, 0, :], hs0[:, STEPS, :]), "h.carry")

        def step(s):
            if s == 0:
                wait("DVE", "bxs", "h.carry")
            else:
                wait("DVE", f"h{s - 1}")
            done("DVE", stt(ub[:], hs0[:, s, :], decay[:, 1:2], bxs[:, s, :], ALU.mult, ALU.add), f"u{s}")
            wait("ACT", f"u{s}")
            done("ACT", A.activation(hs0[:, s + 1, :], ub[:], ACT.Tanh), f"h{s}")

        def accumulate(e, q):
            if q == 0:
                wait("DVE", f"y{e}")
                if e == 0:
                    wait("DVE", "acc.kept", lag=1)
            ys = bank[4 + e % 2][:, q * D:(q + 1) * D]
            w = cwb[:, q, e:e + 1]
            if e == 0:
                op = ts(acc[:, q, :], ys, w, None, ALU.mult)
            else:
                wait("DVE", f"acc{e - 1}.{q}")
                op = stt(acc[:, q, :], ys, w, acc[:, q, :], ALU.mult, ALU.add)
            done("DVE", op, f"acc{e}.{q}")

        def down(e):
            wait("PE", f"g{e}.{HC - 1}")
            if e >= 2:
                wait("PE", f"acc{e - 2}.{NQ - 1}")
            else:
                wait("PE", f"acc{NE - 2 + e}.{NQ - 1}", lag=1)
            for q in range(NQ):
                for m in range(HC):
                    last = mm(bank[4 + e % 2][:, q * D:(q + 1) * D], HG[:, e % 2, m, q * P:(q + 1) * P],
                              WB[:, e, m * D:(m + 1) * D], start=(m == 0), stop=(m == HC - 1))
            done("PE", last, f"y{e}")

        per = STEPS // (NE * HC)
        for e in range(NE):
            for m in range(HC):
                if e >= 1:
                    wait("PE", f"g{e - 1}.{m}")
                else:
                    wait("PE", f"g{NE - 1}.{m}", lag=1)
                done("PE", mm(bank[m][:], WA[:, e, m * P:(m + 1) * P],
                              WC[:, bass.ds(b, 1), :].rearrange("p a n -> p (a n)")), f"x{e}.{m}")
            if e >= 1:
                down(e - 1)
            for m in range(HC):
                wait("ACT", f"x{e}.{m}")
                if m == 0:
                    if e >= 2:
                        wait("ACT", f"y{e - 2}")
                    else:
                        wait("ACT", f"y{NE - 2 + e}", lag=1)
                done("ACT", A.activation(HG[:, e % 2, m, :], bank[m][:], ACT.Gelu), f"g{e}.{m}")
                for s in range(per):
                    step((e * HC + m) * per + s)
                if e >= 2:
                    accumulate(e - 2, m)
        down(NE - 1)
        for q in range(NQ):
            accumulate(NE - 2, q)
        for q in range(NQ):
            accumulate(NE - 1, q)
        wait("POOL", f"h{STEPS - 1}")
        done("POOL", G.tensor_copy(H[:, :, bass.ds(b * STEPS, STEPS)],
                                   hs0[:, 1:STEPS + 1, :].rearrange("p t n -> p n t")), "h.kept")
        wait("POOL", f"acc{NE - 1}.{NQ - 1}")
        done("POOL", G.tensor_copy(GT[:, bass.ds(b * NQ, NQ), :], acc[:]), "acc.kept")
        pr.leave()

    with nc.Fori(0, NB) as b:
        pr.enter("fin0", b, NB)
        wait("PE", "h.kept", of="moe0")
        wait("PE", "x", lag=1)
        done("PE", mm(bank[1][:], l0wo[:], H[:, bass.ds(b, 1), :].rearrange("p a n -> p (a n)")), "o")
        wait("DVE", "o")
        done("DVE", ts(s0[:, 0, :], bank[1][:], col(C_L0BO), None, ALU.add), "s")
        wait("PE", "s")
        for q in range(NQ):
            last = PE.transpose(bank[0][:, q * P:(q + 1) * P], s0[:, 0, q * P:(q + 1) * P], ident[:])
        done("PE", last, "sT")
        wait("ACT", "acc.kept", of="moe0")
        wait("ACT", "x", lag=1)
        done("ACT", A.activation(s0[:, 1, :], GT[:, bass.ds(b * NQ, NQ), :].rearrange("p q d -> p (q d)"), ACT.Silu),
             "sg")
        wait("DVE", "sT", "sg")
        done("DVE", tt(s0[:, 1, :], s0[:, 1, :], bank[0][:], ALU.mult), "sx")
        wait("DVE", "sx")
        xt = X[:, bass.ds(b * NQ, NQ), :].rearrange("p q d -> p (q d)")
        done("DVE", tt(xt, xt, s0[:, 1, :], ALU.add), "x")
        pr.leave()
    ph0.close()

    for e in ("PE", "DVE", "ACT", "POOL", "SP"):
        wait(e, "x", of="fin0")

    pr.dma("w1")
    pr.dma("w3")
    l1w = sb("l1w", [P, NE, T])
    l2w = sb("l2w", [P, NE * D])
    KS = [sb(f"KS{r}", [P, NG, T], F32R) for r in range(4)]
    QS = sb("QS", [P, NG, T], F32R)
    mats = {}
    shapes = {"l1_b": (P, 32), "l1_wp1": (P, P), "l1_wp2": (P, NE), "l1_wo": (P, D),
              "l1_bias": (P, 3 * NE), "l1_bp2": (P, NE),
              "l2_q": (P, 2 * D), "l2_k": (P, 64), "l2_v": (P, 32), "l2_gw": (P, NE), "l2_gb": (P, NQ * NE),
              "den": (P, P), "l3_rw": (P, NE), "c5": (P, 3 * P), "c1": (P, 3 * 64), "c4": (P, 64),
              "m1_in": (P, 2 * D), "m1_ssm": (P, 32), "m1_out": (P, D),
              "m2_in": (P, 2 * D), "m2_ssm": (P, 32), "m2_out": (P, D)}
    for n, s in shapes.items():
        mats[n] = sb(n, list(s))
        load(mats[n][:], a[n], "w1")
    l1c = sb("l1c", [32, D])
    load(l1c[:], a["l1_c"], "w1")
    l2eb = sb("l2eb", [NE, D])
    load(l2eb[:], a["l2_eb"], "w1")
    cosq = sb("cosq", [P, 2, T])
    cosk = sb("cosk", [32, 2, T])
    load(cosq[:], a["rope_q"].rearrange("p (c n) -> p c n", c=2), "w1")
    load(cosk[:], a["rope_k"].rearrange("p (c n) -> p c n", c=2), "w1")
    am = [sb(f"am{m}", [32, 2, 32]) for m in range(2)]
    for m in range(2):
        load(am[m][:], a[f"m{m + 1}_A"].rearrange("p (c n) -> p c n", c=2), "w1")
    wox = sb("wox", [P, NG, D])
    load(l1w[:], a["l1_w"], "w1")
    load(l2w[:], a["l2_w"], "w1")
    done("DVE", V.memset(wox[:], 0.0), "wox0")
    wait("SP", "wox0")
    for r in range(4):
        load(wox[32 * r:32 * r + HD, :, :], a["l2_wo"].rearrange("(g r j) o -> r j g o", g=NG, r=4)[r], "w1")
    load(WA[:], a["l3_wv"], "w3")
    load(WB[:], a["l3_w"], "w3")
    load(WC[:], a["l3_w1"], "w3")
    pr.names[(None, "w1")] = ("w1", pr.count["w1"])
    pr.names[(None, "w3")] = ("w3", pr.count["w3"])
    for e in ("PE", "DVE", "ACT", "POOL"):
        wait(e, "w1", of="start")

    fm = {n: sb(n, [P, T]) for n in ("sT", "t1", "t2", "t3", "gel0", "gel1", "u", "gs")}
    gt = xn
    sg = fm["t2"][:].rearrange("p (q d) -> p q d", q=NQ)
    abar = sb("abar", [32, 2])
    ab = sb("ab", [32, T])
    oh = sb("oh", [P, 40])
    b3 = sb("b3", [P, 3])
    hp = sb("hp", [P, 2])
    hpr = sb("hpr", [P, P])
    qhl = sb("qhl", [P, 2, T], F32R)
    khl = sb("khl", [32, 2, T], F32R)
    VA = sb("VA", [P, NQ, NG, 32])
    ex = sb("ex", [P, 2, 2, T])
    wsel = ex[:, 1, 0, :]
    o1, orec, xres = fm["gel0"], fm["gel1"], fm["t3"]
    qmax = sb("qmax", [P, NQ, HEADS])
    mrow = sb("mrow", [HEADS, T], F32R)
    w8 = sb("w8", [P, NQ, NE])
    w8T = sb("w8T", [NE, T])
    pad = sb("pad", [P, T + 4])
    cpad = sb("cpad", [P, T + 2])
    opad = pad[:, 2:T + 4]
    CH = T // 4
    hx = sb("hx", [P, CH])
    he = sb("he", [32, 2, CH + 1])
    hf = sb("hf", [P, CH])
    one = sb("one", [1, P])

    for r in range(4):
        V.memset(KS[r][:].bitcast(F32), 0.0)
    V.memset(QS[96:P, :, :].bitcast(F32), 0.0)
    V.memset(VA[:], 0.0)
    V.memset(pad[:], 0.0)
    V.memset(cpad[:], 0.0)
    V.memset(one[:], 1.0)
    V.memset(ab[:], 1.0)
    V.memset(fm["t1"][:], 1.0)
    done("DVE", V.memset(he[:], 0.0), "c0")
    wait("DVE", "c0")
    V.memset(VA[:, :, :, HD:HD + 1], 1.0)
    for r in range(4):
        for g in range(NG):
            last = ts(KS[r][96:P, g, :], fm["t1"][96:P, :], ident[96:P, 96 + r:97 + r], None, ALU.mult)
    done("DVE", last, "c1")
    wait("ACT", "c1")
    done("ACT", A.activation(abar[:, 0:1], col(C_L1A, 32), ACT.Exp), "ab0")
    wait("ACT", "ab0")
    done("ACT", A.activation(abar[:, 1:2], abar[:, 0:1], ACT.Exp, scale=-1.0), "ab1")
    wait("DVE", "ab1")
    done("DVE", ts(ab[:], ab[:], abar[:, 1:2], None, ALU.mult), "ab")

    NLV = 9
    pw = [sb(f"pw{m}", [32, NLV, 2, 32]) for m in range(2)]
    blk = [sb(f"blk{m}", [P, P]) for m in range(2)]
    car = [sb(f"car{m}", [32, P]) for m in range(2)]
    cst = [sb(f"cst{m}", [P, P]) for m in range(2)]
    for m in range(2):
        done("DVE", V.tensor_copy(pw[m][:, 0, :, :], am[m][:]), f"pw{m}.0")
        for k in range(1, NLV):
            wait("PE", f"pw{m}.{k - 1}")
            mm(bank[0][0:32, 0:32], pw[m][:, k - 1, 1, :], pw[m][:, k - 1, 0, :])
            done("PE", mm(bank[0][0:32, 32:64], pw[m][:, k - 1, 0, :], pw[m][:, k - 1, 1, :]), f"sq{m}.{k}")
            wait("DVE", f"sq{m}.{k}")
            done("DVE", V.tensor_copy(pw[m][:, k, :, :],
                                      bank[0][0:32, 0:64].rearrange("p (c n) -> p c n", c=2)), f"pw{m}.{k}")
        done("DVE", V.tensor_copy(car[m][:, 0:32], pw[m][:, 0, 1, :]), f"car{m}.0")
        for k in range(1, 4):
            wait("PE", f"car{m}.{k - 1}")
            done("PE", mm(bank[0][0:32, 0:32], pw[m][:, 0, 0, :], car[m][:, 32 * (k - 1):32 * k]), f"cm{m}.{k}")
            wait("DVE", f"cm{m}.{k}")
            done("DVE", V.tensor_copy(car[m][:, 32 * k:32 * k + 32], bank[0][0:32, 0:32]), f"car{m}.{k}")
        done("DVE", V.memset(blk[m][:], 0.0), f"blk{m}.0")
        wait("PE", f"car{m}.3")
        for s in range(4):
            for t in range(s, 4):
                src = ident[0:32, 0:32] if t == s else car[m][:, 32 * (t - s - 1):32 * (t - s)]
                last = mm(bank[1][32 * s:32 * s + 32, 32 * t:32 * t + 32], ident[0:32, 0:32], src)
        done("PE", last, f"bm{m}")
        wait("DVE", f"bm{m}", f"blk{m}.0")
        for s in range(4):
            V.tensor_copy(blk[m][32 * s:32 * s + 32, 32 * s:P], bank[1][32 * s:32 * s + 32, 32 * s:P])
        done("DVE", ts(cst[m][:], fm["t1"][:, 0:P], col(C_M[m] + C_CV), None, ALU.mult), f"cst{m}")
        wait("PE", f"cst{m}")

    sc = fm["t2"]
    pr.dma("sc")
    wait("PE", "c1", "w3", of="start")
    k = 0
    for wt, nm in ((WA, "l3_sv"), (WB, "l3_s"), (WC, "l3_s1")):
        for e in range(NE):
            if k:
                wait("SP", f"scb{k - 1}")
            load(sc[0:1, :], a[nm].rearrange("(o e) n -> o e n", o=1)[:, e, :], "sc")
            pr.names[(None, f"sc{k}")] = ("sc", pr.count["sc"])
            wait("PE", f"sc{k}")
            if k >= 2:
                wait("PE", f"scm{k - 2}")
            done("PE", mm(bank[k % 2][:], one[:], sc[0:1, :]), f"scb{k}")
            wait("DVE", f"scb{k}")
            done("DVE", tt(wt[:, e, :], wt[:, e, :], bank[k % 2][:], ALU.mult), f"scm{k}")
            k += 1
    for e in ("PE", "ACT", "POOL", "DVE", "SP"):
        wait(e, f"scm{k - 1}")

    pr.dma("st", 64 * 16)
    pr.dma("mr", 64 * 16)
    pr.dma("out", 64 * 16)
    M = mats

    def x_tiles(b):
        return X[:, bass.ds(b * NQ, NQ), :]

    def update_token(b, n, g_src, g_ready):
        wait("PE", f"{n}.s")
        for q in range(NQ):
            last = PE.transpose(bank[0][:, q * P:(q + 1) * P], fm["sT"][:, q * P:(q + 1) * P], ident[:])
        done("PE", last, f"{n}.st")
        wait("ACT", *g_ready)
        done("ACT", A.activation(sg, g_src, ACT.Silu), f"{n}.sg")
        wait("DVE", f"{n}.st", f"{n}.sg")
        done("DVE", tt(sg, sg, bank[0][:].rearrange("p (q d) -> p q d", q=NQ), ALU.mult), f"{n}.sx")
        wait("DVE", f"{n}.sx")
        done("DVE", tt(x_tiles(b), x_tiles(b), sg, ALU.add), f"{n}.x")
        wait("DVE", f"{n}.x")

    def mamba(m, n, src, src_ready, dst, dst_name):
        c = C_M[m]
        w_in, w_out, w_ssm = M[f"m{m + 1}_in"], M[f"m{m + 1}_out"], M[f"m{m + 1}_ssm"]
        wait("PE", *src_ready)
        done("PE", mm(bank[1][:], w_in[:, 0:D], src), f"{n}.xs")
        done("PE", mm(bank[2][:], w_in[:, D:2 * D], src), f"{n}.gate")
        wait("ACT", f"{n}.xs")
        done("ACT", A.activation(pad[:, 3:T + 3], bank[1][:], ACT.Identity, bias=col(c + C_INX)), f"{n}.pad")
        wait("ACT", f"{n}.gate")
        done("ACT", A.activation(fm["gs"][:], bank[2][:], ACT.Silu, bias=col(c + C_ING)), f"{n}.gs")
        wait("DVE", f"{n}.pad")
        done("DVE", ts(fm["t1"][:], pad[:, 0:T], col(c + C_CVW), None, ALU.mult), f"{n}.cv0")
        for j in range(1, 4):
            wait("DVE", f"{n}.cv{j - 1}")
            done("DVE", stt(fm["t1"][:], pad[:, j:j + T], col(c + C_CVW + j), fm["t1"][:], ALU.mult, ALU.add),
                 f"{n}.cv{j}")
        wait("ACT", f"{n}.cv3")
        done("ACT", A.activation(fm["u"][:], fm["t1"][:], ACT.Silu, bias=col(c + C_CVB)), f"{n}.u")
        wait("PE", f"{n}.u")
        uv = fm["u"][:].rearrange("p (c t) -> p t c", t=4)
        for t in range(4):
            last = mm(bank[3][32 * t:32 * t + 32, 0:CH], w_ssm[:], uv[:, t, :])
        done("PE", last, f"{n}.ssm")
        wait("DVE", f"{n}.ssm")
        done("DVE", ts(hx[:], bank[3][:, 0:CH], col(c + C_SSB), col(c + C_BV), ALU.add, ALU.mult), f"{n}.hx")
        wait("PE", f"{n}.hx")
        done("PE", mm(bank[3][0:32, P:2 * P], blk[m][:, 96:P], hx[:]), f"{n}.e")
        wait("DVE", f"{n}.e")
        done("DVE", V.tensor_copy(he[:, 0, 1:CH + 1], bank[3][0:32, P:2 * P]), f"{n}.he")
        cur = f"{n}.he"
        lv = 0
        while (1 << lv) < CH:
            o = 1 << lv
            wait("PE", cur, alone=True)
            done("PE", mm(bank[3][0:32, 2 * P:2 * P + CH - o], pw[m][:, lv + 2, 1, :],
                          he[:, lv % 2, 1:CH + 1 - o]), f"{n}.sh{lv}")
            wait("DVE", f"{n}.sh{lv}")
            V.tensor_copy(he[:, (lv + 1) % 2, 1:1 + o], he[:, lv % 2, 1:1 + o])
            done("DVE", tt(he[:, (lv + 1) % 2, 1 + o:CH + 1], he[:, lv % 2, 1 + o:CH + 1],
                           bank[3][0:32, 2 * P:2 * P + CH - o], ALU.add), f"{n}.he{lv}")
            cur = f"{n}.he{lv}"
            wait("DVE", cur)
            lv += 1
        wait("PE", cur)
        mm(bank[4][:, 0:CH], blk[m][:], hx[:], stop=False)
        done("PE", mm(bank[4][:, 0:CH], car[m][:], he[:, lv % 2, 0:CH], start=False), f"{n}.h")
        wait("DVE", f"{n}.h")
        done("DVE", V.tensor_copy(hf[:], bank[4][:, 0:CH]), f"{n}.hf")
        wait("PE", f"{n}.hf")
        cb = (5, 7, 1, 0)
        for t in range(4):
            last = mm(bank[cb[t]][:, 0:CH], cst[m][32 * t:32 * t + 32, :], hf[32 * t:32 * t + 32, :])
        done("PE", last, f"{n}.c")
        wait("DVE", f"{n}.c", f"{n}.u")
        for t in range(4):
            last = stt(fm["t1"][:].rearrange("p (c t) -> p t c", t=4)[:, t, :], bank[cb[t]][:, 0:CH],
                       col(c + C_DV), uv[:, t, :], ALU.add, ALU.mult)
        done("DVE", last, f"{n}.cu")
        wait("DVE", f"{n}.cu", f"{n}.gs")
        done("DVE", tt(fm["t1"][:], fm["t1"][:], fm["gs"][:], ALU.mult), f"{n}.y")
        wait("PE", f"{n}.y")
        done("PE", mm(bank[6][:], w_out[:], fm["t1"][:]), f"{n}.o")
        wait("DVE", f"{n}.o")
        done("DVE", stt(dst, bank[6][:], col(c + C_OB), src, ALU.add, ALU.add), dst_name)

    with nc.Fori(0, NB) as b:
        pr.enter("batch", b, NB)
        layer_norm(b, "n1")
        wait("PE", "n1.xf")
        done("PE", mm(bank[1][0:32, :], M["l1_b"][:], xf[:]), "l1.bx")
        wait("DVE", "l1.bx")
        done("DVE", V.tensor_tensor_scan(fm["t1"][0:32, :], ab[:], bank[1][0:32, :], 0.0, ALU.mult, ALU.add),
             "l1.h")
        wait("PE", "l1.h")
        done("PE", mm(bank[2][:], l1c[:], fm["t1"][0:32, :]), "l1.y")
        wait("DVE", "l1.y")
        done("DVE", stt(fm["sT"][:], xf[:], col(C_L1D), bank[2][:], ALU.mult, ALU.add), "l1.s")
        done("PE", mm(bank[3][:, 0:1], M["l1_wp1"][:], xf[:, T - 1:T]), "l1.p1")
        wait("ACT", "l1.p1")
        done("ACT", A.activation(hp[:, 0:1], bank[3][:, 0:1], ACT.Gelu, bias=col(C_BP1)), "l1.hp")
        wait("DVE", "l1.hp")
        done("DVE", V.tensor_copy(hpr[:], hp[:, 0:1].to_broadcast([P, P])), "l1.hpr")
        wait("PE", "l1.hpr")
        done("PE", mm(bank[3][:, 8:8 + NE], hpr[:], M["l1_wp2"][:]), "l1.p2")
        wait("DVE", "l1.p2")
        done("DVE", tt(oh[:, 0:8], bank[3][:, 8:8 + NE], M["l1_bp2"][:], ALU.add), "l1.lg")
        wait("DVE", "l1.lg", alone=True)
        done("DVE", V.max(oh[:, 8:16], oh[:, 0:8]), "l1.mx")
        wait("DVE", "l1.mx", alone=True)
        done("DVE", V.max_index(ix[:, 0, :], oh[:, 8:16], oh[:, 0:8]), "l1.ix")
        wait("DVE", "l1.ix")
        done("DVE", V.tensor_copy(oh[:, 16:17], ix[:, 0, 0:1]), "l1.ixf")
        wait("DVE", "l1.ixf")
        done("DVE", ts(oh[:, 24:32], iota[:, 0, :], oh[:, 16:17], None, ALU.is_equal), "l1.oh")
        wait("DVE", "l1.oh")
        done("DVE", ts(wsel, l1w[:, 0, :], oh[:, 24:25], None, ALU.mult), "l1.w0")
        for e in range(1, NE):
            wait("DVE", f"l1.w{e - 1}")
            done("DVE", stt(wsel, l1w[:, e, :], oh[:, 24 + e:25 + e], wsel, ALU.mult, ALU.add), f"l1.w{e}")
        bt = fm["t2"][:, 0:3 * NE].rearrange("p (c e) -> p c e", c=3)
        done("DVE", tt(bt, M["l1_bias"][:].rearrange("p (c e) -> p c e", c=3),
                       oh[:, 24:32].unsqueeze(1).to_broadcast([P, 3, NE]), ALU.mult), "l1.bt")
        wait("DVE", "l1.bt")
        done("DVE", V.tensor_reduce(b3[:], bt, AX_X, ALU.add), "l1.b3")
        wait("PE", f"l1.w{NE - 1}")
        for m in range(2):
            last = mm(bank[4 + m][:], wsel[:, m * P:(m + 1) * P], xf[:])
        done("PE", last, "l1.f1")
        wait("ACT", "l1.f1", "l1.b3")
        for m in range(2):
            last = A.activation(fm[f"gel{m}"][:], bank[4 + m][:], ACT.Gelu, bias=b3[:, m:m + 1])
        done("ACT", last, "l1.g")
        wait("PE", "l1.g")
        for m in range(2):
            last = mm(bank[6][:], wsel[:, 256 + m * P:256 + (m + 1) * P], fm[f"gel{m}"][:],
                      start=(m == 0), stop=(m == 1))
        done("PE", last, "l1.f2")
        wait("DVE", "l1.f2")
        done("DVE", ts(fm["t1"][:], bank[6][:], b3[:, 2:3], None, ALU.add), "l1.r")
        wait("PE", "l1.r")
        done("PE", mm(bank[7][:], M["l1_wo"][:], fm["t1"][:]), "l1.f3")
        wait("DVE", "l1.f3")
        done("DVE", ts(fm["t1"][:], bank[7][:], col(C_L1BO), 0.3, ALU.add, ALU.mult), "l1.f4")
        wait("DVE", "l1.f4")
        done("DVE", tt(fm["t1"][:], fm["t1"][:], xf[:], ALU.add), "l1.f5")
        wait("ACT", "l1.f5")
        done("ACT", A.activation(fm["t1"][:], fm["t1"][:], ACT.Silu), "l1.sg")
        wait("DVE", "l1.sg", "l1.s")
        done("DVE", tt(fm["sT"][:], fm["sT"][:], fm["t1"][:], ALU.mult), "l1.p")
        wait("PE", "l1.p")
        for q in range(NQ):
            last = PE.transpose(bank[0][:, q * P:(q + 1) * P], fm["sT"][:, q * P:(q + 1) * P], ident[:])
        done("PE", last, "l1.pT")
        wait("DVE", "l1.pT")
        done("DVE", tt(x_tiles(b), x_tiles(b), bank[0][:].rearrange("p (q d) -> p q d", q=NQ), ALU.add), "l1.x")
        wait("DVE", "l1.x")

        layer_norm(b, "n2")
        wait("PE", "n2.xf")
        mm(bank[1][:], M["l2_q"][:, 0:D], xf[:])
        done("PE", mm(bank[2][:], M["l2_q"][:, D:2 * D], xf[:]), "l2.q")
        mm(bank[3][0:32, :], M["l2_k"][:, 0:32], xf[:])
        done("PE", mm(bank[4][0:32, :], M["l2_k"][:, 32:64], xf[:]), "l2.k")
        for q in range(NQ):
            last = mm(bank[5][:, q * 32:(q + 1) * 32], xf[:, q * P:(q + 1) * P], M["l2_v"][:])
        done("PE", last, "l2.v")
        for nm, b1, b2, w, tab, n in (("q", 1, 2, qhl, cosq, P), ("k", 3, 4, khl, cosk, 32)):
            wait("DVE", f"l2.{nm}")
            tt(fm["t1"][0:n, :], bank[b1][0:n, :], tab[:, 0, :], ALU.mult)
            done("DVE", tt(fm["t2"][0:n, :], bank[b2][0:n, :], tab[:, 1, :], ALU.mult), f"l2.{nm}1")
            wait("DVE", f"l2.{nm}1")
            done("DVE", tt(fm["t3"][0:n, :], fm["t1"][0:n, :], fm["t2"][0:n, :], ALU.add), f"l2.{nm}2")
            wait("DVE", f"l2.{nm}2")
            done("DVE", V.tensor_copy(w[:, 0, :], fm["t3"][0:n, :]), f"l2.{nm}3")
            wait("DVE", f"l2.{nm}3")
            done("DVE", tt(w[:, 1, :], fm["t3"][0:n, :], w[:, 0, :].bitcast(F32), ALU.subtract), f"l2.{nm}hl")
            wait("DVE", f"l2.{nm}hl")
        wait("DVE", "l2.v")
        done("DVE", V.tensor_copy(VA[:, :, :, 0:HD],
                                  bank[5][:, 0:P].rearrange("p (q g d) -> p q g d", q=NQ, g=NG)), "l2.va")
        wait("DVE", "l2.va")
        wait("SP", "l2.qhl", "l2.khl")
        for p, c in ((0, 0), (1, 1), (2, 0)):
            for g in range(NG):
                done("st", S.dma_start(QS[32 * p:32 * p + 32, g, :].bitcast(F32),
                                        qhl[32 * g:32 * g + 32, c, :].bitcast(F32)), by=16)
        for p, c in ((0, 0), (1, 0), (2, 1)):
            for r in range(4):
                for g in range(NG):
                    w = dict(by=16)
                    if (p, r, g) == (2, 3, NG - 1):
                        w["name"] = "l2.stacked"
                    done("st", S.dma_start(KS[r][32 * p + HD * r:32 * p + HD * (r + 1), g, :].bitcast(F32),
                                           khl[HD * g:HD * (g + 1), c, :].bitcast(F32)), **w)
        wait("PE", "l2.stacked")
        n = 0
        for g in range(NG):
            for r in range(4):
                for q in range(NQ):
                    k = n % 4
                    if n >= 4:
                        wait("PE", f"l2.mx{n - 4}")
                    else:
                        wait("PE", "l2.q1", "l2.k1")
                    done("PE", mm(bank[k + 1][:], QS[0:96, g, q * P:(q + 1) * P], KS[r][0:96, g, :]), f"l2.sc{n}")
                    wait("DVE", f"l2.sc{n}")
                    done("DVE", V.tensor_reduce(qmax[:, q, 4 * g + r:4 * g + r + 1], bank[k + 1][:], AX_X, ALU.max),
                         f"l2.mx{n}")
                    n += 1
        wait("PE", f"l2.mx{n - 1}")
        for q in range(NQ):
            last = PE.transpose(bank[0][0:HEADS, q * P:(q + 1) * P], qmax[:, q, :], ident[:])
        done("PE", last, "l2.mT")
        wait("DVE", "l2.mT")
        done("DVE", ts(mrow[:], bank[0][0:HEADS, :], -1.0, None, ALU.mult), "l2.mrow")
        wait("SP", "l2.mrow")
        for g in range(NG):
            done("mr", S.dma_start(QS[96:100, g, :].bitcast(F32), mrow[4 * g:4 * g + 4, :].bitcast(F32)), **(
                dict(by=16) if g < NG - 1 else dict(by=16, name="l2.mrows")))
        wait("PE", "l2.mrows", "l2.va")
        n = 0
        for g in range(NG):
            for r in range(4):
                for kh in range(2):
                    c = n % 2
                    if n >= 2:
                        wait("PE", f"l2.ex{n - 2}")
                    for j in range(2):
                        last = mm(bank[1 + 2 * c + j][:], KS[r][:, g, (2 * kh + j) * P:(2 * kh + j + 1) * P],
                                  QS[:, g, :])
                    done("PE", last, f"l2.se{n}")
                    wait("ACT", f"l2.se{n}")
                    if n >= 2:
                        wait("ACT", f"l2.pv{n - 2}")
                    for j in range(2):
                        last = A.activation(ex[:, c, j, :], bank[1 + 2 * c + j][:], ACT.Exp, scale=SM_SCALE)
                    done("ACT", last, f"l2.ex{n}")
                    wait("PE", f"l2.ex{n}")
                    if r == 0 and kh == 0 and g >= 1:
                        wait("PE", f"l2.o{g - 1}")
                    for j in range(2):
                        last = mm(bank[5][32 * r:32 * r + 32, :], VA[:, 2 * kh + j, g, :], ex[:, c, j, :],
                                  start=(kh == 0 and j == 0), stop=(kh == 1 and j == 1))
                    done("PE", last, f"l2.pv{n}")
                    n += 1
            wait("ACT", f"l2.pv{n - 1}")
            if g >= 1:
                wait("ACT", f"l2.on{g - 1}")
            done("ACT", A.copy(o1[:], bank[5][:]), f"l2.o{g}")
            wait("PE", f"l2.o{g}")
            done("PE", mm(bank[6][:], M["den"][:], o1[:]), f"l2.d{g}")
            wait("DVE", f"l2.d{g}")
            done("DVE", V.reciprocal(orec[:], bank[6][:]), f"l2.rec{g}")
            wait("DVE", f"l2.rec{g}")
            if g >= 1:
                wait("DVE", f"l2.wo{g - 1}")
            done("DVE", tt(fm["t3"][:], o1[:], orec[:], ALU.mult), f"l2.on{g}")
            wait("PE", f"l2.on{g}")
            done("PE", mm(bank[7][:], wox[:, g, :], fm["t3"][:], start=(g == 0), stop=(g == NG - 1)), f"l2.wo{g}")
        wait("DVE", f"l2.wo{NG - 1}")
        done("DVE", V.tensor_copy(fm["sT"][:], bank[7][:]), "l2.s")
        for q in range(NQ):
            last = mm(bank[1][:, q * NE:(q + 1) * NE], xf[:, q * P:(q + 1) * P], M["l2_gw"][:])
        done("PE", last, "r2.logits")
        top_two("r2", "masked", bias=M["l2_gb"][:].rearrange("p (q e) -> p q e", q=NQ), dst=w8[:])
        wait("PE", "r2.w")
        for q in range(NQ):
            last = PE.transpose(bank[2][0:NE, q * P:(q + 1) * P], w8[:, q, :], ident[:])
        done("PE", last, "l2.w8T")
        wait("DVE", "l2.w8T")
        done("DVE", V.tensor_copy(w8T[:], bank[2][0:NE, :]), "l2.w8")
        wait("PE", "l2.w8")
        for q in range(NQ):
            last = mm(bank[3][:, q * D:(q + 1) * D], w8T[:, q * P:(q + 1) * P], l2eb[:])
        done("PE", last, "l2.eb")
        wait("DVE", "l2.eb")
        done("DVE", V.tensor_copy(gt[:], bank[3][:].rearrange("p (q d) -> p q d", q=NQ)), "l2.gt")
        wait("DVE", "l2.gt")
        for q in range(NQ):
            for h in range(2):
                k = 2 * q + h
                if k >= 4:
                    wait("PE", f"l2.a{k - 4}.3")
                done("PE", mm(bank[4 + k % 4][:], xf[:, q * P:(q + 1) * P], l2w[:, h * T:(h + 1) * T]), f"l2.e{k}")
                wait("DVE", f"l2.e{k}")
                for e in range(4):
                    if e:
                        wait("DVE", f"l2.a{k}.{e - 1}")
                    done("DVE", stt(gt[:, q, :], bank[4 + k % 4][:, e * D:(e + 1) * D],
                                    w8[:, q, 4 * h + e:4 * h + e + 1], gt[:, q, :], ALU.mult, ALU.add),
                         f"l2.a{k}.{e}")
                wait("DVE", f"l2.a{k}.3")
        update_token(b, "l2", gt[:], ("l2.a7.3",))

        layer_norm(b, "n3")
        mamba(0, "ma", xf[:], ("n3.xf",), xres[:], "ma.x")
        wait("DVE", "ma.x")
        mamba(1, "mb", xres[:], ("ma.x",), cpad[:, 1:T + 1], "mb.x")
        wait("PE", "mb.x")
        for j in range(3):
            last = mm(bank[1][0:64, :], M["c1"][:, 64 * j:64 * j + 64], cpad[:, j:j + T],
                      start=(j == 0), stop=(j == 2))
        done("PE", mm(bank[1][64:P, :], M["c4"][:], cpad[:, 1:T + 1]), "l3.c14")
        wait("DVE", "l3.c14")
        done("DVE", ts(fm["t1"][:], bank[1][:], col(C_C1B), 0.0, ALU.add, ALU.max), "l3.relu")
        wait("DVE", "l3.relu")
        ts(opad[0:64, 1:T + 1], fm["t1"][0:64, :], BN_SCALE, None, ALU.mult)
        done("DVE", V.tensor_copy(opad[64:P, 1:T + 1], fm["t1"][64:P, :]), "l3.oc")
        wait("PE", "l3.oc")
        for j in range(3):
            last = mm(bank[2][:], M["c5"][:, P * j:P * j + P], opad[:, j:j + T], start=(j == 0), stop=(j == 2))
        done("PE", last, "l3.c5")
        wait("DVE", "l3.c5")
        done("DVE", ts(fm["t1"][:], bank[2][:], 0.0, BN_SCALE, ALU.max, ALU.mult), "l3.o5")
        wait("DVE", "l3.o5")
        done("DVE", tt(fm["sT"][:], fm["t1"][:], cpad[:, 1:T + 1], ALU.add), "l3.s")
        for q in range(NQ):
            last = mm(bank[1][:, q * NE:(q + 1) * NE], xf[:, q * P:(q + 1) * P], M["l3_rw"][:])
        done("PE", last, "r3.logits")
        top_two("r3", "probs", dst=w8[:])
        wait("DVE", "r3.w")
        vy = [fm["gel0"], fm["gel1"], fm["u"], fm["gs"]]
        n = 0
        for e in range(NE):
            for m in range(HC):
                c = n % 2
                if n >= 2:
                    wait("PE", f"l3.vy{n - 2}")
                else:
                    wait("PE", "r3.lg")
                mm(bank[1 + 2 * c][:], WA[:, e, m * P:(m + 1) * P], xf[:])
                done("PE", mm(bank[2 + 2 * c][:], WB[:, e, m * P:(m + 1) * P], xf[:]), f"l3.vw{n}")
                wait("ACT", f"l3.vw{n}")
                if n >= 2:
                    wait("ACT", f"l3.vy{n - 2}")
                done("ACT", A.activation(ex[:, c, 0, :], bank[2 + 2 * c][:], ACT.Gelu_apprx_tanh), f"l3.ge{n}")
                wait("DVE", f"l3.ge{n}")
                if e and m == 0:
                    wait("DVE", f"l3.y{e - 1}")
                done("DVE", tt(vy[m][:], ex[:, c, 0, :], bank[1 + 2 * c][:], ALU.mult), f"l3.vy{n}")
                n += 1
            wait("PE", f"l3.vy{n - 1}")
            if e >= 2:
                wait("PE", f"l3.a{e - 2}")
            for q in range(NQ):
                for m in range(HC):
                    last = mm(bank[5 + e % 2][:, q * D:(q + 1) * D], vy[m][:, q * P:(q + 1) * P],
                              WC[:, e, m * D:(m + 1) * D], start=(m == 0), stop=(m == HC - 1))
            done("PE", last, f"l3.y{e}")
            wait("DVE", f"l3.y{e}")
            if e:
                wait("DVE", f"l3.a{e - 1}")
            for q in range(NQ):
                ys = bank[5 + e % 2][:, q * D:(q + 1) * D]
                if e == 0:
                    last = ts(gt[:, q, :], ys, w8[:, q, e:e + 1], None, ALU.mult)
                else:
                    last = stt(gt[:, q, :], ys, w8[:, q, e:e + 1], gt[:, q, :], ALU.mult, ALU.add)
            done("DVE", last, f"l3.a{e}")
        update_token(b, "l3", gt[:], (f"l3.a{NE - 1}",))
        wait("SP", "l3.x")
        done("out", S.dma_start(out[bass.ds(b, 1)].rearrange("a (q p) d -> p (a q) d", p=P), x_tiles(b)),
             "out", by=16)
        pr.leave()
    wait("SP", "out", of="batch")
    ctx.close()
    return pr


_OUT_SHAPE = (NB, T, D)


def _rope():
    inv = (1.0 / np.float32(10000.0) ** (np.arange(0, D, 2, dtype=np.float32) / np.float32(D))).astype(np.float32)
    ang = (np.arange(T, dtype=np.float32)[:, None] * inv[None, :]).astype(np.float32)
    cos, sin = np.cos(ang).T, np.sin(ang).T
    c = np.repeat(cos, 2, axis=0)
    s = np.stack([-sin, sin], axis=1).reshape(D, T)
    ck, sk = np.concatenate([c[0:HD]] * NG), np.concatenate([s[0:HD]] * NG)
    return (np.concatenate([c, s], axis=1).astype(np.float32), np.concatenate([ck, sk], axis=1).astype(np.float32))


def _lay_out(i):
    t = np.ascontiguousarray
    swap = np.arange(D).reshape(-1, 2)[:, ::-1].reshape(-1)
    swk = np.arange(32).reshape(-1, 2)[:, ::-1].reshape(-1)
    z = np.zeros(P, np.float32)
    a = {"x": i["L0_attn_x"], "l0_wo": t(i["L0_attn_Wo"].T), "l0_bw": t(i["L0_attn_B_w"].T),
         "l0_rw": t(i["L0_ffn_router_w"].T)}
    cols = [i["L0_attn_A"], i["L0_attn_bo"], np.tile(i["L1_attn_A"], 4), i["L1_attn_D"], i["L1_ffn_bp1"],
            i["L1_ffn_bo"], np.concatenate([i["L3_attn_c1_b"], z[0:64]]), z]
    for m in ("m1", "m2"):
        g = lambda n: i[f"L3_attn_{m}_{n}"]
        cols += [g("in_b")[0:D], g("in_b")[D:], g("conv_b")] + [g("conv_w")[:, 0, k] for k in range(4)]
        cols += [np.tile(g("ssm_b"), 4), np.tile(g("B"), 4), g("D"), g("out_b"), np.tile(g("C"), 4)]
        a[f"{m}_in"], a[f"{m}_ssm"], a[f"{m}_out"] = g("in_w"), g("ssm_w"), g("out_w")
        a[f"{m}_A"] = np.concatenate([g("A"), g("A").T], axis=1)
    a["cv"] = np.stack(cols, axis=1)
    a["ident"] = np.eye(P, dtype=np.float32)
    a["iota"] = np.tile(np.arange(NE, dtype=np.float32), (P, NQ))
    den = np.zeros((P, P), np.float32)
    for r in range(4):
        den[32 * r + HD, 32 * r:32 * r + 32] = 1.0
    a["den"] = den
    a["l0_w1"] = i["L0_ffn_w1"].transpose(1, 0, 2)
    a["l0_w2"] = i["L0_ffn_w2"].reshape(NE, HC, P, D).transpose(2, 0, 1, 3).reshape(P, NE, T)
    a["l1_b"], a["l1_c"] = i["L1_attn_B"].T, i["L1_attn_C"].T
    a["l1_wp1"], a["l1_wp2"], a["l1_wo"] = i["L1_ffn_Wp1"], i["L1_ffn_Wp2"], i["L1_ffn_Wo"]
    a["l1_bp2"] = np.tile(i["L1_ffn_bp2"], (P, 1))
    b1 = i["L1_ffn_b1"].reshape(NE, 2, P).transpose(2, 1, 0)
    a["l1_bias"] = np.concatenate([b1, i["L1_ffn_b2"].T[:, None, :]], axis=1).reshape(P, 3 * NE)
    w2 = i["L1_ffn_W2"].reshape(NE, 2, P, D).transpose(2, 0, 1, 3).reshape(P, NE, 2 * D)
    a["l1_w"] = np.concatenate([i["L1_ffn_W1"].transpose(1, 0, 2), w2], axis=2)
    a["l2_q"] = np.concatenate([i["L2_attn_Wq"], i["L2_attn_Wq"][:, swap]], axis=1)
    a["l2_k"] = np.concatenate([i["L2_attn_Wk"], i["L2_attn_Wk"][:, swk]], axis=1)
    a["l2_v"], a["l2_wo"] = i["L2_attn_Wv"], i["L2_attn_Wo"]
    a["l2_gw"], a["l2_gb"] = i["L2_ffn_gate_w"].T, np.tile(i["L2_ffn_gate_b"], (P, NQ))
    a["l2_w"], a["l2_eb"] = i["L2_ffn_expert_w"].transpose(1, 0, 2).reshape(P, NE * D), i["L2_ffn_expert_b"]
    a["rope_q"], a["rope_k"] = _rope()
    a["c1"] = i["L3_attn_c1_w"].transpose(1, 2, 0).reshape(P, 3 * 64)
    a["c4"] = i["L3_attn_c4_w"][:, :, 0].T
    a["c5"] = i["L3_attn_c5_w"].transpose(1, 2, 0).reshape(P, 3 * P)
    a["l3_rw"] = i["L3_ffn_router_w"]
    a["l3_wv"], a["l3_w"] = i["L3_ffn_wv"].transpose(1, 0, 2), i["L3_ffn_w"].transpose(1, 0, 2)
    a["l3_w1"] = i["L3_ffn_w1"].reshape(NE, HC, P, D).transpose(2, 0, 1, 3).reshape(P, NE, T)
    a["l3_sv"], a["l3_s"] = i["L3_ffn_sv"][:, 0, :], i["L3_ffn_s"][:, 0, :]
    a["l3_s1"] = np.tile(i["L3_ffn_s1"][:, 0, :], (1, HC))
    return {n: t(v) for n, v in a.items()}


def kernel(**inputs):
    import concourse.bacc as bacc
    from concourse.bass_utils import run_bass_kernel_spmd

    arrays = _lay_out({n: np.asarray(v) for n, v in inputs.items()})
    known = None
    for _ in range(2):
        nc = bacc.Bacc("TRN2", target_bir_lowering=False, num_devices=1)
        aps = {n: nc.dram_tensor(f"in_{n}", v.shape, F32, kind="ExternalInput").ap() for n, v in arrays.items()}
        out = nc.dram_tensor("out", _OUT_SHAPE, F32, kind="ExternalOutput").ap()
        pr = build(nc, known, aps, out)
        known = (pr.names, pr.loops)
    r = run_bass_kernel_spmd(nc, [{f"in_{n}": v for n, v in arrays.items()}], core_ids=[0])
    return r.results[0]["out"]
```

```python
from contextlib import ExitStack

import numpy as np
import concourse.bass as bass
from concourse import mybir

ALU = mybir.AluOpType
ACT = mybir.ActivationFunctionType
AX_X = mybir.AxisListType.X
F32 = mybir.dt.float32
F32R = mybir.dt.float32r
U32 = mybir.dt.uint32

P = 128
NB, T, D = 8, 512, 128
NQ = T // P
NE = 8
HC = 4
HEADS, HD, NG = 16, 8, 4
LN_EPS = 1e-5
SM_SCALE = float(1.0 / np.sqrt(np.float32(D)))
BN_SCALE = float(1.0 / np.float32(np.sqrt(1.0 + 1e-5)))
CREDIT = 2000
STEPS = T // NB

C_L0A, C_L0BO, C_L1A, C_L1D, C_BP1, C_L1BO, C_C1B = range(7)
C_INX, C_ING, C_CVB, C_CVW, C_SSB, C_BV, C_DV, C_OB, C_CV = 0, 1, 2, 3, 7, 8, 9, 10, 11
C_M = (8, 20)
NCV = 32


class Progress:

    def __init__(self, nc, ctx, known):
        self.eng = {"PE": nc.tensor, "DVE": nc.vector, "ACT": nc.scalar, "POOL": nc.gpsimd, "SP": nc.sync}
        self.nc, self.ctx, self.known = nc, ctx, known
        self.sem, self.count = {}, {}
        for e in ("PE", "DVE", "ACT", "POOL"):
            self.sem[e] = ctx.enter_context(nc.semaphore(f"progress_{e}"))
            self.count[e] = CREDIT
            self.eng[e].sem_inc(self.sem[e], CREDIT)
        self.names, self.loops = {}, {}
        self.loop, self.seen, self.stream = None, {}, None

    def dma(self, name, credit=0):
        self.sem[name] = self.ctx.enter_context(self.nc.semaphore(f"dma_{name}"))
        self.count[name] = credit
        if credit:
            self.nc.sync.sem_inc(self.sem[name], credit)

    def enter(self, name, i, n):
        self.loop, self.i, self.n, self.seen = name, i, n, {}
        self.base = dict(self.count)

    def leave(self):
        for e in self.count:
            per = self.count[e] - self.base[e]
            self.loops[(self.loop, e)] = (self.base[e], per, self.n)
            self.count[e] = self.base[e] + per * self.n
            self.names[(None, f"{self.loop} ended on {e}")] = (e, self.count[e])
        self.loop, self.seen = None, {}

    def fence(self, loop):
        for e in self.eng:
            self.wait(e, *[f"{loop} ended on {c}" for c in ("PE", "DVE", "ACT", "POOL")], of="start")

    def interleave(self, *streams):
        live = [g if isinstance(g, tuple) else (k, g) for k, g in enumerate(streams)]
        while live:
            for k, g in list(live):
                self.stream = k
                if next(g, self) is self:
                    live.remove((k, g))
        self.stream = None

    def done(self, chan, instr, name=None, by=1):
        instr.then_inc(self.sem[chan], by)
        self.count[chan] += by
        if name and self.stream is not None:
            name = f"{self.stream}:{name}"
        if name:
            assert (self.loop, name) not in self.names, name
            self.names[(self.loop, name)] = (chan, self.count[chan] - (self.base[chan] if self.loop else 0))

    def wait(self, engine, *names, lag=0, of=None, alone=False):
        if not self.known:
            return
        names_of, loops = self.known
        loop = of if of is not None else self.loop
        if loop == "start":
            loop = None
        need = {}
        for name in names:
            if self.stream is not None and of is None:
                name = f"{self.stream}:{name}"
            chan, k = names_of[(loop, name)]
            need[chan] = max(need.get(chan, 0), k)
        for chan, k in need.items():
            key = (engine, chan, loop, lag)
            if self.seen.get(key, -1) >= k:
                continue
            self.seen[key] = k
            value = k
            if loop:
                base, per, n = loops[(loop, chan)]
                if loop == self.loop:
                    value = self.i * per + (base + k - lag * per)
                else:
                    value = base + (n - 1) * per + k
            self.eng[engine].wait_ge(self.sem[chan], value)
            if alone:
                self.eng[engine].sem_inc(self.sem["aside"], 1)


def build(nc, known, a, out):
    V, A, PE, G, S = nc.vector, nc.scalar, nc.tensor, nc.gpsimd, nc.sync
    ctx = ExitStack()
    pr = Progress(nc, ctx, known)
    done, wait = pr.done, pr.wait
    pr.dma("aside")

    def sb(name, shape, dt=F32, c=ctx):
        return c.enter_context(nc.sbuf_tensor(name, shape, dt))

    bank = [ctx.enter_context(nc.psum_tensor(f"bank{i}", [P, T], F32)) for i in range(8)]

    def tt(o, x, y, op):
        return V.tensor_tensor(o, x, y, op)

    def ts(o, x, s1, s2, op0, op1=None):
        return V.tensor_scalar(o, x, s1, s2, op0, op1) if op1 is not None else V.tensor_scalar(o, x, s1, s2, op0)

    def stt(o, x, s, y, op0, op1):
        return V.scalar_tensor_tensor(out=o, in0=x, scalar=s, in1=y, op0=op0, op1=op1)

    def mm(o, l, r, start=True, stop=True):
        return PE.matmul(o, l, r, start=start, stop=stop)

    def load(dst, src, name):
        done(name, S.dma_start(dst, src), by=16)

    X = sb("X", [P, NB * NQ, D])
    XNT = sb("XNT", [P, NB, T])
    ST = sb("ST", [P, NB, T])
    cv = sb("cv", [P, NCV])
    ident = sb("ident", [P, P])
    iota = sb("iota", [P, NQ, NE])
    expo = sb("expo", [P, NQ])
    wox = sb("wox", [P, NG, D])
    M = {}
    shapes = {"l0_bw": (P, D), "l0_rw": (P, NE), "l0_wo": (P, D),
              "l1_b": (P, 32), "l1_wp1": (P, P), "l1_wp2": (P, NE), "l1_wo": (P, D), "l1_c": (32, D),
              "l1_bias": (P, 3 * NE), "l1_bp2": (P, NE),
              "l2_q": (P, 2 * D), "l2_k": (P, 64), "l2_v": (P, 32), "l2_gw": (P, NE), "l2_gb": (P, NQ * NE),
              "l2_eb": (NE, D), "l2_w": (P, NE * D),
              "den": (P, P), "l3_rw": (P, NE), "c5": (P, 3 * P), "c1": (P, 3 * 64), "c4": (P, 64),
              "m1_in": (P, 2 * D), "m1_ssm": (P, 32), "m1_out": (P, D), "m1_A": (32, 64),
              "m2_in": (P, 2 * D), "m2_ssm": (P, 32), "m2_out": (P, D), "m2_A": (32, 64)}
    for n, s in shapes.items():
        M[n] = sb(n, list(s))

    def col(c, n=P):
        return cv[0:n, c:c + 1]

    def flat(ap):
        return ap.rearrange("p a n -> p (a n)")

    pr.dma("in")
    load(X[:], a["x"].rearrange("b (q p) d -> p (b q) d", p=P), "in")
    load(cv[:], a["cv"], "in")
    load(ident[:], a["ident"], "in")
    load(iota[:], a["iota"].rearrange("p (q e) -> p q e", q=NQ), "in")
    for n in ("l0_bw", "l0_rw", "l0_wo"):
        load(M[n][:], a[n], "in")
    pr.names[(None, "in")] = ("in", pr.count["in"])

    def working(c, tag, names, ways):
        sets = []
        for k in range(ways):
            w = {n: sb(f"{n}_{k}_{tag}", [P, T], c=c) for n in names}
            for n, s in {"st": [P, NQ, 6], "mv": [P, NQ, 2], "rstd": [P, 2, NQ], "xn": [P, NQ, D], "xf": [P, T],
                         "lg": [P, NQ, NE], "mx": [P, NQ, 8], "ixf": [P, NQ, 2], "sel": [P, NQ, NE],
                         "sel2": [P, NQ, NE], "ee": [P, NQ, NE], "zz": [P, 4, NQ], "w8": [P, NQ, NE]}.items():
                w[n] = sb(f"{n}_{k}_{tag}", s, c=c)
            w["ix"] = sb(f"ix_{k}_{tag}", [P, NQ, 8], U32, c=c)
            w["B"] = bank[8 // ways * k:8 // ways * (k + 1)]
            sets.append(w)
        return sets

    def layer_norm(w, b, n, keep=None):
        V.sem_inc(pr.sem["aside"], 1)
        for q in range(NQ):
            last = V.bn_stats(w["st"][:, q, :], flat(X[:, bass.ds(b * NQ + q, 1), :]))
        done("DVE", last, f"{n}.stats")
        wait("DVE", f"{n}.stats", alone=True)
        for q in range(NQ):
            last = V.bn_aggr(w["mv"][:, q, :], w["st"][:, q, :])
        done("DVE", last, f"{n}.aggr")
        wait("POOL", f"{n}.aggr", alone=True)
        done("POOL", G.tensor_scalar(w["rstd"][:, 0, :], w["mv"][:, :, 1], LN_EPS, None, ALU.add), f"{n}.var")
        wait("POOL", f"{n}.var", alone=True)
        done("POOL", G.tensor_tensor(w["rstd"][:, 1, :], w["rstd"][:, 0, :], expo[:], ALU.pow), f"{n}.rstd")
        yield
        wait("DVE", f"{n}.rstd")
        for q in range(NQ):
            last = ts(w["xn"][:, q, :], flat(X[:, bass.ds(b * NQ + q, 1), :]),
                      w["mv"][:, q, 0:1], w["rstd"][:, 1, q:q + 1], ALU.subtract, ALU.mult)
        done("DVE", last, f"{n}.xn")
        wait("PE", f"{n}.xn")
        for q in range(NQ):
            last = PE.transpose(w["B"][0][:, q * P:(q + 1) * P], w["xn"][:, q, :], ident[:])
        done("PE", last, f"{n}.xnT")
        wait("ACT", f"{n}.xnT")
        done("ACT", A.copy(w["xf"][:], w["B"][0][:]), f"{n}.xf")
        if keep is not None:
            wait("POOL", f"{n}.xf")
            done("POOL", G.tensor_copy(flat(keep[:, bass.ds(b, 1), :]), w["xf"][:]), f"{n}.kept")
        yield

    def top_two(w, n, kind, lhs, weights, bias=None, dst=None):
        for q in range(NQ):
            last = mm(w["B"][1][:, q * NE:(q + 1) * NE], lhs(q), weights)
        done("PE", last, f"{n}.logits")
        wait("DVE", f"{n}.logits")
        src = w["B"][1][:, 0:NQ * NE].rearrange("p (q e) -> p q e", q=NQ)
        if bias is None:
            done("DVE", V.tensor_copy(w["lg"][:], src), f"{n}.lg")
        else:
            done("DVE", tt(w["lg"][:], src, bias, ALU.add), f"{n}.lg")
        yield
        wait("DVE", f"{n}.lg", alone=True)
        for q in range(NQ):
            last = V.max(w["mx"][:, q, :], w["lg"][:, q, :])
        done("DVE", last, f"{n}.mx")
        yield
        wait("DVE", f"{n}.mx", alone=True)
        for q in range(NQ):
            last = V.max_index(w["ix"][:, q, :], w["mx"][:, q, :], w["lg"][:, q, :])
        done("DVE", last, f"{n}.ix")
        ee, sel, sel2, zz = w["ee"], w["sel"], w["sel2"], w["zz"]
        done("DVE", tt(ee[:], w["lg"][:], w["mx"][:, :, 0:1].to_broadcast([P, NQ, NE]), ALU.subtract), f"{n}.shift")
        wait("DVE", f"{n}.ix")
        done("DVE", V.tensor_copy(w["ixf"][:], w["ix"][:, :, 0:2]), f"{n}.ixf")
        wait("ACT", f"{n}.shift")
        done("ACT", A.activation(ee[:], ee[:], ACT.Exp), f"{n}.exp")
        yield
        wait("DVE", f"{n}.ixf")
        tt(sel[:], iota[:], w["ixf"][:, :, 0:1].to_broadcast([P, NQ, NE]), ALU.is_equal)
        done("DVE", tt(sel2[:], iota[:], w["ixf"][:, :, 1:2].to_broadcast([P, NQ, NE]), ALU.is_equal), f"{n}.sel2")
        yield
        wait("DVE", f"{n}.sel2")
        done("DVE", tt(sel[:], sel[:], sel2[:], ALU.add), f"{n}.sel")
        yield
        wait("DVE", f"{n}.exp", f"{n}.sel")
        if kind != "masked":
            done("DVE", V.tensor_reduce(zz[:, 0, :], ee[:], AX_X, ALU.add), f"{n}.z0")
            yield
            wait("DVE", f"{n}.z0")
            done("DVE", V.reciprocal(zz[:, 1, :], zz[:, 0, :]), f"{n}.z1")
            yield
            wait("DVE", f"{n}.z1")
            done("DVE", tt(ee[:], ee[:], zz[:, 1, :].unsqueeze(2).to_broadcast([P, NQ, NE]), ALU.mult), f"{n}.p")
            yield
            wait("DVE", f"{n}.p")
        if kind == "probs":
            done("DVE", tt(dst, ee[:], sel[:], ALU.mult), f"{n}.w")
            yield
            return
        done("DVE", tt(ee[:], ee[:], sel[:], ALU.mult), f"{n}.ps")
        yield
        wait("DVE", f"{n}.ps")
        done("DVE", V.tensor_reduce(zz[:, 2, :], ee[:], AX_X, ALU.add), f"{n}.s0")
        yield
        wait("DVE", f"{n}.s0")
        if kind == "renormed":
            done("DVE", ts(zz[:, 2, :], zz[:, 2, :], 1e-9, None, ALU.add), f"{n}.s1")
            yield
            wait("DVE", f"{n}.s1")
        done("DVE", V.reciprocal(zz[:, 3, :], zz[:, 2, :]), f"{n}.s2")
        yield
        wait("DVE", f"{n}.s2")
        done("DVE", tt(dst, ee[:], zz[:, 3, :].unsqueeze(2).to_broadcast([P, NQ, NE]), ALU.mult), f"{n}.w")
        yield

    def turn_over(*names):
        for e in ("PE", "DVE", "ACT", "POOL"):
            wait(e, *names)

    def x_tiles(b):
        return X[:, bass.ds(b * NQ, NQ), :]

    def tokens(ap):
        return ap.rearrange("p (q d) -> p q d", q=NQ)

    def update(w, b, n, s_fm, g_src, g_ready):
        for q in range(NQ):
            last = PE.transpose(w["B"][0][:, q * P:(q + 1) * P], s_fm[:, q * P:(q + 1) * P], ident[:])
        done("PE", last, f"{n}.sT")
        wait("ACT", *g_ready)
        done("ACT", A.activation(w["sg"][:], g_src, ACT.Silu), f"{n}.sg")
        yield
        wait("DVE", f"{n}.sT", f"{n}.sg")
        done("DVE", tt(w["sg"][:], w["sg"][:], w["B"][0][:], ALU.mult), f"{n}.sx")
        yield
        wait("DVE", f"{n}.sx")
        done("DVE", tt(x_tiles(b), x_tiles(b), tokens(w["sg"][:]), ALU.add), f"{n}.x")
        yield

    l1s = ExitStack()
    l1w = sb("l1w", [P, NE, T], c=l1s)
    ph0 = ExitStack()
    H = ST
    WA = sb("WA", [P, NE, T], c=ph0)
    WB = sb("WB", [P, NE, T], c=ph0)
    GT = sb("GT", [P, NB * NQ, D], c=ph0)
    BX = sb("BX", [P, NB, T], c=ph0)
    cw = sb("cw", [P, NB * NQ, NE], c=ph0)
    decay = sb("decay", [P, 2], c=ph0)
    HG = sb("HG", [P, 2, HC, T], c=ph0)
    acc = sb("acc", [P, NQ, D], c=ph0)
    cwb = sb("cwb", [P, NQ, NE], c=ph0)
    bxs = sb("bxs", [P, STEPS, NB], c=ph0)
    hs0 = sb("hs0", [P, STEPS + 1, NB], c=ph0)
    ub = sb("ub", [P, NB], c=ph0)
    sets0 = working(ph0, "l0", ("sg", "s"), 2)

    pr.dma("w0")
    load(WA[:], a["l0_w1"], "w0")
    load(WB[:], a["l0_w2"], "w0")
    pr.names[(None, "w0")] = ("w0", pr.count["w0"])
    pr.dma("w1")
    done("DVE", V.memset(wox[:], 0.0), "wox0")
    for n in shapes:
        if not n.startswith("l0"):
            load(M[n][:], a[n], "w1")
    load(l1w[:], a["l1_w"], "w1")
    wait("SP", "wox0", of="start")
    for r in range(4):
        load(wox[32 * r:32 * r + HD, :, :], a["l2_wo"].rearrange("(g r j) o -> r j g o", g=NG, r=4)[r], "w1")
    pr.names[(None, "w1")] = ("w1", pr.count["w1"])

    for e in ("PE", "DVE", "ACT", "POOL"):
        wait(e, "in", of="start")
    done("POOL", G.memset(expo[:], -0.5), "expo")
    wait("POOL", "expo")
    done("DVE", ts(decay[:, 0:1], col(C_L0A), 10.0, None, ALU.min), "amin")
    done("DVE", V.memset(hs0[:, STEPS, :], 0.0), "h_init")
    wait("ACT", "amin")
    done("ACT", A.activation(decay[:, 1:2], decay[:, 0:1], ACT.Exp, scale=-1.0), "decay")
    wait("DVE", "decay")

    def prepare(w, b):
        yield from layer_norm(w, b, "n", keep=XNT)
        wait("PE", "n.xf")
        done("PE", mm(w["B"][2][:], M["l0_bw"][:], w["xf"][:]), "bx")
        wait("ACT", "bx")
        done("ACT", A.copy(flat(BX[:, bass.ds(b, 1), :]), w["B"][2][:]), "bx.copied")
        yield from top_two(w, "r", "renormed", lambda q: w["xf"][:, q * P:(q + 1) * P], M["l0_rw"][:],
                           dst=cw[:, bass.ds(b * NQ, NQ), :])
        turn_over("r.w", "n.kept", "bx.copied")

    with nc.Fori(0, NB // 2) as i:
        pr.enter("prep", i, NB // 2)
        pr.interleave(*[prepare(sets0[k], i * 2 + k) for k in range(2)])
        pr.leave()

    wait("PE", "w0", of="start")
    wait("PE", "1:n.kept", "1:bx.copied", "1:r.lg", of="prep")
    with nc.Fori(0, NB) as b:
        pr.enter("moe0", b, NB)
        wait("POOL", "1:bx.copied", of="prep")
        wait("POOL", f"u{STEPS - 1}", lag=1)
        done("POOL", G.tensor_copy(bxs[:], BX[:, :, bass.ds(b * STEPS, STEPS)].rearrange("p n t -> p t n")), "bxs")
        wait("DVE", "1:r.w", of="prep")
        wait("DVE", f"acc{NE - 1}.{NQ - 1}", lag=1)
        done("DVE", V.tensor_copy(cwb[:], cw[:, bass.ds(b * NQ, NQ), :]), "cwb")
        wait("DVE", "cwb")
        wait("ACT", "h.kept", lag=1)
        wait("ACT", f"h{STEPS - 1}", lag=1)
        done("ACT", A.copy(hs0[:, 0, :], hs0[:, STEPS, :]), "h.carry")

        def step(s):
            if s == 0:
                wait("DVE", "bxs", "h.carry")
            else:
                wait("DVE", f"h{s - 1}")
            done("DVE", stt(ub[:], hs0[:, s, :], decay[:, 1:2], bxs[:, s, :], ALU.mult, ALU.add), f"u{s}")
            wait("ACT", f"u{s}")
            done("ACT", A.activation(hs0[:, s + 1, :], ub[:], ACT.Tanh), f"h{s}")

        def accumulate(e, q):
            if q == 0:
                wait("DVE", f"y{e}")
                if e == 0:
                    wait("DVE", "acc.kept", lag=1)
            ys = bank[4 + e % 2][:, q * D:(q + 1) * D]
            w = cwb[:, q, e:e + 1]
            if e == 0:
                op = ts(acc[:, q, :], ys, w, None, ALU.mult)
            else:
                wait("DVE", f"acc{e - 1}.{q}")
                op = stt(acc[:, q, :], ys, w, acc[:, q, :], ALU.mult, ALU.add)
            done("DVE", op, f"acc{e}.{q}")

        def down(e):
            wait("PE", f"g{e}.{HC - 1}")
            if e >= 2:
                wait("PE", f"acc{e - 2}.{NQ - 1}")
            else:
                wait("PE", f"acc{NE - 2 + e}.{NQ - 1}", lag=1)
            for q in range(NQ):
                for m in range(HC):
                    last = mm(bank[4 + e % 2][:, q * D:(q + 1) * D], HG[:, e % 2, m, q * P:(q + 1) * P],
                              WB[:, e, m * D:(m + 1) * D], start=(m == 0), stop=(m == HC - 1))
            done("PE", last, f"y{e}")

        per = STEPS // (NE * HC)
        for e in range(NE):
            for m in range(HC):
                if e >= 1:
                    wait("PE", f"g{e - 1}.{m}")
                else:
                    wait("PE", f"g{NE - 1}.{m}", lag=1)
                done("PE", mm(bank[m][:], WA[:, e, m * P:(m + 1) * P],
                              flat(XNT[:, bass.ds(b, 1), :])), f"x{e}.{m}")
            if e >= 1:
                down(e - 1)
            for m in range(HC):
                wait("ACT", f"x{e}.{m}")
                if m == 0:
                    if e >= 2:
                        wait("ACT", f"y{e - 2}")
                    else:
                        wait("ACT", f"y{NE - 2 + e}", lag=1)
                done("ACT", A.activation(HG[:, e % 2, m, :], bank[m][:], ACT.Gelu), f"g{e}.{m}")
                for s in range(per):
                    step((e * HC + m) * per + s)
                if e >= 2:
                    accumulate(e - 2, m)
        down(NE - 1)
        for q in range(NQ):
            accumulate(NE - 2, q)
        for q in range(NQ):
            accumulate(NE - 1, q)
        wait("POOL", f"h{STEPS - 1}")
        done("POOL", G.tensor_copy(H[:, :, bass.ds(b * STEPS, STEPS)],
                                   hs0[:, 1:STEPS + 1, :].rearrange("p t n -> p n t")), "h.kept")
        wait("POOL", f"acc{NE - 1}.{NQ - 1}")
        done("POOL", G.tensor_copy(GT[:, bass.ds(b * NQ, NQ), :], acc[:]), "acc.kept")
        pr.leave()

    def finish0(w, b):
        done("PE", mm(w["B"][1][:], M["l0_wo"][:], flat(H[:, bass.ds(b, 1), :])), "o")
        wait("DVE", "o")
        done("DVE", ts(w["s"][:], w["B"][1][:], col(C_L0BO), None, ALU.add), "s")
        yield
        wait("PE", "s")
        yield from update(w, b, "u", w["s"], GT[:, bass.ds(b * NQ, NQ), :].rearrange("p q d -> p (q d)"), ())
        turn_over("u.x")

    wait("PE", "h.kept", "acc.kept", of="moe0")
    wait("ACT", "acc.kept", of="moe0")
    with nc.Fori(0, NB // 2) as i:
        pr.enter("fin0", i, NB // 2)
        pr.interleave(*[finish0(sets0[k], i * 2 + k) for k in range(2)])
        pr.leave()
    ph0.close()
    pr.fence("fin0")
    for e in ("PE", "DVE", "ACT", "POOL"):
        wait(e, "w1", of="start")

    ph1 = ExitStack()
    sets1 = working(ph1, "l1", ("sT", "t1", "t2", "g0", "g1", "wsel", "hpr"), 2)
    for k in range(2):
        for n, s in {"b3": [P, 3], "hp": [P, 2], "oh": [P, 40]}.items():
            sets1[k][n] = sb(f"{n}_{k}", s, c=ph1)
    abar = sb("abar", [32, 2], c=ph1)
    ab = sb("ab", [32, T], c=ph1)
    done("DVE", V.memset(ab[:], 1.0), "ones")
    done("ACT", A.activation(abar[:, 0:1], col(C_L1A, 32), ACT.Exp), "ab0")
    wait("ACT", "ab0")
    done("ACT", A.activation(abar[:, 1:2], abar[:, 0:1], ACT.Exp, scale=-1.0), "ab1")
    wait("DVE", "ab1", "ones")
    done("DVE", ts(ab[:], ab[:], abar[:, 1:2], None, ALU.mult), "ab")
    wait("DVE", "ab")

    def layer1(w, b):
        B, xf, sT, t1, oh, b3, wsel = w["B"], w["xf"], w["sT"], w["t1"], w["oh"], w["b3"], w["wsel"]
        yield from layer_norm(w, b, "n")
        wait("PE", "n.xf")
        done("PE", mm(B[1][0:32, :], M["l1_b"][:], xf[:]), "bx")
        done("PE", mm(B[3][:, 0:1], M["l1_wp1"][:], xf[:, T - 1:T]), "p1")
        wait("ACT", "p1")
        done("ACT", A.activation(w["hp"][:, 0:1], B[3][:, 0:1], ACT.Gelu, bias=col(C_BP1)), "hp")
        wait("DVE", "bx")
        done("DVE", V.tensor_tensor_scan(t1[0:32, :], ab[:], B[1][0:32, :], 0.0, ALU.mult, ALU.add), "h")
        yield
        wait("DVE", "hp")
        done("DVE", V.tensor_copy(w["hpr"][:, 0:P], w["hp"][:, 0:1].to_broadcast([P, P])), "hpr")
        wait("PE", "hpr")
        done("PE", mm(B[3][:, 8:8 + NE], w["hpr"][:, 0:P], M["l1_wp2"][:]), "p2")
        wait("PE", "h")
        done("PE", mm(B[2][:], M["l1_c"][:], t1[0:32, :]), "y")
        yield
        wait("DVE", "p2")
        done("DVE", tt(oh[:, 0:8], B[3][:, 8:8 + NE], M["l1_bp2"][:], ALU.add), "lg1")
        yield
        wait("DVE", "lg1", alone=True)
        done("DVE", V.max(oh[:, 8:16], oh[:, 0:8]), "mx1")
        yield
        wait("DVE", "mx1", alone=True)
        done("DVE", V.max_index(w["ix"][:, 0, :], oh[:, 8:16], oh[:, 0:8]), "ix1")
        yield
        wait("DVE", "ix1")
        done("DVE", V.tensor_copy(oh[:, 16:17], w["ix"][:, 0, 0:1]), "ixf1")
        yield
        wait("DVE", "ixf1")
        done("DVE", ts(oh[:, 24:32], iota[:, 0, :], oh[:, 16:17], None, ALU.is_equal), "oh1")
        yield
        wait("DVE", "oh1")
        done("DVE", ts(wsel[:], l1w[:, 0, :], oh[:, 24:25], None, ALU.mult), "w.0")
        yield
        for e in range(1, NE):
            wait("DVE", f"w.{e - 1}")
            done("DVE", stt(wsel[:], l1w[:, e, :], oh[:, 24 + e:25 + e], wsel[:], ALU.mult, ALU.add), f"w.{e}")
            yield
        bt = w["t2"][:, 0:3 * NE].rearrange("p (c e) -> p c e", c=3)
        done("DVE", tt(bt, M["l1_bias"][:].rearrange("p (c e) -> p c e", c=3),
                       oh[:, 24:32].unsqueeze(1).to_broadcast([P, 3, NE]), ALU.mult), "bt")
        yield
        wait("DVE", "bt")
        done("DVE", V.tensor_reduce(b3[:], bt, AX_X, ALU.add), "b3")
        wait("PE", f"w.{NE - 1}")
        for m in range(2):
            last = mm(B[m][:], wsel[:, m * P:(m + 1) * P], xf[:])
        done("PE", last, "f1")
        wait("ACT", "f1", "b3")
        for m in range(2):
            last = A.activation(w[f"g{m}"][:], B[m][:], ACT.Gelu, bias=b3[:, m:m + 1])
        done("ACT", last, "g")
        wait("DVE", "y")
        done("DVE", stt(sT[:], xf[:], col(C_L1D), B[2][:], ALU.mult, ALU.add), "s")
        yield
        wait("PE", "g")
        for m in range(2):
            last = mm(B[3][:], wsel[:, 256 + m * P:256 + (m + 1) * P], w[f"g{m}"][:], start=(m == 0), stop=(m == 1))
        done("PE", last, "f2")
        wait("DVE", "f2")
        done("DVE", ts(t1[:], B[3][:], b3[:, 2:3], None, ALU.add), "r")
        yield
        wait("PE", "r")
        done("PE", mm(B[1][:], M["l1_wo"][:], t1[:]), "f3")
        wait("DVE", "f3")
        done("DVE", ts(t1[:], B[1][:], col(C_L1BO), 0.3, ALU.add, ALU.mult), "f4")
        yield
        wait("DVE", "f4")
        done("DVE", tt(t1[:], t1[:], xf[:], ALU.add), "f5")
        wait("ACT", "f5")
        done("ACT", A.activation(t1[:], t1[:], ACT.Silu), "sg")
        yield
        wait("DVE", "sg", "s")
        done("DVE", tt(sT[:], sT[:], t1[:], ALU.mult), "p")
        yield
        wait("PE", "p")
        for q in range(NQ):
            last = PE.transpose(B[0][:, q * P:(q + 1) * P], sT[:, q * P:(q + 1) * P], ident[:])
        done("PE", last, "pT")
        wait("DVE", "pT")
        done("DVE", tt(x_tiles(b), x_tiles(b), tokens(B[0][:]), ALU.add), "x")
        yield
        turn_over("x")

    with nc.Fori(0, NB // 2) as i:
        pr.enter("layer1", i, NB // 2)
        pr.interleave(*[layer1(sets1[k], i * 2 + k) for k in range(2)])
        pr.leave()
    ph1.close()
    l1s.close()
    pr.fence("layer1")

    ph2 = ExitStack()
    cosq = sb("cosq", [P, 2, T], c=ph2)
    cosk = sb("cosk", [32, 2, T], c=ph2)
    selq = sb("selq", [P, NG, 2, P], F32R, c=ph2)
    selk = sb("selk", [33, NG, 2, P], F32R, c=ph2)
    negid = sb("negid", [P, P], F32R, c=ph2)
    pr.dma("w2")
    load(cosq[:], a["rope_q"].rearrange("p (c n) -> p c n", c=2), "w2")
    load(cosk[:], a["rope_k"].rearrange("p (c n) -> p c n", c=2), "w2")
    ao = sb("ao", [P, NG, T], c=ph2)
    ssel = ao[:].rearrange("p (c x) n -> p c (x n)", c=2)
    load(ssel[:, 0, :], a["selq"], "w2")
    load(ssel[0:33, 1, :], a["selk"], "w2")
    pr.names[(None, "w2")] = ("w2", pr.count["w2"])
    sets2 = working(ph2, "l2", ("t1", "t2", "t3"), 2)
    for k in range(2):
        w = sets2[k]
        w["KS"] = sb(f"KS_{k}", [P, NG, T], F32R, c=ph2)
        w["QS"] = sb(f"QS_{k}", [P, NG, T], F32R, c=ph2)
        w["qhl"] = sb(f"qhl_{k}", [P, 2, T], F32R, c=ph2)
        w["khl"] = sb(f"khl_{k}", [33, 2, T], F32R, c=ph2)
        w["VA"] = sb(f"VA_{k}", [P, NQ, NG, 32], c=ph2)
        w["ex"] = sb(f"ex_{k}", [P, 4, T], c=ph2)
        w["qmax"] = sb(f"qmax_{k}", [P, NQ, NG, P], F32R, c=ph2)
        w["ao"] = ao
        V.memset(w["khl"][32:33, :, :].bitcast(F32), 1.0)
        V.memset(w["qmax"][:].bitcast(F32), 0.0)
        done("DVE", V.memset(w["VA"][:], 0.0), f"k0.{k}")
    wait("DVE", "k0.1")
    for k in range(2):
        last = V.memset(sets2[k]["VA"][:, :, :, HD:HD + 1], 1.0)
    done("DVE", ts(negid[:], ident[:], -1.0, None, ALU.mult), "k1")
    wait("DVE", "w2", of="start")
    V.tensor_copy(selq[:].rearrange("p g c n -> p (g c n)"), ssel[:, 0, :])
    done("DVE", V.tensor_copy(selk[:].rearrange("p g c n -> p (g c n)"), ssel[0:33, 1, :]), "sel")
    wait("PE", "sel")
    wait("DVE", "sel")

    def scale_maxima(w, b):
        B, xf, t1, t2, t3 = w["B"], w["xf"], w["t1"], w["t2"], w["t3"]
        QS, KS, VA = w["QS"], w["KS"], w["VA"]
        yield from layer_norm(w, b, "n", keep=XNT)
        wait("PE", "n.xf")
        for nm, mat, wt, tab, n in (("q", "l2_q", w["qhl"], cosq, P), ("k", "l2_k", w["khl"], cosk, 32)):
            mm(B[1][0:n, :], M[mat][:, 0:n], xf[:])
            done("PE", mm(B[2][0:n, :], M[mat][:, n:2 * n], xf[:]), nm)
            wait("DVE", nm)
            tt(t1[0:n, :], B[1][0:n, :], tab[:, 0, :], ALU.mult)
            done("DVE", tt(t2[0:n, :], B[2][0:n, :], tab[:, 1, :], ALU.mult), f"{nm}1")
            yield
            wait("DVE", f"{nm}1")
            wait("PE", f"{nm}1")
            done("DVE", tt(t3[0:n, :], t1[0:n, :], t2[0:n, :], ALU.add), f"{nm}2")
            yield
            wait("DVE", f"{nm}2")
            done("DVE", V.tensor_copy(wt[0:n, 0, :], t3[0:n, :]), f"{nm}3")
            yield
            wait("DVE", f"{nm}3")
            done("DVE", tt(wt[0:n, 1, :], t3[0:n, :], wt[0:n, 0, :].bitcast(F32), ALU.subtract), f"{nm}hl")
            yield
            wait("DVE", f"{nm}hl")
        for q in range(NQ):
            last = mm(B[3][:, q * 32:(q + 1) * 32], xf[:, q * P:(q + 1) * P], M["l2_v"][:])
        done("PE", last, "v")
        wait("ACT", "v")
        done("ACT", A.copy(VA[:, :, :, 0:HD],
                           B[3][:, 0:P].rearrange("p (q g d) -> p q g d", q=NQ, g=NG)), "va")
        yield
        wait("PE", "qhl", "khl", "va")
        k = 0
        for g in range(NG):
            for sel, hl, dst, n in ((selq, w["qhl"], QS, P), (selk, w["khl"], KS, 33)):
                if k >= 4:
                    wait("PE", f"st{k - 4}")
                for c in range(2):
                    last = mm(B[k % 4][:], sel[0:n, g, c, :], hl[0:n, c, :], start=(c == 0), stop=(c == 1))
                done("PE", last, f"sel{k}")
                wait("ACT", f"sel{k}")
                done("ACT", A.copy(dst[:, g, :], B[k % 4][:]), f"st{k}")
                k += 1
            yield
        wait("PE", f"st{k - 1}")
        n = 0
        for g in range(NG):
            for q in range(NQ):
                for r in range(4):
                    if n >= 4:
                        wait("PE", f"mx{n - 4}")
                    rows = slice(32 * r, 32 * r + 32)
                    done("PE", mm(B[r][:], QS[rows, g, q * P:(q + 1) * P], KS[rows, g, :]), f"sc{n}")
                    wait("DVE", f"sc{n}")
                    done("DVE", V.tensor_reduce(w["qmax"][:, q, g, 32 * r + 24:32 * r + 25], B[r][:], AX_X,
                                                ALU.max), f"mx{n}")
                    n += 1
                    if r:
                        yield
        wait("PE", f"mx{n - 1}")
        for g in range(NG):
            for c in range(2):
                mm(B[g][:], selq[:, g, c, :], w["qhl"][:, c, :], start=(c == 0), stop=False)
            for q in range(NQ):
                last = mm(B[g][:, q * P:(q + 1) * P], w["qmax"][:, q, g, :], negid[:], start=False, stop=(q == NQ - 1))
            done("PE", last, f"mrow{g}")
            wait("ACT", f"mrow{g}")
            done("ACT", A.copy(QS[:, g, :], B[g][:]), f"qe{g}")
            yield
        turn_over(f"qe{NG - 1}", "n.kept")

    def attend(w, b):
        B, t1, t2 = w["B"], w["t1"], w["t2"]
        QS, KS, VA, ex, ao = w["QS"], w["KS"], w["VA"], w["ex"], w["ao"]
        tiles = [(g, r, kt) for g in range(NG) for r in range(4) for kt in range(NQ)]

        def scores(n):
            g, r, kt = tiles[n]
            if n >= 2:
                wait("PE", f"ex{n - 2}")
            rows = slice(32 * r, 32 * r + 32)
            done("PE", mm(B[n % 2][:], KS[rows, g, kt * P:(kt + 1) * P], QS[rows, g, :]), f"se{n}")
            wait("ACT", f"se{n}")
            if n >= 4:
                wait("ACT", f"pv{n - 4}")
            done("ACT", A.activation(ex[:, n % 4, :], B[n % 2][:], ACT.Exp, scale=SM_SCALE), f"ex{n}")

        scores(0)
        for n, (g, r, kt) in enumerate(tiles):
            if n + 1 < len(tiles):
                scores(n + 1)
            wait("PE", f"ex{n}")
            if r == 0 and kt == 0 and g >= 1:
                wait("PE", f"o{g - 1}")
            done("PE", mm(B[2][32 * r:32 * r + 32, :], VA[:, kt, g, :], ex[:, n % 4, :],
                          start=(kt == 0), stop=(kt == NQ - 1)), f"pv{n}")
            if r == 3 and kt == NQ - 1:
                wait("ACT", f"pv{n}")
                if g >= 1:
                    wait("ACT", f"on{g - 1}")
                done("ACT", A.copy(t1[:], B[2][:]), f"o{g}")
            yield
            if (r == 0 and kt == 2 and g >= 1) or n == len(tiles) - 1:
                k = g - 1 if n < len(tiles) - 1 else g
                wait("PE", f"o{k}")
                if k >= 1:
                    wait("PE", f"rec{k - 1}")
                done("PE", mm(B[3][:], M["den"][:], t1[:]), f"d{k}")
                wait("DVE", f"d{k}")
                if k >= 1:
                    wait("DVE", f"on{k - 1}")
                done("DVE", V.reciprocal(t2[:], B[3][:]), f"rec{k}")
                yield
                wait("DVE", f"rec{k}")
                done("DVE", tt(ao[:, k, :], t1[:], t2[:], ALU.mult), f"on{k}")
        wait("PE", f"on{NG - 1}")
        for g in range(NG):
            last = mm(B[3][:], wox[:, g, :], ao[:, g, :], start=(g == 0), stop=(g == NG - 1))
        done("PE", last, "wo")
        wait("ACT", "wo")
        done("ACT", A.copy(flat(ST[:, bass.ds(b, 1), :]), B[3][:]), "s")
        yield
        turn_over("s")

    pr.enter("attn first", 0, 1)
    pr.interleave((0, scale_maxima(sets2[0], 0)))
    pr.leave()
    pr.fence("attn first")
    with nc.Fori(0, NB // 2 - 1) as i:
        pr.enter("attn", i, NB // 2 - 1)
        pr.interleave((0, attend(sets2[0], i * 2)), (1, scale_maxima(sets2[1], i * 2 + 1)))
        pr.interleave((1, attend(sets2[1], i * 2 + 1)), (0, scale_maxima(sets2[0], i * 2 + 2)))
        pr.leave()
    pr.fence("attn")
    pr.enter("attn last", 0, 1)
    pr.interleave((0, attend(sets2[0], NB - 2)), (1, scale_maxima(sets2[1], NB - 1)))
    pr.interleave((1, attend(sets2[1], NB - 1)))
    pr.leave()
    ph2.close()
    pr.fence("attn last")

    W3 = [sb(n, [P, NE, T]) for n in ("wv", "w", "w1")]
    pr.dma("w3")
    for wt, n in zip(W3, ("l3_wv", "l3_w", "l3_w1")):
        load(wt[:], a[n], "w3")
    pr.names[(None, "w3")] = ("w3", pr.count["w3"])
    ph3 = ExitStack()
    sets3 = working(ph3, "l3", ("sg", "sT", "gt"), 2)
    for k in range(2):
        sets3[k]["w8T"] = sb(f"w8T_{k}", [NE, T], c=ph3)

    def mixture2(w, b):
        B, xf = w["B"], w["xf"]
        done("ACT", A.copy(xf[:], flat(XNT[:, bass.ds(b, 1), :])), "xf")
        wait("PE", "xf")
        yield from top_two(w, "r", "masked", lambda q: xf[:, q * P:(q + 1) * P], M["l2_gw"][:],
                           bias=M["l2_gb"][:].rearrange("p (q e) -> p q e", q=NQ), dst=w["w8"][:])
        wait("PE", "r.w")
        for q in range(NQ):
            last = PE.transpose(B[2][0:NE, q * P:(q + 1) * P], w["w8"][:, q, :], ident[:])
        done("PE", last, "w8T")
        wait("ACT", "w8T")
        done("ACT", A.copy(w["w8T"][:], B[2][0:NE, :]), "w8")
        yield
        wait("PE", "w8")
        for q in range(NQ):
            last = mm(B[3][:, q * D:(q + 1) * D], w["w8T"][:, q * P:(q + 1) * P], M["l2_eb"][:])
        done("PE", last, "eb")
        wait("ACT", "eb")
        done("ACT", A.copy(w["gt"][:], B[3][:]), "gt")
        yield
        wait("DVE", "gt")
        wait("PE", "gt")
        for k in range(2 * NQ):
            q, h = k // 2, k % 2
            if k >= 3:
                wait("PE", f"a{k - 3}.3")
            bk = B[1 + k % 3]
            done("PE", mm(bk[:], xf[:, q * P:(q + 1) * P], M["l2_w"][:, h * T:(h + 1) * T]), f"e{k}")
            for e in range(4):
                if e == 0:
                    wait("DVE", f"e{k}")
                    if h:
                        wait("DVE", f"a{k - 1}.3")
                else:
                    wait("DVE", f"a{k}.{e - 1}")
                gq = tokens(w["gt"][:])[:, q, :]
                done("DVE", stt(gq, bk[:, e * D:(e + 1) * D], w["w8"][:, q, 4 * h + e:4 * h + e + 1], gq,
                                ALU.mult, ALU.add), f"a{k}.{e}")
                yield
        done("ACT", A.copy(w["sT"][:], flat(ST[:, bass.ds(b, 1), :])), "s")
        wait("PE", "s")
        yield from update(w, b, "u", w["sT"], w["gt"][:], ("a7.3",))
        wait("PE", "u.x")

    with nc.Fori(0, NB // 2) as i:
        pr.enter("mix2", i, NB // 2)
        pr.interleave(*[mixture2(sets3[k], i * 2 + k) for k in range(2)])
        pr.leave()
    ph3.close()
    pr.fence("mix2")

    ph4 = ExitStack()
    CH = T // 4
    sets4 = working(ph4, "l4", ("t1", "u", "gs", "xres", "sT"), 2)
    for k in range(2):
        w = sets4[k]
        w["pad"] = sb(f"pad_{k}", [P, T + 4], c=ph4)
        w["cpad"] = sb(f"cpad_{k}", [P, T + 2], c=ph4)
        w["hx"] = sb(f"hx_{k}", [P, CH], c=ph4)
        w["he"] = sb(f"he_{k}", [32, 2, CH + 1], c=ph4)
        w["hf"] = sb(f"hf_{k}", [P, CH], c=ph4)
        V.memset(w["pad"][:], 0.0)
        V.memset(w["cpad"][:], 0.0)
        V.memset(w["he"][:], 0.0)
    done("DVE", V.memset(sets4[0]["t1"][:], 1.0), "ones4")
    wait("DVE", "ones4")

    NLV = 9
    pw = [sb(f"pw{m}", [32, NLV, 2, 32], c=ph4) for m in range(2)]
    blk = [sb(f"blk{m}", [P, P], c=ph4) for m in range(2)]
    car = [sb(f"car{m}", [32, P], c=ph4) for m in range(2)]
    cst = [sb(f"cst{m}", [P, P], c=ph4) for m in range(2)]

    def powers(m):
        B = sets4[m]["B"]
        done("DVE", V.tensor_copy(pw[m][:, 0, :, :], M[f"m{m + 1}_A"][:].rearrange("p (c n) -> p c n", c=2)), "pw0")
        yield
        for k in range(1, NLV):
            wait("PE", f"pw{k - 1}")
            mm(B[0][0:32, 0:32], pw[m][:, k - 1, 1, :], pw[m][:, k - 1, 0, :])
            done("PE", mm(B[0][0:32, 32:64], pw[m][:, k - 1, 0, :], pw[m][:, k - 1, 1, :]), f"sq{k}")
            wait("DVE", f"sq{k}")
            done("DVE", V.tensor_copy(pw[m][:, k, :, :],
                                      B[0][0:32, 0:64].rearrange("p (c n) -> p c n", c=2)), f"pw{k}")
            yield
        done("DVE", V.tensor_copy(car[m][:, 0:32], pw[m][:, 0, 1, :]), "car0")
        for k in range(1, 4):
            wait("PE", f"car{k - 1}")
            done("PE", mm(B[0][0:32, 0:32], pw[m][:, 0, 0, :], car[m][:, 32 * (k - 1):32 * k]), f"cm{k}")
            wait("DVE", f"cm{k}")
            done("DVE", V.tensor_copy(car[m][:, 32 * k:32 * k + 32], B[0][0:32, 0:32]), f"car{k}")
            yield
        done("DVE", V.memset(blk[m][:], 0.0), "blk0")
        wait("PE", "car3")
        for s in range(4):
            for t in range(s, 4):
                src = ident[0:32, 0:32] if t == s else car[m][:, 32 * (t - s - 1):32 * (t - s)]
                last = mm(B[1][32 * s:32 * s + 32, 32 * t:32 * t + 32], ident[0:32, 0:32], src)
        done("PE", last, "bm")
        wait("DVE", "bm", "blk0")
        for s in range(4):
            V.tensor_copy(blk[m][32 * s:32 * s + 32, 32 * s:P], B[1][32 * s:32 * s + 32, 32 * s:P])
        done("DVE", ts(cst[m][:], sets4[0]["t1"][:, 0:P], col(C_M[m] + C_CV), None, ALU.mult), "cst")
        wait("PE", "cst")
        wait("ACT", "cst")
        wait("DVE", "cst")
        yield

    pr.interleave(*[powers(m) for m in range(2)])

    def mamba(w, m, n, src, dst, dst_name):
        B, t1, u, gs, pad, hx, he, hf = (w[x] for x in ("B", "t1", "u", "gs", "pad", "hx", "he", "hf"))
        c = C_M[m]
        w_in, w_out, w_ssm = M[f"m{m + 1}_in"], M[f"m{m + 1}_out"], M[f"m{m + 1}_ssm"]
        done("PE", mm(B[1][:], w_in[:, 0:D], src), f"{n}.xs")
        done("PE", mm(B[2][:], w_in[:, D:2 * D], src), f"{n}.gate")
        wait("ACT", f"{n}.xs")
        done("ACT", A.activation(pad[:, 3:T + 3], B[1][:], ACT.Identity, bias=col(c + C_INX)), f"{n}.pad")
        wait("ACT", f"{n}.gate")
        done("ACT", A.activation(gs[:], B[2][:], ACT.Silu, bias=col(c + C_ING)), f"{n}.gs")
        yield
        wait("DVE", f"{n}.pad")
        done("DVE", ts(t1[:], pad[:, 0:T], col(c + C_CVW), None, ALU.mult), f"{n}.cv0")
        yield
        for j in range(1, 4):
            wait("DVE", f"{n}.cv{j - 1}")
            done("DVE", stt(t1[:], pad[:, j:j + T], col(c + C_CVW + j), t1[:], ALU.mult, ALU.add), f"{n}.cv{j}")
            yield
        wait("ACT", f"{n}.cv3")
        done("ACT", A.activation(u[:], t1[:], ACT.Silu, bias=col(c + C_CVB)), f"{n}.u")
        yield
        wait("PE", f"{n}.u")
        uv = u[:].rearrange("p (c t) -> p t c", t=4)
        for t in range(4):
            last = mm(B[3][32 * t:32 * t + 32, 0:CH], w_ssm[:], uv[:, t, :])
        done("PE", last, f"{n}.ssm")
        wait("DVE", f"{n}.ssm")
        done("DVE", ts(hx[:], B[3][:, 0:CH], col(c + C_SSB), col(c + C_BV), ALU.add, ALU.mult), f"{n}.hx")
        yield
        wait("PE", f"{n}.hx")
        done("PE", mm(B[3][0:32, P:2 * P], blk[m][:, 96:P], hx[:]), f"{n}.e")
        wait("DVE", f"{n}.e")
        done("DVE", V.tensor_copy(he[:, 0, 1:CH + 1], B[3][0:32, P:2 * P]), f"{n}.he")
        yield
        cur = f"{n}.he"
        lv = 0
        while (1 << lv) < CH:
            o = 1 << lv
            wait("PE", cur, alone=True)
            done("PE", mm(B[3][0:32, 2 * P:2 * P + CH - o], pw[m][:, lv + 2, 1, :],
                          he[:, lv % 2, 1:CH + 1 - o]), f"{n}.sh{lv}")
            wait("DVE", f"{n}.sh{lv}")
            V.tensor_copy(he[:, (lv + 1) % 2, 1:1 + o], he[:, lv % 2, 1:1 + o])
            done("DVE", tt(he[:, (lv + 1) % 2, 1 + o:CH + 1], he[:, lv % 2, 1 + o:CH + 1],
                           B[3][0:32, 2 * P:2 * P + CH - o], ALU.add), f"{n}.he{lv}")
            cur = f"{n}.he{lv}"
            yield
            wait("DVE", cur)
            lv += 1
        wait("PE", cur)
        mm(B[3][:, 3 * P:], blk[m][:], hx[:], stop=False)
        done("PE", mm(B[3][:, 3 * P:], car[m][:], he[:, lv % 2, 0:CH], start=False), f"{n}.h")
        wait("DVE", f"{n}.h")
        done("DVE", V.tensor_copy(hf[:], B[3][:, 3 * P:]), f"{n}.hf")
        yield
        wait("PE", f"{n}.hf", f"{n}.gs")
        for t in range(4):
            last = mm(B[t][:, 0:CH], cst[m][32 * t:32 * t + 32, :], hf[32 * t:32 * t + 32, :])
        done("PE", last, f"{n}.c")
        wait("DVE", f"{n}.c", f"{n}.u")
        for t in range(4):
            last = stt(t1[:].rearrange("p (c t) -> p t c", t=4)[:, t, :], B[t][:, 0:CH],
                       col(c + C_DV), uv[:, t, :], ALU.add, ALU.mult)
        done("DVE", last, f"{n}.cu")
        yield
        wait("DVE", f"{n}.cu", f"{n}.gs")
        done("DVE", tt(t1[:], t1[:], gs[:], ALU.mult), f"{n}.y")
        yield
        wait("PE", f"{n}.y")
        done("PE", mm(B[0][:], w_out[:], t1[:]), f"{n}.o")
        wait("DVE", f"{n}.o")
        done("DVE", stt(dst, B[0][:], col(c + C_OB), src, ALU.add, ALU.add), dst_name)
        yield

    def mixer3(w, b):
        B, t1, cpad, sT = w["B"], w["t1"], w["cpad"], w["sT"]
        opad = w["pad"][:, 2:T + 4]
        yield from layer_norm(w, b, "n", keep=XNT)
        wait("PE", "n.xf")
        yield from mamba(w, 0, "ma", w["xf"][:], w["xres"][:], "ma.x")
        wait("DVE", "ma.x")
        wait("PE", "ma.x")
        yield from mamba(w, 1, "mb", w["xres"][:], cpad[:, 1:T + 1], "mb.x")
        wait("PE", "mb.x")
        for j in range(3):
            last = mm(B[1][0:64, :], M["c1"][:, 64 * j:64 * j + 64], cpad[:, j:j + T], start=(j == 0), stop=(j == 2))
        done("PE", mm(B[1][64:P, :], M["c4"][:], cpad[:, 1:T + 1]), "c14")
        wait("DVE", "c14")
        done("DVE", ts(t1[:], B[1][:], col(C_C1B), 0.0, ALU.add, ALU.max), "relu")
        yield
        wait("DVE", "relu")
        ts(opad[0:64, 1:T + 1], t1[0:64, :], BN_SCALE, None, ALU.mult)
        done("DVE", V.tensor_copy(opad[64:P, 1:T + 1], t1[64:P, :]), "oc")
        yield
        wait("PE", "oc")
        for j in range(3):
            last = mm(B[2][:], M["c5"][:, P * j:P * j + P], opad[:, j:j + T], start=(j == 0), stop=(j == 2))
        done("PE", last, "c5")
        wait("DVE", "c5")
        done("DVE", ts(t1[:], B[2][:], 0.0, BN_SCALE, ALU.max, ALU.mult), "o5")
        yield
        wait("DVE", "o5")
        done("DVE", tt(flat(ST[:, bass.ds(b, 1), :]), t1[:], cpad[:, 1:T + 1], ALU.add), "s")
        yield
        turn_over("s", "n.kept")

    with nc.Fori(0, NB // 2) as i:
        pr.enter("mixer3", i, NB // 2)
        pr.interleave(*[mixer3(sets4[k], i * 2 + k) for k in range(2)])
        pr.leave()
    ph4.close()
    pr.fence("mixer3")

    sets5 = working(ctx, "l5", ("sg", "sT", "gt", "ge", "vy0", "vy1", "vy2", "vy3"), 2)
    one = sb("one", [1, P])
    sc = sb("sc", [1, 2, T])
    done("DVE", V.memset(one[:], 1.0), "one")
    pr.dma("sc0")
    pr.dma("sc1")
    wait("PE", "one")
    wait("DVE", "w3", of="start")
    k = 0
    for wt, nm in zip(W3, ("l3_sv", "l3_s", "l3_s1")):
        for e in range(NE):
            if k >= 2:
                wait("SP", f"scb{k - 2}")
            load(sc[:, k % 2, :], a[nm].rearrange("(o e) n -> o e n", o=1)[:, e, :], f"sc{k % 2}")
            pr.names[(None, f"sc{k}")] = (f"sc{k % 2}", pr.count[f"sc{k % 2}"])
            wait("PE", f"sc{k}")
            if k >= 2:
                wait("PE", f"scm{k - 2}")
            done("PE", mm(bank[k % 2][:], one[:], sc[0:1, k % 2, :]), f"scb{k}")
            wait("DVE", f"scb{k}")
            done("DVE", tt(wt[:, e, :], wt[:, e, :], bank[k % 2][:], ALU.mult), f"scm{k}")
            k += 1
    wait("PE", f"scm{k - 1}")
    for j in range(2):
        pr.dma(f"out{j}")
    WA3, WB3, WC3 = W3

    def mixture3(w, b, way):
        B, xf, ge = w["B"], w["xf"], w["ge"]
        vy = [w[f"vy{m}"] for m in range(HC)]
        gt = tokens(w["gt"][:])
        done("ACT", A.copy(xf[:], flat(XNT[:, bass.ds(b, 1), :])), "xf")
        wait("PE", "xf")
        yield from top_two(w, "r", "probs", lambda q: xf[:, q * P:(q + 1) * P], M["l3_rw"][:], dst=w["w8"][:])
        wait("DVE", "r.w")
        n = 0
        for e in range(NE):
            for m in range(HC):
                if n >= 1:
                    wait("PE", f"vy{n - 1}")
                else:
                    wait("PE", "r.lg")
                mm(B[1][:], WA3[:, e, m * P:(m + 1) * P], xf[:])
                done("PE", mm(B[2][:], WB3[:, e, m * P:(m + 1) * P], xf[:]), f"vw{n}")
                wait("ACT", f"vw{n}")
                if n >= 1:
                    wait("ACT", f"vy{n - 1}")
                done("ACT", A.activation(ge[:], B[2][:], ACT.Gelu_apprx_tanh), f"ge{n}")
                wait("DVE", f"ge{n}")
                if e and m == 0:
                    wait("DVE", f"y{e - 1}")
                done("DVE", tt(vy[m][:], ge[:], B[1][:], ALU.mult), f"vy{n}")
                n += 1
                yield
            wait("PE", f"vy{n - 1}")
            if e >= 1:
                wait("PE", f"a{e - 1}")
            for q in range(NQ):
                for m in range(HC):
                    last = mm(B[3][:, q * D:(q + 1) * D], vy[m][:, q * P:(q + 1) * P],
                              WC3[:, e, m * D:(m + 1) * D], start=(m == 0), stop=(m == HC - 1))
            done("PE", last, f"y{e}")
            wait("DVE", f"y{e}")
            if e:
                wait("DVE", f"a{e - 1}")
            for q in range(NQ):
                ys = B[3][:, q * D:(q + 1) * D]
                if e == 0:
                    last = ts(gt[:, q, :], ys, w["w8"][:, q, e:e + 1], None, ALU.mult)
                else:
                    last = stt(gt[:, q, :], ys, w["w8"][:, q, e:e + 1], gt[:, q, :], ALU.mult, ALU.add)
            done("DVE", last, f"a{e}")
            yield
        done("ACT", A.copy(w["sT"][:], flat(ST[:, bass.ds(b, 1), :])), "s")
        wait("PE", "s")
        yield from update(w, b, "u", w["sT"], w["gt"][:], (f"a{NE - 1}",))
        wait("SP", "u.x")
        done(f"out{way}", S.dma_start(out[bass.ds(b, 1)].rearrange("a (q p) d -> p (a q) d", p=P), x_tiles(b)),
             "out", by=16)

    with nc.Fori(0, NB // 2) as i:
        pr.enter("mix3", i, NB // 2)
        pr.interleave(*[mixture3(sets5[k], i * 2 + k, k) for k in range(2)])
        pr.leave()
    wait("SP", "0:out", of="mix3")
    wait("SP", "1:out", of="mix3")
    ctx.close()
    return pr


_OUT_SHAPE = (NB, T, D)


def _rope():
    inv = (1.0 / np.float32(10000.0) ** (np.arange(0, D, 2, dtype=np.float32) / np.float32(D))).astype(np.float32)
    ang = (np.arange(T, dtype=np.float32)[:, None] * inv[None, :]).astype(np.float32)
    cos, sin = np.cos(ang).T, np.sin(ang).T
    c = np.repeat(cos, 2, axis=0)
    s = np.stack([-sin, sin], axis=1).reshape(D, T)
    ck, sk = np.concatenate([c[0:HD]] * NG), np.concatenate([s[0:HD]] * NG)
    return (np.concatenate([c, s], axis=1).astype(np.float32), np.concatenate([ck, sk], axis=1).astype(np.float32))


def _lay_out(i):
    t = np.ascontiguousarray
    swap = np.arange(D).reshape(-1, 2)[:, ::-1].reshape(-1)
    swk = np.arange(32).reshape(-1, 2)[:, ::-1].reshape(-1)
    z = np.zeros(P, np.float32)
    a = {"x": i["L0_attn_x"], "l0_wo": t(i["L0_attn_Wo"].T), "l0_bw": t(i["L0_attn_B_w"].T),
         "l0_rw": t(i["L0_ffn_router_w"].T)}
    cols = [i["L0_attn_A"], i["L0_attn_bo"], np.tile(i["L1_attn_A"], 4), i["L1_attn_D"], i["L1_ffn_bp1"],
            i["L1_ffn_bo"], np.concatenate([i["L3_attn_c1_b"], z[0:64]]), z]
    for m in ("m1", "m2"):
        g = lambda n: i[f"L3_attn_{m}_{n}"]
        cols += [g("in_b")[0:D], g("in_b")[D:], g("conv_b")] + [g("conv_w")[:, 0, k] for k in range(4)]
        cols += [np.tile(g("ssm_b"), 4), np.tile(g("B"), 4), g("D"), g("out_b"), np.tile(g("C"), 4)]
        a[f"{m}_in"], a[f"{m}_ssm"], a[f"{m}_out"] = g("in_w"), g("ssm_w"), g("out_w")
        a[f"{m}_A"] = np.concatenate([g("A"), g("A").T], axis=1)
    a["cv"] = np.stack(cols, axis=1)
    a["ident"] = np.eye(P, dtype=np.float32)
    a["iota"] = np.tile(np.arange(NE, dtype=np.float32), (P, NQ))
    den = np.zeros((P, P), np.float32)
    for r in range(4):
        den[32 * r + HD, 32 * r:32 * r + 32] = 1.0
    a["den"] = den
    a["l0_w1"] = i["L0_ffn_w1"].transpose(1, 0, 2)
    a["l0_w2"] = i["L0_ffn_w2"].reshape(NE, HC, P, D).transpose(2, 0, 1, 3).reshape(P, NE, T)
    a["l1_b"], a["l1_c"] = i["L1_attn_B"].T, i["L1_attn_C"].T
    a["l1_wp1"], a["l1_wp2"], a["l1_wo"] = i["L1_ffn_Wp1"], i["L1_ffn_Wp2"], i["L1_ffn_Wo"]
    a["l1_bp2"] = np.tile(i["L1_ffn_bp2"], (P, 1))
    b1 = i["L1_ffn_b1"].reshape(NE, 2, P).transpose(2, 1, 0)
    a["l1_bias"] = np.concatenate([b1, i["L1_ffn_b2"].T[:, None, :]], axis=1).reshape(P, 3 * NE)
    w2 = i["L1_ffn_W2"].reshape(NE, 2, P, D).transpose(2, 0, 1, 3).reshape(P, NE, 2 * D)
    a["l1_w"] = np.concatenate([i["L1_ffn_W1"].transpose(1, 0, 2), w2], axis=2)
    a["l2_q"] = np.concatenate([i["L2_attn_Wq"], i["L2_attn_Wq"][:, swap]], axis=1)
    a["l2_k"] = np.concatenate([i["L2_attn_Wk"], i["L2_attn_Wk"][:, swk]], axis=1)
    a["l2_v"], a["l2_wo"] = i["L2_attn_Wv"], i["L2_attn_Wo"]
    a["l2_gw"], a["l2_gb"] = i["L2_ffn_gate_w"].T, np.tile(i["L2_ffn_gate_b"], (P, NQ))
    a["l2_w"], a["l2_eb"] = i["L2_ffn_expert_w"].transpose(1, 0, 2).reshape(P, NE * D), i["L2_ffn_expert_b"]
    a["rope_q"], a["rope_k"] = _rope()
    selq, selk = np.zeros((P, NG, 2, P), np.float32), np.zeros((33, NG, 2, P), np.float32)
    for g in range(NG):
        for r in range(4):
            for d in range(HD):
                for p in range(3):
                    selq[32 * g + HD * r + d, g, int(p == 1), 32 * r + HD * p + d] = 1.0
                    selk[HD * g + d, g, int(p == 2), 32 * r + HD * p + d] = 1.0
            selk[32, g, 0, 32 * r + 24] = 1.0
    a["selq"], a["selk"] = selq.reshape(P, -1), selk.reshape(33, -1)
    a["c1"] = i["L3_attn_c1_w"].transpose(1, 2, 0).reshape(P, 3 * 64)
    a["c4"] = i["L3_attn_c4_w"][:, :, 0].T
    a["c5"] = i["L3_attn_c5_w"].transpose(1, 2, 0).reshape(P, 3 * P)
    a["l3_rw"] = i["L3_ffn_router_w"]
    a["l3_wv"], a["l3_w"] = i["L3_ffn_wv"].transpose(1, 0, 2), i["L3_ffn_w"].transpose(1, 0, 2)
    a["l3_w1"] = i["L3_ffn_w1"].reshape(NE, HC, P, D).transpose(2, 0, 1, 3).reshape(P, NE, T)
    a["l3_sv"], a["l3_s"] = i["L3_ffn_sv"][:, 0, :], i["L3_ffn_s"][:, 0, :]
    a["l3_s1"] = np.tile(i["L3_ffn_s1"][:, 0, :], (1, HC))
    return {n: t(v) for n, v in a.items()}


def kernel(**inputs):
    import concourse.bacc as bacc
    from concourse.bass_utils import run_bass_kernel_spmd

    arrays = _lay_out({n: np.asarray(v) for n, v in inputs.items()})
    known = None
    for _ in range(2):
        nc = bacc.Bacc("TRN2", target_bir_lowering=False, num_devices=1)
        aps = {n: nc.dram_tensor(f"in_{n}", v.shape, F32, kind="ExternalInput").ap() for n, v in arrays.items()}
        out = nc.dram_tensor("out", _OUT_SHAPE, F32, kind="ExternalOutput").ap()
        pr = build(nc, known, aps, out)
        known = (pr.names, pr.loops)
    r = run_bass_kernel_spmd(nc, [{f"in_{n}": v for n, v in arrays.items()}], core_ids=[0])
    return r.results[0]["out"]
```

```python
from contextlib import ExitStack

import numpy as np
import concourse.bass as bass
from concourse import mybir

ALU = mybir.AluOpType
ACT = mybir.ActivationFunctionType
AX_X = mybir.AxisListType.X
F32 = mybir.dt.float32
F32R = mybir.dt.float32r
U32 = mybir.dt.uint32

P = 128
NB, T, D = 8, 512, 128
NQ = T // P
NE = 8
HC = 4
HEADS, HD, NG = 16, 8, 4
LN_EPS = 1e-5
SM_SCALE = float(1.0 / np.sqrt(np.float32(D)))
BN_SCALE = float(1.0 / np.float32(np.sqrt(1.0 + 1e-5)))
CREDIT = 2000
STEPS = T // NB

C_L0A, C_L0BO, C_L1A, C_L1D, C_BP1, C_L1BO, C_C1B = range(7)
C_INX, C_ING, C_CVB, C_CVW, C_SSB, C_BV, C_DV, C_OB, C_CV = 0, 1, 2, 3, 7, 8, 9, 10, 11
C_M = (8, 20)
NCV = 32


class Progress:

    def __init__(self, nc, ctx, known):
        self.eng = {"PE": nc.tensor, "DVE": nc.vector, "ACT": nc.scalar, "POOL": nc.gpsimd, "SP": nc.sync}
        self.nc, self.ctx, self.known = nc, ctx, known
        self.sem, self.count = {}, {}
        for e in ("PE", "DVE", "ACT", "POOL"):
            self.sem[e] = ctx.enter_context(nc.semaphore(f"progress_{e}"))
            self.count[e] = CREDIT
            self.eng[e].sem_inc(self.sem[e], CREDIT)
        self.names, self.loops, self.lengths = {}, {}, []
        self.loop, self.seen, self.stream = None, {}, None

    def dma(self, name, credit=0):
        self.sem[name] = self.ctx.enter_context(self.nc.semaphore(f"dma_{name}"))
        self.count[name] = credit
        if credit:
            self.nc.sync.sem_inc(self.sem[name], credit)

    def enter(self, name, i, n):
        self.loop, self.i, self.n, self.seen = name, i, n, {}
        self.base = dict(self.count)

    def leave(self):
        for e in self.count:
            per = self.count[e] - self.base[e]
            self.loops[(self.loop, e)] = (self.base[e], per, self.n)
            self.count[e] = self.base[e] + per * self.n
            self.names[(None, f"{self.loop} ended on {e}")] = (e, self.count[e])
        self.loop, self.seen = None, {}

    def fence(self, loop):
        for e in self.eng:
            self.wait(e, *[f"{loop} ended on {c}" for c in ("PE", "DVE", "ACT", "POOL")], of="start")

    def interleave(self, *streams, apart=0.0):
        call = len(self.lengths)
        live = [g if isinstance(g, tuple) else (k, g) for k, g in enumerate(streams)]
        told = self.known[2][call] if self.known else {}
        taken = {k: 0 for k, _ in live}
        while live:
            k, g = min(live, key=lambda s: (taken[s[0]] + 1) / told.get(s[0], 1) + apart * s[0])
            self.stream = k
            taken[k] += 1
            if next(g, self) is self:
                live.remove((k, g))
        self.stream = None
        self.lengths.append(taken)

    def done(self, chan, instr, name=None, by=1):
        instr.then_inc(self.sem[chan], by)
        self.count[chan] += by
        if name and self.stream is not None:
            name = f"{self.stream}:{name}"
        if name:
            assert (self.loop, name) not in self.names, name
            self.names[(self.loop, name)] = (chan, self.count[chan] - (self.base[chan] if self.loop else 0))

    def wait(self, engine, *names, lag=0, of=None, alone=False):
        if not self.known:
            return
        names_of, loops, _ = self.known
        loop = of if of is not None else self.loop
        if loop == "start":
            loop = None
        need = {}
        for name in names:
            if self.stream is not None and of is None and ":" not in name:
                name = f"{self.stream}:{name}"
            chan, k = names_of[(loop, name)]
            need[chan] = max(need.get(chan, 0), k)
        for chan, k in need.items():
            key = (engine, chan, loop, lag)
            if self.seen.get(key, -1) >= k:
                continue
            self.seen[key] = k
            value = k
            if loop:
                base, per, n = loops[(loop, chan)]
                if loop == self.loop:
                    value = self.i * per + (base + k - lag * per)
                else:
                    value = base + (n - 1) * per + k
            self.eng[engine].wait_ge(self.sem[chan], value)
            if alone:
                self.eng[engine].sem_inc(self.sem["aside"], 1)


def build(nc, known, a, out):
    V, A, PE, G, S = nc.vector, nc.scalar, nc.tensor, nc.gpsimd, nc.sync
    ctx = ExitStack()
    pr = Progress(nc, ctx, known)
    done, wait = pr.done, pr.wait
    pr.dma("aside")

    def sb(name, shape, dt=F32, c=ctx):
        return c.enter_context(nc.sbuf_tensor(name, shape, dt))

    bank = [ctx.enter_context(nc.psum_tensor(f"bank{i}", [P, T], F32)) for i in range(8)]

    def tt(o, x, y, op):
        return V.tensor_tensor(o, x, y, op)

    def ts(o, x, s1, s2, op0, op1=None):
        return V.tensor_scalar(o, x, s1, s2, op0, op1) if op1 is not None else V.tensor_scalar(o, x, s1, s2, op0)

    def stt(o, x, s, y, op0, op1):
        return V.scalar_tensor_tensor(out=o, in0=x, scalar=s, in1=y, op0=op0, op1=op1)

    def mm(o, l, r, start=True, stop=True):
        return PE.matmul(o, l, r, start=start, stop=stop)

    def load(dst, src, name):
        done(name, S.dma_start(dst, src), by=16)

    X = sb("X", [P, NB * NQ, D])
    XNT = sb("XNT", [P, NB, T])
    ST = sb("ST", [P, NB, T])
    cv = sb("cv", [P, NCV])
    ident = sb("ident", [P, P])
    iota = sb("iota", [P, NQ, NE])
    expo = sb("expo", [P, NQ])
    wox = sb("wox", [P, NG, D])
    M = {}
    shapes = {"l0_bw": (P, D), "l0_rw": (P, NE), "l0_wo": (P, D),
              "l1_b": (P, 32), "l1_wp1": (P, P), "l1_wp2": (P, NE), "l1_wo": (P, D), "l1_c": (32, D),
              "l1_bias": (P, 3 * NE), "l1_bp2": (P, NE),
              "l2_q": (P, 2 * D), "l2_k": (P, 64), "l2_v": (P, 32), "l2_gw": (P, NE), "l2_gb": (P, NQ * NE),
              "l2_eb": (NE, D), "l2_w": (P, NE * D),
              "den": (P, P), "l3_rw": (P, NE), "c5": (P, 3 * P), "c1": (P, 3 * 64), "c4": (P, 64),
              "m1_in": (P, 2 * D), "m1_ssm": (P, 32), "m1_out": (P, D), "m1_A": (32, 64),
              "m2_in": (P, 2 * D), "m2_ssm": (P, 32), "m2_out": (P, D), "m2_A": (32, 64)}
    for n, s in shapes.items():
        M[n] = sb(n, list(s))

    def col(c, n=P):
        return cv[0:n, c:c + 1]

    def flat(ap):
        return ap.rearrange("p a n -> p (a n)")

    pr.dma("in")
    load(X[:], a["x"].rearrange("b (q p) d -> p (b q) d", p=P), "in")
    load(cv[:], a["cv"], "in")
    load(ident[:], a["ident"], "in")
    load(iota[:], a["iota"].rearrange("p (q e) -> p q e", q=NQ), "in")
    for n in ("l0_bw", "l0_rw", "l0_wo"):
        load(M[n][:], a[n], "in")
    pr.names[(None, "in")] = ("in", pr.count["in"])

    def working(c, tag, names, ways):
        sets = []
        for k in range(ways):
            w = {n: sb(f"{n}_{k}_{tag}", [P, T], c=c) for n in names}
            for n, s in {"st": [P, NQ, 6], "mv": [P, NQ, 2], "rstd": [P, 2, NQ], "xn": [P, NQ, D], "xf": [P, T],
                         "lg": [P, NQ, NE], "mx": [P, NQ, 8], "ixf": [P, NQ, 2], "sel": [P, NQ, NE],
                         "sel2": [P, NQ, NE], "ee": [P, NQ, NE], "zz": [P, 4, NQ], "w8": [P, NQ, NE]}.items():
                w[n] = sb(f"{n}_{k}_{tag}", s, c=c)
            w["ix"] = sb(f"ix_{k}_{tag}", [P, NQ, 8], U32, c=c)
            w["B"] = bank[8 // ways * k:8 // ways * (k + 1)]
            sets.append(w)
        return sets

    def layer_norm(w, b, n, keep=None):
        V.sem_inc(pr.sem["aside"], 1)
        for q in range(NQ):
            last = V.bn_stats(w["st"][:, q, :], flat(X[:, bass.ds(b * NQ + q, 1), :]))
        done("DVE", last, f"{n}.stats")
        yield
        wait("DVE", f"{n}.stats", alone=True)
        for q in range(NQ):
            last = V.bn_aggr(w["mv"][:, q, :], w["st"][:, q, :])
        done("DVE", last, f"{n}.aggr")
        yield
        wait("POOL", f"{n}.aggr", alone=True)
        done("POOL", G.tensor_scalar(w["rstd"][:, 0, :], w["mv"][:, :, 1], LN_EPS, None, ALU.add), f"{n}.var")
        yield
        wait("POOL", f"{n}.var", alone=True)
        done("POOL", G.tensor_tensor(w["rstd"][:, 1, :], w["rstd"][:, 0, :], expo[:], ALU.pow), f"{n}.rstd")
        yield
        yield
        wait("DVE", f"{n}.rstd")
        for q in range(NQ):
            last = ts(w["xn"][:, q, :], flat(X[:, bass.ds(b * NQ + q, 1), :]),
                      w["mv"][:, q, 0:1], w["rstd"][:, 1, q:q + 1], ALU.subtract, ALU.mult)
        done("DVE", last, f"{n}.xn")
        yield
        wait("PE", f"{n}.xn")
        for q in range(NQ):
            last = PE.transpose(w["B"][0][:, q * P:(q + 1) * P], w["xn"][:, q, :], ident[:])
        done("PE", last, f"{n}.xnT")
        wait("ACT", f"{n}.xnT")
        done("ACT", A.copy(w["xf"][:], w["B"][0][:]), f"{n}.xf")
        if keep is not None:
            wait("POOL", f"{n}.xf")
            done("POOL", G.tensor_copy(flat(keep[:, bass.ds(b, 1), :]), w["xf"][:]), f"{n}.kept")
        yield

    def top_two(w, n, kind, lhs, weights, bias=None, dst=None, at=1):
        for q in range(NQ):
            last = mm(w["B"][at][:, q * NE:(q + 1) * NE], lhs(q), weights)
        done("PE", last, f"{n}.logits")
        wait("DVE", f"{n}.logits")
        src = w["B"][at][:, 0:NQ * NE].rearrange("p (q e) -> p q e", q=NQ)
        if bias is None:
            done("DVE", V.tensor_copy(w["lg"][:], src), f"{n}.lg")
        else:
            done("DVE", tt(w["lg"][:], src, bias, ALU.add), f"{n}.lg")
        yield
        wait("DVE", f"{n}.lg", alone=True)
        for q in range(NQ):
            last = V.max(w["mx"][:, q, :], w["lg"][:, q, :])
        done("DVE", last, f"{n}.mx")
        yield
        wait("DVE", f"{n}.mx", alone=True)
        for q in range(NQ):
            last = V.max_index(w["ix"][:, q, :], w["mx"][:, q, :], w["lg"][:, q, :])
        done("DVE", last, f"{n}.ix")
        ee, sel, sel2, zz = w["ee"], w["sel"], w["sel2"], w["zz"]
        done("DVE", tt(ee[:], w["lg"][:], w["mx"][:, :, 0:1].to_broadcast([P, NQ, NE]), ALU.subtract), f"{n}.shift")
        wait("DVE", f"{n}.ix")
        done("DVE", V.tensor_copy(w["ixf"][:], w["ix"][:, :, 0:2]), f"{n}.ixf")
        wait("ACT", f"{n}.shift")
        done("ACT", A.activation(ee[:], ee[:], ACT.Exp), f"{n}.exp")
        yield
        wait("DVE", f"{n}.ixf")
        tt(sel[:], iota[:], w["ixf"][:, :, 0:1].to_broadcast([P, NQ, NE]), ALU.is_equal)
        done("DVE", tt(sel2[:], iota[:], w["ixf"][:, :, 1:2].to_broadcast([P, NQ, NE]), ALU.is_equal), f"{n}.sel2")
        yield
        wait("DVE", f"{n}.sel2")
        done("DVE", tt(sel[:], sel[:], sel2[:], ALU.add), f"{n}.sel")
        yield
        wait("DVE", f"{n}.exp", f"{n}.sel")
        if kind != "masked":
            done("DVE", V.tensor_reduce(zz[:, 0, :], ee[:], AX_X, ALU.add), f"{n}.z0")
            yield
            wait("DVE", f"{n}.z0")
            done("DVE", V.reciprocal(zz[:, 1, :], zz[:, 0, :]), f"{n}.z1")
            yield
            wait("DVE", f"{n}.z1")
            done("DVE", tt(ee[:], ee[:], zz[:, 1, :].unsqueeze(2).to_broadcast([P, NQ, NE]), ALU.mult), f"{n}.p")
            yield
            wait("DVE", f"{n}.p")
        if kind == "probs":
            done("DVE", tt(dst, ee[:], sel[:], ALU.mult), f"{n}.w")
            yield
            return
        done("DVE", tt(ee[:], ee[:], sel[:], ALU.mult), f"{n}.ps")
        yield
        wait("DVE", f"{n}.ps")
        done("DVE", V.tensor_reduce(zz[:, 2, :], ee[:], AX_X, ALU.add), f"{n}.s0")
        yield
        wait("DVE", f"{n}.s0")
        if kind == "renormed":
            done("DVE", ts(zz[:, 2, :], zz[:, 2, :], 1e-9, None, ALU.add), f"{n}.s1")
            yield
            wait("DVE", f"{n}.s1")
        done("DVE", V.reciprocal(zz[:, 3, :], zz[:, 2, :]), f"{n}.s2")
        yield
        wait("DVE", f"{n}.s2")
        done("DVE", tt(dst, ee[:], zz[:, 3, :].unsqueeze(2).to_broadcast([P, NQ, NE]), ALU.mult), f"{n}.w")
        yield

    def turn_over(*names):
        for e in ("PE", "DVE", "ACT", "POOL", "SP"):
            wait(e, *names, alone=(e == "SP"))

    def x_tiles(b):
        return X[:, bass.ds(b * NQ, NQ), :]

    def tokens(ap):
        return ap.rearrange("p (q d) -> p q d", q=NQ)

    def update(w, b, n, s_fm, g_src, g_ready):
        for q in range(NQ):
            last = PE.transpose(w["B"][0][:, q * P:(q + 1) * P], s_fm[:, q * P:(q + 1) * P], ident[:])
        done("PE", last, f"{n}.sT")
        wait("ACT", *g_ready)
        done("ACT", A.activation(w["sg"][:], g_src, ACT.Silu), f"{n}.sg")
        yield
        wait("DVE", f"{n}.sT", f"{n}.sg")
        done("DVE", tt(w["sg"][:], w["sg"][:], w["B"][0][:], ALU.mult), f"{n}.sx")
        yield
        wait("DVE", f"{n}.sx")
        done("DVE", tt(x_tiles(b), x_tiles(b), tokens(w["sg"][:]), ALU.add), f"{n}.x")
        yield

    l1s = ExitStack()
    l1w = sb("l1w", [P, NE, T], c=l1s)
    ph0 = ExitStack()
    H = ST
    WA = sb("WA", [P, NE, T], c=ph0)
    WB = sb("WB", [P, NE, T], c=ph0)
    GT = sb("GT", [P, NB * NQ, D], c=ph0)
    BX = sb("BX", [P, NB, T], c=ph0)
    cw = sb("cw", [P, NB * NQ, NE], c=ph0)
    decay = sb("decay", [P, 2], c=ph0)
    HG = sb("HG", [P, 2, HC, T], c=ph0)
    acc = sb("acc", [P, NQ, D], c=ph0)
    cwb = sb("cwb", [P, NQ, NE], c=ph0)
    bxs = sb("bxs", [P, STEPS, NB], c=ph0)
    hs0 = sb("hs0", [P, STEPS + 1, NB], c=ph0)
    ub = sb("ub", [P, NB], c=ph0)
    sets0 = working(ph0, "l0", ("sg", "s"), 4)

    pr.dma("w0")
    load(WA[:], a["l0_w1"], "w0")
    load(WB[:], a["l0_w2"], "w0")
    pr.names[(None, "w0")] = ("w0", pr.count["w0"])
    pr.dma("w1")
    done("DVE", V.memset(wox[:], 0.0), "wox0")
    for n in shapes:
        if not n.startswith("l0"):
            load(M[n][:], a[n], "w1")
    load(l1w[:], a["l1_w"], "w1")
    wait("SP", "wox0", of="start")
    for r in range(4):
        load(wox[32 * r:32 * r + HD, :, :], a["l2_wo"].rearrange("(g r j) o -> r j g o", g=NG, r=4)[r], "w1")
    pr.names[(None, "w1")] = ("w1", pr.count["w1"])

    for e in ("PE", "DVE", "ACT", "POOL"):
        wait(e, "in", of="start")
    done("POOL", G.memset(expo[:], -0.5), "expo")
    wait("POOL", "expo")
    done("DVE", ts(decay[:, 0:1], col(C_L0A), 10.0, None, ALU.min), "amin")
    done("DVE", V.memset(hs0[:, STEPS, :], 0.0), "h_init")
    wait("ACT", "amin")
    done("ACT", A.activation(decay[:, 1:2], decay[:, 0:1], ACT.Exp, scale=-1.0), "decay")
    wait("DVE", "decay")

    def prepare(w, b):
        yield from layer_norm(w, b, "n", keep=XNT)
        wait("PE", "n.xf")
        done("PE", mm(w["B"][0][:], M["l0_bw"][:], w["xf"][:]), "bx")
        wait("ACT", "bx")
        done("ACT", A.copy(flat(BX[:, bass.ds(b, 1), :]), w["B"][0][:]), "bx.copied")
        yield from top_two(w, "r", "renormed", lambda q: w["xf"][:, q * P:(q + 1) * P], M["l0_rw"][:],
                           dst=cw[:, bass.ds(b * NQ, NQ), :])
        turn_over("r.w", "n.kept", "bx.copied")

    with nc.Fori(0, NB // 4) as i:
        pr.enter("prep", i, NB // 4)
        pr.interleave(*[prepare(sets0[k], i * 4 + k) for k in range(4)])
        pr.leave()

    wait("PE", "w0", of="start")
    wait("PE", "3:n.kept", "3:bx.copied", "3:r.lg", of="prep")
    chain_u, chain_h = (ctx.enter_context(nc.semaphore(n)) for n in ("chain_u", "chain_h"))
    with nc.Fori(0, NB) as b:
        pr.enter("moe0", b, NB)
        wait("POOL", "3:bx.copied", of="prep")
        wait("POOL", "h.kept", lag=1)
        done("POOL", G.tensor_copy(bxs[:], BX[:, :, bass.ds(b * STEPS, STEPS)].rearrange("p n t -> p t n")), "bxs")
        wait("DVE", "3:r.w", of="prep")
        wait("DVE", f"acc{NE - 1}.{NQ - 1}", lag=1)
        done("DVE", V.tensor_copy(cwb[:], cw[:, bass.ds(b * NQ, NQ), :]), "cwb")
        wait("DVE", "cwb")
        wait("ACT", "h.kept", lag=1, alone=True)
        A.sem_clear(chain_u)
        A.sem_clear(chain_h)
        done("ACT", A.copy(hs0[:, 0, :], hs0[:, STEPS, :]), "h.carry")

        def step(s):
            if s == 0:
                wait("DVE", "bxs", "h.carry")
            else:
                V.wait_ge(chain_h, s)
            stt(ub[:], hs0[:, s, :], decay[:, 1:2], bxs[:, s, :], ALU.mult, ALU.add).then_inc(chain_u, 1)
            A.wait_ge(chain_u, s + 1)
            A.activation(hs0[:, s + 1, :], ub[:], ACT.Tanh).then_inc(chain_h, 1)

        def accumulate(e, q):
            if q == 0:
                wait("DVE", f"y{e}")
                if e == 0:
                    wait("DVE", "acc.kept", lag=1)
            ys = bank[4 + e % 2][:, q * D:(q + 1) * D]
            w = cwb[:, q, e:e + 1]
            if e == 0:
                op = ts(acc[:, q, :], ys, w, None, ALU.mult)
            else:
                wait("DVE", f"acc{e - 1}.{q}")
                op = stt(acc[:, q, :], ys, w, acc[:, q, :], ALU.mult, ALU.add)
            done("DVE", op, f"acc{e}.{q}")

        def down(e):
            wait("PE", f"g{e}.{HC - 1}")
            if e >= 2:
                wait("PE", f"acc{e - 2}.{NQ - 1}")
            else:
                wait("PE", f"acc{NE - 2 + e}.{NQ - 1}", lag=1)
            for q in range(NQ):
                for m in range(HC):
                    last = mm(bank[4 + e % 2][:, q * D:(q + 1) * D], HG[:, e % 2, m, q * P:(q + 1) * P],
                              WB[:, e, m * D:(m + 1) * D], start=(m == 0), stop=(m == HC - 1))
            done("PE", last, f"y{e}")

        per = STEPS // (NE * HC)
        for e in range(NE):
            for m in range(HC):
                if e >= 1:
                    wait("PE", f"g{e - 1}.{m}")
                else:
                    wait("PE", f"g{NE - 1}.{m}", lag=1)
                done("PE", mm(bank[m][:], WA[:, e, m * P:(m + 1) * P],
                              flat(XNT[:, bass.ds(b, 1), :])), f"x{e}.{m}")
            if e >= 1:
                down(e - 1)
            for m in range(HC):
                wait("ACT", f"x{e}.{m}")
                if m == 0:
                    if e >= 2:
                        wait("ACT", f"y{e - 2}")
                    else:
                        wait("ACT", f"y{NE - 2 + e}", lag=1)
                done("ACT", A.activation(HG[:, e % 2, m, :], bank[m][:], ACT.Gelu), f"g{e}.{m}")
                for s in range(per):
                    step((e * HC + m) * per + s)
                if e >= 2:
                    accumulate(e - 2, m)
        down(NE - 1)
        for q in range(NQ):
            accumulate(NE - 2, q)
        for q in range(NQ):
            accumulate(NE - 1, q)
        wait("POOL", "h.carry", alone=True)
        G.wait_ge(chain_h, STEPS)
        done("POOL", G.tensor_copy(H[:, :, bass.ds(b * STEPS, STEPS)],
                                   hs0[:, 1:STEPS + 1, :].rearrange("p t n -> p n t")), "h.kept")
        wait("POOL", f"acc{NE - 1}.{NQ - 1}")
        done("POOL", G.tensor_copy(GT[:, bass.ds(b * NQ, NQ), :], acc[:]), "acc.kept")
        pr.leave()

    def finish0(w, b):
        done("PE", mm(w["B"][1][:], M["l0_wo"][:], flat(H[:, bass.ds(b, 1), :])), "o")
        wait("DVE", "o")
        done("DVE", ts(w["s"][:], w["B"][1][:], col(C_L0BO), None, ALU.add), "s")
        yield
        wait("PE", "s")
        yield from update(w, b, "u", w["s"], GT[:, bass.ds(b * NQ, NQ), :].rearrange("p q d -> p (q d)"), ())
        turn_over("u.x")

    wait("PE", "h.kept", "acc.kept", of="moe0")
    wait("ACT", "acc.kept", of="moe0")
    with nc.Fori(0, NB // 4) as i:
        pr.enter("fin0", i, NB // 4)
        pr.interleave(*[finish0(sets0[k], i * 4 + k) for k in range(4)])
        pr.leave()
    ph0.close()
    pr.fence("fin0")
    for e in ("PE", "DVE", "ACT", "POOL"):
        wait(e, "w1", of="start")

    ph1 = ExitStack()
    sets1 = working(ph1, "l1", ("sT", "t1", "t2", "g0", "g1", "wsel", "hpr"), 4)
    for k in range(4):
        for n, s in {"b3": [P, 3], "hp": [P, 2], "oh": [P, 40]}.items():
            sets1[k][n] = sb(f"{n}_{k}", s, c=ph1)
    abar = sb("abar", [32, 2], c=ph1)
    ab = sb("ab", [32, T], c=ph1)
    done("DVE", V.memset(ab[:], 1.0), "ones")
    done("ACT", A.activation(abar[:, 0:1], col(C_L1A, 32), ACT.Exp), "ab0")
    wait("ACT", "ab0")
    done("ACT", A.activation(abar[:, 1:2], abar[:, 0:1], ACT.Exp, scale=-1.0), "ab1")
    wait("DVE", "ab1", "ones")
    done("DVE", ts(ab[:], ab[:], abar[:, 1:2], None, ALU.mult), "ab")
    wait("DVE", "ab")

    def layer1(w, b):
        B, xf, sT, t1, oh, b3, wsel = w["B"], w["xf"], w["sT"], w["t1"], w["oh"], w["b3"], w["wsel"]
        yield from layer_norm(w, b, "n")
        wait("PE", "n.xf")
        done("PE", mm(B[1][0:32, :], M["l1_b"][:], xf[:]), "bx")
        done("PE", mm(B[0][:, 0:1], M["l1_wp1"][:], xf[:, T - 1:T]), "p1")
        wait("ACT", "p1")
        done("ACT", A.activation(w["hp"][:, 0:1], B[0][:, 0:1], ACT.Gelu, bias=col(C_BP1)), "hp")
        wait("DVE", "bx")
        done("DVE", V.tensor_tensor_scan(t1[0:32, :], ab[:], B[1][0:32, :], 0.0, ALU.mult, ALU.add), "h")
        yield
        wait("DVE", "hp")
        done("DVE", V.tensor_copy(w["hpr"][:, 0:P], w["hp"][:, 0:1].to_broadcast([P, P])), "hpr")
        wait("PE", "hpr")
        done("PE", mm(B[0][:, 8:8 + NE], w["hpr"][:, 0:P], M["l1_wp2"][:]), "p2")
        wait("PE", "h")
        done("PE", mm(B[1][:], M["l1_c"][:], t1[0:32, :]), "y")
        yield
        wait("DVE", "y")
        done("DVE", stt(sT[:], xf[:], col(C_L1D), B[1][:], ALU.mult, ALU.add), "s")
        yield
        wait("DVE", "p2")
        done("DVE", tt(oh[:, 0:8], B[0][:, 8:8 + NE], M["l1_bp2"][:], ALU.add), "lg1")
        yield
        wait("DVE", "lg1", alone=True)
        done("DVE", V.max(oh[:, 8:16], oh[:, 0:8]), "mx1")
        yield
        wait("DVE", "mx1", alone=True)
        done("DVE", V.max_index(w["ix"][:, 0, :], oh[:, 8:16], oh[:, 0:8]), "ix1")
        yield
        wait("DVE", "ix1")
        done("DVE", V.tensor_copy(oh[:, 16:17], w["ix"][:, 0, 0:1]), "ixf1")
        yield
        wait("DVE", "ixf1")
        done("DVE", ts(oh[:, 24:32], iota[:, 0, :], oh[:, 16:17], None, ALU.is_equal), "oh1")
        yield
        wait("DVE", "oh1")
        done("DVE", ts(wsel[:], l1w[:, 0, :], oh[:, 24:25], None, ALU.mult), "w.0")
        yield
        for e in range(1, NE):
            wait("DVE", f"w.{e - 1}")
            done("DVE", stt(wsel[:], l1w[:, e, :], oh[:, 24 + e:25 + e], wsel[:], ALU.mult, ALU.add), f"w.{e}")
            yield
        bt = w["t2"][:, 0:3 * NE].rearrange("p (c e) -> p c e", c=3)
        done("DVE", tt(bt, M["l1_bias"][:].rearrange("p (c e) -> p c e", c=3),
                       oh[:, 24:32].unsqueeze(1).to_broadcast([P, 3, NE]), ALU.mult), "bt")
        yield
        wait("DVE", "bt")
        done("DVE", V.tensor_reduce(b3[:], bt, AX_X, ALU.add), "b3")
        wait("PE", f"w.{NE - 1}")
        for m in range(2):
            last = mm(B[m][:], wsel[:, m * P:(m + 1) * P], xf[:])
        done("PE", last, "f1")
        wait("ACT", "f1", "b3")
        for m in range(2):
            last = A.activation(w[f"g{m}"][:], B[m][:], ACT.Gelu, bias=b3[:, m:m + 1])
        done("ACT", last, "g")
        wait("PE", "g")
        for m in range(2):
            last = mm(B[0][:], wsel[:, 256 + m * P:256 + (m + 1) * P], w[f"g{m}"][:], start=(m == 0), stop=(m == 1))
        done("PE", last, "f2")
        wait("DVE", "f2")
        done("DVE", ts(t1[:], B[0][:], b3[:, 2:3], None, ALU.add), "r")
        yield
        wait("PE", "r")
        done("PE", mm(B[1][:], M["l1_wo"][:], t1[:]), "f3")
        wait("DVE", "f3")
        done("DVE", ts(t1[:], B[1][:], col(C_L1BO), 0.3, ALU.add, ALU.mult), "f4")
        yield
        wait("DVE", "f4")
        done("DVE", tt(t1[:], t1[:], xf[:], ALU.add), "f5")
        wait("ACT", "f5")
        done("ACT", A.activation(t1[:], t1[:], ACT.Silu), "sg")
        yield
        wait("DVE", "sg", "s")
        done("DVE", tt(sT[:], sT[:], t1[:], ALU.mult), "p")
        yield
        wait("PE", "p")
        for q in range(NQ):
            last = PE.transpose(B[0][:, q * P:(q + 1) * P], sT[:, q * P:(q + 1) * P], ident[:])
        done("PE", last, "pT")
        wait("DVE", "pT")
        done("DVE", tt(x_tiles(b), x_tiles(b), tokens(B[0][:]), ALU.add), "x")
        yield
        turn_over("x")

    with nc.Fori(0, NB // 4) as i:
        pr.enter("layer1", i, NB // 4)
        pr.interleave(*[layer1(sets1[k], i * 4 + k) for k in range(4)])
        pr.leave()
    ph1.close()
    l1s.close()
    pr.fence("layer1")

    ph2 = ExitStack()
    cosq = sb("cosq", [P, 2, T], c=ph2)
    cosk = sb("cosk", [32, 2, T], c=ph2)
    selq = sb("selq", [P, NG, 2, P], F32R, c=ph2)
    selk = sb("selk", [33, NG, 2, P], F32R, c=ph2)
    negid = sb("negid", [P, P], F32R, c=ph2)
    pr.dma("w2")
    load(cosq[:], a["rope_q"].rearrange("p (c n) -> p c n", c=2), "w2")
    load(cosk[:], a["rope_k"].rearrange("p (c n) -> p c n", c=2), "w2")
    ao = sb("ao", [P, NG, T], c=ph2)
    ssel = ao[:].rearrange("p (c x) n -> p c (x n)", c=2)
    load(ssel[:, 0, :], a["selq"], "w2")
    load(ssel[0:33, 1, :], a["selk"], "w2")
    pr.names[(None, "w2")] = ("w2", pr.count["w2"])
    both = working(ph2, "l2", ("t1", "t2", "t3", "a1", "a2"), 1)[0]
    both["qhl"] = sb("qhl", [P, 2, T], F32R, c=ph2)
    both["khl"] = sb("khl", [33, 2, T], F32R, c=ph2)
    both["qmax"] = sb("qmax", [P, NQ, NG, P], F32R, c=ph2)
    both["ex"] = sb("ex", [P, 4, T], c=ph2)
    both["ao"] = ao
    both["Qp"] = sb("Qp", [P, 2, 4, T], F32R, c=ph2)
    both["Kp"] = sb("Kp", [P, 2, 4, T], F32R, c=ph2)
    V.memset(both["khl"][32:33, :, :].bitcast(F32), 1.0)
    for n in ("qmax", "Qp", "Kp"):
        V.memset(both[n][:].bitcast(F32), 0.0)
    sets2 = [dict(both, B=bank[4 * k:4 * k + 4]) for k in range(2)]
    for k in range(2):
        w = sets2[k]
        w["KS"] = sb(f"KS_{k}", [P, NG, T], F32R, c=ph2)
        w["QS"] = sb(f"QS_{k}", [P, NG, T], F32R, c=ph2)
        w["VA"] = sb(f"VA_{k}", [P, NQ, NG, 32], c=ph2)
        done("DVE", V.memset(w["VA"][:], 0.0), f"k0.{k}")
    wait("DVE", "k0.1")
    for k in range(2):
        last = V.memset(sets2[k]["VA"][:, :, :, HD:HD + 1], 1.0)
    done("DVE", ts(negid[:], ident[:], -1.0, None, ALU.mult), "k1")
    wait("DVE", "w2", of="start")
    V.tensor_copy(selq[:].rearrange("p g c n -> p (g c n)"), ssel[:, 0, :])
    done("DVE", V.tensor_copy(selk[:].rearrange("p g c n -> p (g c n)"), ssel[0:33, 1, :]), "sel")
    wait("PE", "sel")
    wait("SP", "sel")
    wait("DVE", "sel")

    for n in ("qp0", "qp1", "kp0", "kp1"):
        pr.dma(n)

    def spread(dst, src, g, name, *before, called=None):
        wait("SP", *before)
        for r in range(4):
            rows = slice(32 * r, 32 * r + 32)
            done(f"{name}{g % 2}", S.dma_start(dst[rows, g % 2, r, :].bitcast(F32), src[rows, g, :].bitcast(F32)),
                 (called or f"{name}.{g}") if r == 3 else None, by=16)

    def scale_maxima(w, b):
        B, xf, t1, t2, t3 = w["B"], w["xf"], w["t1"], w["t2"], w["t3"]
        QS, KS, VA = w["QS"], w["KS"], w["VA"]
        yield from layer_norm(w, b, "n", keep=XNT)
        wait("PE", "n.xf")
        for nm, mat, wt, tab, n in (("q", "l2_q", w["qhl"], cosq, P), ("k", "l2_k", w["khl"], cosk, 32)):
            mm(B[1][0:n, :], M[mat][:, 0:n], xf[:])
            done("PE", mm(B[2][0:n, :], M[mat][:, n:2 * n], xf[:]), nm)
            yield
            wait("DVE", nm)
            tt(t1[0:n, :], B[1][0:n, :], tab[:, 0, :], ALU.mult)
            done("DVE", tt(t2[0:n, :], B[2][0:n, :], tab[:, 1, :], ALU.mult), f"{nm}1")
            yield
            yield
            wait("DVE", f"{nm}1")
            wait("PE", f"{nm}1")
            done("DVE", tt(t3[0:n, :], t1[0:n, :], t2[0:n, :], ALU.add), f"{nm}2")
            yield
            wait("DVE", f"{nm}2")
            done("DVE", V.tensor_copy(wt[0:n, 0, :], t3[0:n, :]), f"{nm}3")
            yield
            wait("DVE", f"{nm}3")
            done("DVE", tt(wt[0:n, 1, :], t3[0:n, :], wt[0:n, 0, :].bitcast(F32), ALU.subtract), f"{nm}hl")
            yield
            wait("DVE", f"{nm}hl")
        for q in range(NQ):
            last = mm(B[3][:, q * 32:(q + 1) * 32], xf[:, q * P:(q + 1) * P], M["l2_v"][:])
        done("PE", last, "v")
        wait("ACT", "v")
        done("ACT", A.copy(VA[:, :, :, 0:HD],
                           B[3][:, 0:P].rearrange("p (q g d) -> p q g d", q=NQ, g=NG)), "va")
        yield
        wait("PE", "qhl", "khl", "va")
        k = 0
        for g in range(NG):
            for sel, hl, dst, n in ((selq, w["qhl"], QS, P), (selk, w["khl"], KS, 33)):
                if k >= 4:
                    wait("PE", f"st{k - 4}")
                for c in range(2):
                    last = mm(B[k % 4][:], sel[0:n, g, c, :], hl[0:n, c, :], start=(c == 0), stop=(c == 1))
                done("PE", last, f"sel{k}")
                wait("ACT", f"sel{k}")
                done("ACT", A.copy(dst[:, g, :], B[k % 4][:]), f"st{k}")
                k += 1
            yield
        wait("PE", f"st{k - 1}")
        n = 0
        spread(w["Qp"], QS, 0, "qp", f"st{k - 1}")
        for _ in range(7):
            yield
        for g in range(NG):
            if g + 1 < NG:
                spread(w["Qp"], QS, g + 1, "qp", *((f"sc{n - 1}",) if g else ()))
            wait("PE", f"qp.{g}")
            for q in range(NQ):
                for r in range(4):
                    if n >= 4:
                        wait("PE", f"mx{n - 4}")
                    done("PE", mm(B[r][:], w["Qp"][:, g % 2, r, q * P:(q + 1) * P], KS[:, g, :]), f"sc{n}")
                    wait("DVE", f"sc{n}")
                    done("DVE", V.tensor_reduce(w["qmax"][:, q, g, 32 * r + 24:32 * r + 25], B[r][:], AX_X,
                                                ALU.max), f"mx{n}")
                    n += 1
                    if r:
                        yield
        for _ in range(4):
            yield
        wait("PE", f"mx{n - 1}")
        for g in range(NG):
            for c in range(2):
                mm(B[g][:], selq[:, g, c, :], w["qhl"][:, c, :], start=(c == 0), stop=False)
            for q in range(NQ):
                last = mm(B[g][:, q * P:(q + 1) * P], w["qmax"][:, q, g, :], negid[:], start=False, stop=(q == NQ - 1))
            done("PE", last, f"mrow{g}")
            wait("ACT", f"mrow{g}")
            done("ACT", A.copy(QS[:, g, :], B[g][:]), f"qe{g}")
            yield
        turn_over(f"qe{NG - 1}", "n.kept")

    def attend(w, b, way, more=True):
        B, t1, t2 = w["B"], w["a1"], w["a2"]
        QS, KS, VA, ex, ao = w["QS"], w["KS"], w["VA"], w["ex"], w["ao"]
        tiles = [(g, r, kt) for g in range(NG) for r in range(4) for kt in range(NQ)]

        def scores(n):
            g, r, kt = tiles[n]
            if n >= 2:
                wait("PE", f"ex{n - 2}")
            if r == 0 and kt == 0:
                if g + 1 < NG:
                    spread(w["Kp"], KS, g + 1, "kp", *((f"se{n - 1}",) if g else ()))
                elif more:
                    spread(w["Kp"], sets2[1 - way]["KS"], 0, "kp", f"se{n - 1}", f"{1 - way}:st{2 * NG - 1}",
                           called="kp.next")
                if g:
                    wait("PE", f"kp.{g}")
            done("PE", mm(B[n % 2][:], w["Kp"][:, g % 2, r, kt * P:(kt + 1) * P], QS[:, g, :]), f"se{n}")
            wait("ACT", f"se{n}")
            if n >= 4:
                wait("ACT", f"pv{n - 4}")
            done("ACT", A.activation(ex[:, n % 4, :], B[n % 2][:], ACT.Exp, scale=SM_SCALE), f"ex{n}")

        scores(0)
        for n, (g, r, kt) in enumerate(tiles):
            if n + 1 < len(tiles):
                scores(n + 1)
            wait("PE", f"ex{n}")
            if r == 0 and kt == 0 and g >= 1:
                wait("PE", f"o{g - 1}")
            done("PE", mm(B[2][32 * r:32 * r + 32, :], VA[:, kt, g, :], ex[:, n % 4, :],
                          start=(kt == 0), stop=(kt == NQ - 1)), f"pv{n}")
            if r == 3 and kt == NQ - 1:
                wait("ACT", f"pv{n}")
                if g >= 1:
                    wait("ACT", f"on{g - 1}")
                done("ACT", A.copy(t1[:], B[2][:]), f"o{g}")
            yield
            if (r == 0 and kt == 2 and g >= 1) or n == len(tiles) - 1:
                k = g - 1 if n < len(tiles) - 1 else g
                wait("PE", f"o{k}")
                if k >= 1:
                    wait("PE", f"rec{k - 1}")
                done("PE", mm(B[3][:], M["den"][:], t1[:]), f"d{k}")
                wait("DVE", f"d{k}")
                if k >= 1:
                    wait("DVE", f"on{k - 1}")
                done("DVE", V.reciprocal(t2[:], B[3][:]), f"rec{k}")
                yield
                yield
                wait("DVE", f"rec{k}")
                done("DVE", tt(ao[:, k, :], t1[:], t2[:], ALU.mult), f"on{k}")
        for _ in range(3):
            yield
        wait("PE", f"on{NG - 1}")
        for g in range(NG):
            last = mm(B[3][:], wox[:, g, :], ao[:, g, :], start=(g == 0), stop=(g == NG - 1))
        done("PE", last, "wo")
        wait("ACT", "wo")
        done("ACT", A.copy(flat(ST[:, bass.ds(b, 1), :]), B[3][:]), "s")
        yield
        turn_over("s", *(("kp.next",) if more else ()))

    def first_maxima():
        yield from scale_maxima(sets2[0], 0)
        spread(sets2[0]["Kp"], sets2[0]["KS"], 0, "kp")
        turn_over("kp.0")

    pr.enter("attn first", 0, 1)
    pr.interleave((0, first_maxima()))
    pr.leave()
    pr.fence("attn first")
    with nc.Fori(0, NB // 2 - 1) as i:
        pr.enter("attn", i, NB // 2 - 1)
        pr.interleave((0, attend(sets2[0], i * 2, 0)), (1, scale_maxima(sets2[1], i * 2 + 1)))
        pr.interleave((1, attend(sets2[1], i * 2 + 1, 1)), (0, scale_maxima(sets2[0], i * 2 + 2)))
        pr.leave()
    pr.fence("attn")
    pr.enter("attn last", 0, 1)
    pr.interleave((0, attend(sets2[0], NB - 2, 0)), (1, scale_maxima(sets2[1], NB - 1)))
    pr.interleave((1, attend(sets2[1], NB - 1, 1, more=False)))
    pr.leave()
    ph2.close()
    pr.fence("attn last")

    W3 = [sb(n, [P, NE, T]) for n in ("wv", "w", "w1")]
    pr.dma("w3")
    for wt, n in zip(W3, ("l3_wv", "l3_w", "l3_w1")):
        load(wt[:], a[n], "w3")
    pr.names[(None, "w3")] = ("w3", pr.count["w3"])
    ph3 = ExitStack()
    sets3 = working(ph3, "l3", ("sg", "sT", "gt"), 4)
    for k in range(4):
        sets3[k]["w8T"] = sb(f"w8T_{k}", [NE, T], c=ph3)

    def mixture2(w, b):
        B, xf = w["B"], w["xf"]
        done("ACT", A.copy(xf[:], flat(XNT[:, bass.ds(b, 1), :])), "xf")
        wait("PE", "xf")
        yield from top_two(w, "r", "masked", lambda q: xf[:, q * P:(q + 1) * P], M["l2_gw"][:],
                           bias=M["l2_gb"][:].rearrange("p (q e) -> p q e", q=NQ), dst=w["w8"][:])
        wait("PE", "r.w")
        for q in range(NQ):
            last = PE.transpose(B[0][0:NE, q * P:(q + 1) * P], w["w8"][:, q, :], ident[:])
        done("PE", last, "w8T")
        wait("ACT", "w8T")
        done("ACT", A.copy(w["w8T"][:], B[0][0:NE, :]), "w8")
        yield
        wait("PE", "w8")
        for q in range(NQ):
            last = mm(B[1][:, q * D:(q + 1) * D], w["w8T"][:, q * P:(q + 1) * P], M["l2_eb"][:])
        done("PE", last, "eb")
        wait("ACT", "eb")
        done("ACT", A.copy(w["gt"][:], B[1][:]), "gt")
        yield
        wait("DVE", "gt")
        wait("PE", "gt")
        for k in range(2 * NQ):
            q, h = k // 2, k % 2
            if k >= 2:
                wait("PE", f"a{k - 2}.3")
            bk = B[k % 2]
            done("PE", mm(bk[:], xf[:, q * P:(q + 1) * P], M["l2_w"][:, h * T:(h + 1) * T]), f"e{k}")
            for e in range(4):
                if e == 0:
                    wait("DVE", f"e{k}")
                    if h:
                        wait("DVE", f"a{k - 1}.3")
                else:
                    wait("DVE", f"a{k}.{e - 1}")
                gq = tokens(w["gt"][:])[:, q, :]
                done("DVE", stt(gq, bk[:, e * D:(e + 1) * D], w["w8"][:, q, 4 * h + e:4 * h + e + 1], gq,
                                ALU.mult, ALU.add), f"a{k}.{e}")
                yield
        done("ACT", A.copy(w["sT"][:], flat(ST[:, bass.ds(b, 1), :])), "s")
        wait("PE", "s", "a7.3")
        yield from update(w, b, "u", w["sT"], w["gt"][:], ("a7.3",))
        turn_over("u.x")

    with nc.Fori(0, NB // 4) as i:
        pr.enter("mix2", i, NB // 4)
        pr.interleave(*[mixture2(sets3[k], i * 4 + k) for k in range(4)])
        pr.leave()
    ph3.close()
    pr.fence("mix2")

    ph4 = ExitStack()
    CH = T // 4
    w4 = working(ph4, "l4", ("t1", "u", "gs", "xres"), 1)[0]
    w4["B"] = bank[0:4]
    w4["pad"] = sb("pad", [P, T + 4], c=ph4)
    w4["cpad"] = sb("cpad", [P, T + 2], c=ph4)
    w4["hx"] = sb("hx", [P, CH], c=ph4)
    w4["he"] = sb("he", [32, 2, CH + 1], c=ph4)
    w4["hf"] = sb("hf", [P, CH], c=ph4)
    V.memset(w4["pad"][:], 0.0)
    V.memset(w4["cpad"][:], 0.0)
    V.memset(w4["he"][:], 0.0)
    done("DVE", V.memset(w4["t1"][:], 1.0), "ones4")
    wait("DVE", "ones4")

    NLV = 9
    pw = [sb(f"pw{m}", [32, NLV, 2, 32], c=ph4) for m in range(2)]
    blk = [sb(f"blk{m}", [P, P], c=ph4) for m in range(2)]
    car = [sb(f"car{m}", [32, P], c=ph4) for m in range(2)]
    cst = [sb(f"cst{m}", [P, P], c=ph4) for m in range(2)]

    def powers(m):
        B = bank[4 * m:4 * m + 4]
        done("DVE", V.tensor_copy(pw[m][:, 0, :, :], M[f"m{m + 1}_A"][:].rearrange("p (c n) -> p c n", c=2)), "pw0")
        yield
        for k in range(1, NLV):
            wait("PE", f"pw{k - 1}")
            mm(B[0][0:32, 0:32], pw[m][:, k - 1, 1, :], pw[m][:, k - 1, 0, :])
            done("PE", mm(B[0][0:32, 32:64], pw[m][:, k - 1, 0, :], pw[m][:, k - 1, 1, :]), f"sq{k}")
            wait("DVE", f"sq{k}")
            done("DVE", V.tensor_copy(pw[m][:, k, :, :],
                                      B[0][0:32, 0:64].rearrange("p (c n) -> p c n", c=2)), f"pw{k}")
            yield
        done("DVE", V.tensor_copy(car[m][:, 0:32], pw[m][:, 0, 1, :]), "car0")
        for k in range(1, 4):
            wait("PE", f"car{k - 1}")
            done("PE", mm(B[0][0:32, 0:32], pw[m][:, 0, 0, :], car[m][:, 32 * (k - 1):32 * k]), f"cm{k}")
            wait("DVE", f"cm{k}")
            done("DVE", V.tensor_copy(car[m][:, 32 * k:32 * k + 32], B[0][0:32, 0:32]), f"car{k}")
            yield
        done("DVE", V.memset(blk[m][:], 0.0), "blk0")
        wait("PE", "car3")
        for s in range(4):
            for t in range(s, 4):
                src = ident[0:32, 0:32] if t == s else car[m][:, 32 * (t - s - 1):32 * (t - s)]
                last = mm(B[1][32 * s:32 * s + 32, 32 * t:32 * t + 32], ident[0:32, 0:32], src)
        done("PE", last, "bm")
        wait("DVE", "bm", "blk0")
        for s in range(4):
            V.tensor_copy(blk[m][32 * s:32 * s + 32, 32 * s:P], B[1][32 * s:32 * s + 32, 32 * s:P])
        done("DVE", ts(cst[m][:], w4["t1"][:, 0:P], col(C_M[m] + C_CV), None, ALU.mult), "cst")
        wait("PE", "cst")
        wait("ACT", "cst")
        wait("DVE", "cst")
        yield

    pr.interleave(*[powers(m) for m in range(2)])

    def mamba(w, m, n, src, dst, dst_name):
        B, t1, u, gs, pad, hx, he, hf = (w[x] for x in ("B", "t1", "u", "gs", "pad", "hx", "he", "hf"))
        c = C_M[m]
        w_in, w_out, w_ssm = M[f"m{m + 1}_in"], M[f"m{m + 1}_out"], M[f"m{m + 1}_ssm"]
        done("PE", mm(B[1][:], w_in[:, 0:D], src), f"{n}.xs")
        done("PE", mm(B[2][:], w_in[:, D:2 * D], src), f"{n}.gate")
        wait("ACT", f"{n}.xs")
        done("ACT", A.activation(pad[:, 3:T + 3], B[1][:], ACT.Identity, bias=col(c + C_INX)), f"{n}.pad")
        wait("ACT", f"{n}.gate")
        done("ACT", A.activation(gs[:], B[2][:], ACT.Silu, bias=col(c + C_ING)), f"{n}.gs")
        yield
        wait("DVE", f"{n}.pad")
        done("DVE", ts(t1[:], pad[:, 0:T], col(c + C_CVW), None, ALU.mult), f"{n}.cv0")
        yield
        for j in range(1, 4):
            wait("DVE", f"{n}.cv{j - 1}")
            done("DVE", stt(t1[:], pad[:, j:j + T], col(c + C_CVW + j), t1[:], ALU.mult, ALU.add), f"{n}.cv{j}")
            yield
        wait("ACT", f"{n}.cv3")
        done("ACT", A.activation(u[:], t1[:], ACT.Silu, bias=col(c + C_CVB)), f"{n}.u")
        yield
        wait("PE", f"{n}.u")
        uv = u[:].rearrange("p (c t) -> p t c", t=4)
        for t in range(4):
            last = mm(B[3][32 * t:32 * t + 32, 0:CH], w_ssm[:], uv[:, t, :])
        done("PE", last, f"{n}.ssm")
        wait("DVE", f"{n}.ssm")
        done("DVE", ts(hx[:], B[3][:, 0:CH], col(c + C_SSB), col(c + C_BV), ALU.add, ALU.mult), f"{n}.hx")
        yield
        wait("PE", f"{n}.hx")
        done("PE", mm(B[3][0:32, P:2 * P], blk[m][:, 96:P], hx[:]), f"{n}.e")
        wait("DVE", f"{n}.e")
        done("DVE", V.tensor_copy(he[:, 0, 1:CH + 1], B[3][0:32, P:2 * P]), f"{n}.he")
        yield
        cur = f"{n}.he"
        lv = 0
        while (1 << lv) < CH:
            o = 1 << lv
            wait("PE", cur, alone=True)
            done("PE", mm(B[3][0:32, 2 * P:2 * P + CH - o], pw[m][:, lv + 2, 1, :],
                          he[:, lv % 2, 1:CH + 1 - o]), f"{n}.sh{lv}")
            wait("DVE", f"{n}.sh{lv}")
            V.tensor_copy(he[:, (lv + 1) % 2, 1:1 + o], he[:, lv % 2, 1:1 + o])
            done("DVE", tt(he[:, (lv + 1) % 2, 1 + o:CH + 1], he[:, lv % 2, 1 + o:CH + 1],
                           B[3][0:32, 2 * P:2 * P + CH - o], ALU.add), f"{n}.he{lv}")
            cur = f"{n}.he{lv}"
            yield
            wait("DVE", cur)
            lv += 1
        wait("PE", cur)
        mm(B[3][:, 3 * P:], blk[m][:], hx[:], stop=False)
        done("PE", mm(B[3][:, 3 * P:], car[m][:], he[:, lv % 2, 0:CH], start=False), f"{n}.h")
        wait("DVE", f"{n}.h")
        done("DVE", V.tensor_copy(hf[:], B[3][:, 3 * P:]), f"{n}.hf")
        yield
        wait("PE", f"{n}.hf", f"{n}.gs")
        for t in range(4):
            last = mm(B[t][:, 0:CH], cst[m][32 * t:32 * t + 32, :], hf[32 * t:32 * t + 32, :])
        done("PE", last, f"{n}.c")
        wait("DVE", f"{n}.c", f"{n}.u")
        for t in range(4):
            last = stt(t1[:].rearrange("p (c t) -> p t c", t=4)[:, t, :], B[t][:, 0:CH],
                       col(c + C_DV), uv[:, t, :], ALU.add, ALU.mult)
        done("DVE", last, f"{n}.cu")
        yield
        wait("DVE", f"{n}.cu", f"{n}.gs")
        done("DVE", tt(t1[:], t1[:], gs[:], ALU.mult), f"{n}.y")
        yield
        wait("PE", f"{n}.y")
        done("PE", mm(B[0][:], w_out[:], t1[:]), f"{n}.o")
        wait("DVE", f"{n}.o")
        done("DVE", stt(dst, B[0][:], col(c + C_OB), src, ALU.add, ALU.add), dst_name)
        yield

    def mixer3(w, b):
        B, t1, cpad = w["B"], w["t1"], w["cpad"]
        opad = w["pad"][:, 2:T + 4]
        yield from layer_norm(w, b, "n", keep=XNT)
        wait("PE", "n.xf")
        yield from mamba(w, 0, "ma", w["xf"][:], w["xres"][:], "ma.x")
        wait("DVE", "ma.x")
        wait("PE", "ma.x")
        yield from mamba(w, 1, "mb", w["xres"][:], cpad[:, 1:T + 1], "mb.x")
        wait("PE", "mb.x")
        for j in range(3):
            last = mm(B[1][0:64, :], M["c1"][:, 64 * j:64 * j + 64], cpad[:, j:j + T], start=(j == 0), stop=(j == 2))
        done("PE", mm(B[1][64:P, :], M["c4"][:], cpad[:, 1:T + 1]), "c14")
        wait("DVE", "c14")
        done("DVE", ts(t1[:], B[1][:], col(C_C1B), 0.0, ALU.add, ALU.max), "relu")
        yield
        wait("DVE", "relu")
        ts(opad[0:64, 1:T + 1], t1[0:64, :], BN_SCALE, None, ALU.mult)
        done("DVE", V.tensor_copy(opad[64:P, 1:T + 1], t1[64:P, :]), "oc")
        yield
        wait("PE", "oc")
        for j in range(3):
            last = mm(B[2][:], M["c5"][:, P * j:P * j + P], opad[:, j:j + T], start=(j == 0), stop=(j == 2))
        done("PE", last, "c5")
        wait("DVE", "c5")
        done("DVE", ts(t1[:], B[2][:], 0.0, BN_SCALE, ALU.max, ALU.mult), "o5")
        yield
        wait("DVE", "o5")
        done("DVE", tt(flat(ST[:, bass.ds(b, 1), :]), t1[:], cpad[:, 1:T + 1], ALU.add), "s")
        yield
        turn_over("s", "n.kept")

    w5 = working(ph4, "l5", ("sg", "sT", "gt", "ge0", "ge1", "vy0", "vy1", "vy2", "vy3"), 1)[0]
    w5["B"] = bank[4:8]
    one = sb("one", [1, P], c=ph4)
    sc = sb("sc", [1, 2, T], c=ph4)
    done("DVE", V.memset(one[:], 1.0), "one")
    for j in range(2):
        pr.dma(f"sc{j}")
    wait("PE", "one")
    wait("DVE", "w3", of="start")
    pr.dma("out")

    def scale(w):
        k = 0
        for wt, nm in zip(W3, ("l3_sv", "l3_s", "l3_s1")):
            for e in range(NE):
                if k >= 2:
                    wait("SP", f"scb{k - 2}")
                done(f"sc{k % 2}", S.dma_start(sc[:, k % 2, :], a[nm].rearrange("(o e) n -> o e n", o=1)[:, e, :]),
                     f"sc{k}", by=16)
                wait("PE", f"sc{k}")
                if k >= 2:
                    wait("PE", f"scm{k - 2}")
                done("PE", mm(w["B"][k % 2][:], one[:], sc[0:1, k % 2, :]), f"scb{k}")
                wait("DVE", f"scb{k}")
                done("DVE", tt(wt[:, e, :], wt[:, e, :], w["B"][k % 2][:], ALU.mult), f"scm{k}")
                k += 1
                yield
        turn_over(f"scm{k - 1}")

    WA3, WB3, WC3 = W3

    def mixture3(w, b):
        B, xf, ge = w["B"], w["xf"], (w["ge0"], w["ge1"])
        vy = [w[f"vy{m}"] for m in range(HC)]
        gt = tokens(w["gt"][:])
        done("ACT", A.copy(xf[:], flat(XNT[:, bass.ds(b, 1), :])), "xf")
        yield
        yield
        wait("PE", "xf")
        router = top_two(w, "r", "probs", lambda q: xf[:, q * P:(q + 1) * P], M["l3_rw"][:], dst=w["w8"][:], at=0)
        next(router)

        def gate(n):
            e, m = divmod(n, HC)
            if n >= 1:
                wait("PE", f"ge{n - 1}")
            done("PE", mm(B[2][:], WB3[:, e, m * P:(m + 1) * P], xf[:]), f"gate{n}")
            wait("ACT", f"gate{n}")
            if n >= 2:
                wait("ACT", f"vy{n - 2}")
            done("ACT", A.activation(ge[n % 2][:], B[2][:], ACT.Gelu_apprx_tanh), f"ge{n}")

        n = 0
        gate(0)
        for e in range(NE):
            for m in range(HC):
                if n >= 1:
                    wait("PE", f"vy{n - 1}")
                done("PE", mm(B[1][:], WA3[:, e, m * P:(m + 1) * P], xf[:]), f"up{n}")
                wait("DVE", f"ge{n}", f"up{n}")
                if e and m == 0:
                    wait("DVE", f"y{e - 1}")
                done("DVE", tt(vy[m][:], ge[n % 2][:], B[1][:], ALU.mult), f"vy{n}")
                n += 1
                if n < NE * HC:
                    gate(n)
                for _ in range(3):
                    next(router, None)
                yield
            wait("PE", f"vy{n - 1}")
            if e >= 1:
                wait("PE", f"a{e - 1}")
            for q in range(NQ):
                for m in range(HC):
                    last = mm(B[3][:, q * D:(q + 1) * D], vy[m][:, q * P:(q + 1) * P],
                              WC3[:, e, m * D:(m + 1) * D], start=(m == 0), stop=(m == HC - 1))
            done("PE", last, f"y{e}")
            wait("DVE", f"y{e}")
            if e:
                wait("DVE", f"a{e - 1}")
            else:
                wait("DVE", "r.w")
            for q in range(NQ):
                ys = B[3][:, q * D:(q + 1) * D]
                if e == 0:
                    last = ts(gt[:, q, :], ys, w["w8"][:, q, e:e + 1], None, ALU.mult)
                else:
                    last = stt(gt[:, q, :], ys, w["w8"][:, q, e:e + 1], gt[:, q, :], ALU.mult, ALU.add)
            done("DVE", last, f"a{e}")
            yield
        done("ACT", A.copy(w["sT"][:], flat(ST[:, bass.ds(b, 1), :])), "s")
        wait("PE", "s")
        yield from update(w, b, "u", w["sT"], w["gt"][:], (f"a{NE - 1}",))
        wait("SP", "u.x")
        done("out", S.dma_start(out[bass.ds(b, 1)].rearrange("a (q p) d -> p (a q) d", p=P), x_tiles(b)),
             "out", by=16)
        wait("PE", "u.sx")
        wait("DVE", "u.x")

    pr.enter("l3 first", 0, 1)
    pr.interleave(mixer3(w4, 0), scale(w5))
    pr.leave()
    pr.fence("l3 first")
    with nc.Fori(0, NB - 1) as i:
        pr.enter("l3", i, NB - 1)
        pr.interleave(mixer3(w4, i + 1), mixture3(w5, i), apart=0.06)
        pr.leave()
    pr.fence("l3")
    pr.enter("l3 last", 0, 1)
    pr.interleave((1, mixture3(w5, NB - 1)))
    pr.leave()
    wait("SP", "1:out", of="l3")
    wait("SP", "1:out", of="l3 last")
    ph4.close()
    ctx.close()
    return pr


_OUT_SHAPE = (NB, T, D)


def _rope():
    inv = (1.0 / np.float32(10000.0) ** (np.arange(0, D, 2, dtype=np.float32) / np.float32(D))).astype(np.float32)
    ang = (np.arange(T, dtype=np.float32)[:, None] * inv[None, :]).astype(np.float32)
    cos, sin = np.cos(ang).T, np.sin(ang).T
    c = np.repeat(cos, 2, axis=0)
    s = np.stack([-sin, sin], axis=1).reshape(D, T)
    ck, sk = np.concatenate([c[0:HD]] * NG), np.concatenate([s[0:HD]] * NG)
    return (np.concatenate([c, s], axis=1).astype(np.float32), np.concatenate([ck, sk], axis=1).astype(np.float32))


def _lay_out(i):
    t = np.ascontiguousarray
    swap = np.arange(D).reshape(-1, 2)[:, ::-1].reshape(-1)
    swk = np.arange(32).reshape(-1, 2)[:, ::-1].reshape(-1)
    z = np.zeros(P, np.float32)
    a = {"x": i["L0_attn_x"], "l0_wo": t(i["L0_attn_Wo"].T), "l0_bw": t(i["L0_attn_B_w"].T),
         "l0_rw": t(i["L0_ffn_router_w"].T)}
    cols = [i["L0_attn_A"], i["L0_attn_bo"], np.tile(i["L1_attn_A"], 4), i["L1_attn_D"], i["L1_ffn_bp1"],
            i["L1_ffn_bo"], np.concatenate([i["L3_attn_c1_b"], z[0:64]]), z]
    for m in ("m1", "m2"):
        g = lambda n: i[f"L3_attn_{m}_{n}"]
        cols += [g("in_b")[0:D], g("in_b")[D:], g("conv_b")] + [g("conv_w")[:, 0, k] for k in range(4)]
        cols += [np.tile(g("ssm_b"), 4), np.tile(g("B"), 4), g("D"), g("out_b"), np.tile(g("C"), 4)]
        a[f"{m}_in"], a[f"{m}_ssm"], a[f"{m}_out"] = g("in_w"), g("ssm_w"), g("out_w")
        a[f"{m}_A"] = np.concatenate([g("A"), g("A").T], axis=1)
    a["cv"] = np.stack(cols, axis=1)
    a["ident"] = np.eye(P, dtype=np.float32)
    a["iota"] = np.tile(np.arange(NE, dtype=np.float32), (P, NQ))
    den = np.zeros((P, P), np.float32)
    for r in range(4):
        den[32 * r + HD, 32 * r:32 * r + 32] = 1.0
    a["den"] = den
    a["l0_w1"] = i["L0_ffn_w1"].transpose(1, 0, 2)
    a["l0_w2"] = i["L0_ffn_w2"].reshape(NE, HC, P, D).transpose(2, 0, 1, 3).reshape(P, NE, T)
    a["l1_b"], a["l1_c"] = i["L1_attn_B"].T, i["L1_attn_C"].T
    a["l1_wp1"], a["l1_wp2"], a["l1_wo"] = i["L1_ffn_Wp1"], i["L1_ffn_Wp2"], i["L1_ffn_Wo"]
    a["l1_bp2"] = np.tile(i["L1_ffn_bp2"], (P, 1))
    b1 = i["L1_ffn_b1"].reshape(NE, 2, P).transpose(2, 1, 0)
    a["l1_bias"] = np.concatenate([b1, i["L1_ffn_b2"].T[:, None, :]], axis=1).reshape(P, 3 * NE)
    w2 = i["L1_ffn_W2"].reshape(NE, 2, P, D).transpose(2, 0, 1, 3).reshape(P, NE, 2 * D)
    a["l1_w"] = np.concatenate([i["L1_ffn_W1"].transpose(1, 0, 2), w2], axis=2)
    a["l2_q"] = np.concatenate([i["L2_attn_Wq"], i["L2_attn_Wq"][:, swap]], axis=1)
    a["l2_k"] = np.concatenate([i["L2_attn_Wk"], i["L2_attn_Wk"][:, swk]], axis=1)
    a["l2_v"], a["l2_wo"] = i["L2_attn_Wv"], i["L2_attn_Wo"]
    a["l2_gw"], a["l2_gb"] = i["L2_ffn_gate_w"].T, np.tile(i["L2_ffn_gate_b"], (P, NQ))
    a["l2_w"], a["l2_eb"] = i["L2_ffn_expert_w"].transpose(1, 0, 2).reshape(P, NE * D), i["L2_ffn_expert_b"]
    a["rope_q"], a["rope_k"] = _rope()
    selq, selk = np.zeros((P, NG, 2, P), np.float32), np.zeros((33, NG, 2, P), np.float32)
    for g in range(NG):
        for r in range(4):
            for d in range(HD):
                for p in range(3):
                    selq[32 * g + HD * r + d, g, int(p == 1), 32 * r + HD * p + d] = 1.0
                    selk[HD * g + d, g, int(p == 2), 32 * r + HD * p + d] = 1.0
            selk[32, g, 0, 32 * r + 24] = 1.0
    a["selq"], a["selk"] = selq.reshape(P, -1), selk.reshape(33, -1)
    a["c1"] = i["L3_attn_c1_w"].transpose(1, 2, 0).reshape(P, 3 * 64)
    a["c4"] = i["L3_attn_c4_w"][:, :, 0].T
    a["c5"] = i["L3_attn_c5_w"].transpose(1, 2, 0).reshape(P, 3 * P)
    a["l3_rw"] = i["L3_ffn_router_w"]
    a["l3_wv"], a["l3_w"] = i["L3_ffn_wv"].transpose(1, 0, 2), i["L3_ffn_w"].transpose(1, 0, 2)
    a["l3_w1"] = i["L3_ffn_w1"].reshape(NE, HC, P, D).transpose(2, 0, 1, 3).reshape(P, NE, T)
    a["l3_sv"], a["l3_s"] = i["L3_ffn_sv"][:, 0, :], i["L3_ffn_s"][:, 0, :]
    a["l3_s1"] = np.tile(i["L3_ffn_s1"][:, 0, :], (1, HC))
    return {n: t(v) for n, v in a.items()}


def kernel(**inputs):
    import concourse.bacc as bacc
    from concourse.bass_utils import run_bass_kernel_spmd

    arrays = _lay_out({n: np.asarray(v) for n, v in inputs.items()})
    known = None
    for _ in range(3):
        nc = bacc.Bacc("TRN2", target_bir_lowering=False, num_devices=1)
        aps = {n: nc.dram_tensor(f"in_{n}", v.shape, F32, kind="ExternalInput").ap() for n, v in arrays.items()}
        out = nc.dram_tensor("out", _OUT_SHAPE, F32, kind="ExternalOutput").ap()
        pr = build(nc, known, aps, out)
        known = (pr.names, pr.loops, pr.lengths)
    r = run_bass_kernel_spmd(nc, [{f"in_{n}": v for n, v in arrays.items()}], core_ids=[0])
    return r.results[0]["out"]
```
